# Optimizing a Trainium2 kernel written in Bass

```python
import numpy as np
import jax
import jax.numpy as jnp

def _softmax(x, axis=-1):
    return jax.nn.softmax(x, axis=axis)

def _gelu(x):
    return jax.nn.gelu(x, approximate=True)

def _silu(x):
    return jax.nn.silu(x)

def _sigmoid(x):
    return jax.nn.sigmoid(x)

def _layernorm(x, axis=-1, eps=1e-05):
    m = jnp.mean(x, axis=axis, keepdims=True)
    v = jnp.var(x, axis=axis, keepdims=True)
    return (x - m) / jnp.sqrt(v + eps)

def _scatter_add(tgt, idx, src, axis=0):
    return tgt.at[idx].add(src)

def _segment_sum(src, seg, n):
    return jax.ops.segment_sum(src, seg, n)
kernel_name = 'mk_adaln_ffn_d2_seqx_r4_37f380'

def setup_inputs(seed: int=0):
    np.random.seed(seed)
    _w = jnp.asarray

    def _rec_inputs():
        import jax
        import jax.numpy as jnp
        _rk = jax.random.key(seed)
        x = 4.136e-05 + 0.9999 * jax.random.normal(jax.random.fold_in(_rk, 1), (2, 1024, 256), jnp.float32)
        _lenS = 1024 - jax.random.randint(jax.random.fold_in(_rk, 7), (2,), 0, max(1, 1024 // 4) + 1, jnp.int32)
        _lenS2 = 1024 - jax.random.randint(jax.random.fold_in(_rk, 8), (2,), 0, max(1, 1024 // 4) + 1, jnp.int32)
        cond_1024 = -0.00608245 + 1.00131 * jax.random.normal(jax.random.fold_in(_rk, 11), (2, 256), jnp.float32)
        return (x, cond_1024)
    x, cond_1024 = _rec_inputs()

    def _L0_cond_setup():
        import jax, jax.numpy as jnp
        import numpy as np
        B, T, D_IN, V_IN, E = (64, 128, 256, 256, 256)
        key = jax.random.key(seed)
        ks = jax.random.split(key, 16)
        s = 0.01
        return {'video': jax.random.normal(ks[0], (B, V_IN), jnp.float32), 'seq': jax.random.normal(ks[1], (B, T, D_IN), jnp.float32), 'W_z': jax.random.normal(ks[2], (D_IN, E), jnp.float32) * s, 'U_z': jax.random.normal(ks[3], (E, E), jnp.float32) * s, 'C_z': jax.random.normal(ks[4], (V_IN, E), jnp.float32) * s, 'b_z': jnp.zeros((E,), jnp.float32), 'W_r': jax.random.normal(ks[5], (D_IN, E), jnp.float32) * s, 'U_r': jax.random.normal(ks[6], (E, E), jnp.float32) * s, 'C_r': jax.random.normal(ks[7], (V_IN, E), jnp.float32) * s, 'b_r': jnp.zeros((E,), jnp.float32), 'W': jax.random.normal(ks[8], (D_IN, E), jnp.float32) * s, 'U': jax.random.normal(ks[9], (E, E), jnp.float32) * s, 'C': jax.random.normal(ks[10], (V_IN, E), jnp.float32) * s, 'b': jnp.zeros((E,), jnp.float32)}
    _L0_cond_all = _L0_cond_setup()
    _L0_cond_in = {k: v for k, v in _L0_cond_all.items() if k in ('W_z', 'U_z', 'C_z', 'b_z', 'W_r', 'U_r', 'C_r', 'b_r', 'W', 'U', 'C', 'b')}
    del _L0_cond_all

    def _L0_ffn_setup():
        import jax, jax.numpy as jnp
        import numpy as np
        B, S, D, E, F = (2, 256, 256, 14, 512)
        key = jax.random.key(seed)
        k0, k1, k2, k3 = jax.random.split(key, 4)
        h = jax.random.normal(k0, (B, S, D), jnp.float32)
        gate_w = jax.random.normal(k1, (E, D), jnp.float32) * 0.02
        w1 = jax.random.normal(k2, (E, D, F), jnp.float32) * (1.0 / np.sqrt(D).astype(np.float32))
        b1 = jnp.zeros((E, F), jnp.float32)
        w2 = jax.random.normal(k3, (E, F, D), jnp.float32) * (1.0 / np.sqrt(F).astype(np.float32))
        b2 = jnp.zeros((E, D), jnp.float32)
        return {'h': h, 'gate_w': gate_w, 'w1': w1, 'b1': b1, 'w2': w2, 'b2': b2}
    _L0_ffn_all = _L0_ffn_setup()
    _L0_ffn_in = {k: v for k, v in _L0_ffn_all.items() if k in ('gate_w', 'w1', 'b1', 'w2', 'b2')}
    del _L0_ffn_all

    def _L1_cond_setup():
        import jax, jax.numpy as jnp
        import numpy as np
        import math
        IN_F = 256
        OUT_F = 256
        B = 16
        L = 1024
        key = jax.random.key(seed)
        k1, k2, k3 = jax.random.split(key, 3)
        Efou = jax.random.normal(k1, (B, L, IN_F), dtype=jnp.float32)
        y = jax.random.normal(k2, (B, IN_F), dtype=jnp.float32)
        weight = jax.random.normal(k3, (1, OUT_F, IN_F, 1), dtype=jnp.float32)
        return {'Efou': Efou, 'y': y, 'weight': weight}
    _L1_cond_all = _L1_cond_setup()
    _L1_cond_in = {k: v for k, v in _L1_cond_all.items() if k in ('weight',)}
    del _L1_cond_all

    def _L1_ffn_setup():
        import jax, jax.numpy as jnp
        import numpy as np
        HIDDEN = 256
        INNER = 1024

        def _weight_quant(w):
            scale = 1.0 / jnp.clip(jnp.mean(jnp.abs(w)), 1e-05)
            wq = jnp.clip(jnp.round(w * scale), -1.0, 1.0) / scale
            return w + jax.lax.stop_gradient(wq - w)

        def _act_quant(x):
            scale = 127.0 / jnp.clip(jnp.max(jnp.abs(x), axis=-1, keepdims=True), 1e-05)
            xq = jnp.clip(jnp.round(x * scale), -128.0, 127.0) / scale
            return x + jax.lax.stop_gradient(xq - x)

        def _bitlinear(x, w):
            return jnp.einsum('bsi,oi->bso', _act_quant(x), _weight_quant(w))
        key = jax.random.key(seed)
        k0, k1, k2, k3 = jax.random.split(key, 4)
        x = jax.random.normal(k0, (4, 512, HIDDEN), dtype=jnp.float32)
        w_gate = jax.random.normal(k1, (INNER, HIDDEN), dtype=jnp.float32) / np.sqrt(HIDDEN)
        w_up = jax.random.normal(k2, (INNER, HIDDEN), dtype=jnp.float32) / np.sqrt(HIDDEN)
        w_down = jax.random.normal(k3, (HIDDEN, INNER), dtype=jnp.float32) / np.sqrt(INNER)
        return {'x': x, 'w_gate': w_gate, 'w_up': w_up, 'w_down': w_down}
    _L1_ffn_all = _L1_ffn_setup()
    _L1_ffn_in = {k: v for k, v in _L1_ffn_all.items() if k in ('w_gate', 'w_up', 'w_down')}
    del _L1_ffn_all
    return {'x': x, 'cond_1024': cond_1024, 'L0_cond_W_z': _L0_cond_in['W_z'], 'L0_cond_U_z': _L0_cond_in['U_z'], 'L0_cond_C_z': _L0_cond_in['C_z'], 'L0_cond_b_z': _L0_cond_in['b_z'], 'L0_cond_W_r': _L0_cond_in['W_r'], 'L0_cond_U_r': _L0_cond_in['U_r'], 'L0_cond_C_r': _L0_cond_in['C_r'], 'L0_cond_b_r': _L0_cond_in['b_r'], 'L0_cond_W': _L0_cond_in['W'], 'L0_cond_U': _L0_cond_in['U'], 'L0_cond_C': _L0_cond_in['C'], 'L0_cond_b': _L0_cond_in['b'], 'L0_ffn_gate_w': _L0_ffn_in['gate_w'], 'L0_ffn_w1': _L0_ffn_in['w1'], 'L0_ffn_b1': _L0_ffn_in['b1'], 'L0_ffn_w2': _L0_ffn_in['w2'], 'L0_ffn_b2': _L0_ffn_in['b2'], 'L1_cond_weight': _L1_cond_in['weight'], 'L1_ffn_w_gate': _L1_ffn_in['w_gate'], 'L1_ffn_w_up': _L1_ffn_in['w_up'], 'L1_ffn_w_down': _L1_ffn_in['w_down']}

def reference(x, cond_1024, L0_cond_W_z, L0_cond_U_z, L0_cond_C_z, L0_cond_b_z, L0_cond_W_r, L0_cond_U_r, L0_cond_C_r, L0_cond_b_r, L0_cond_W, L0_cond_U, L0_cond_C, L0_cond_b, L0_ffn_gate_w, L0_ffn_w1, L0_ffn_b1, L0_ffn_w2, L0_ffn_b2, L1_cond_weight, L1_ffn_w_gate, L1_ffn_w_up, L1_ffn_w_down):
    import jax
    import jax.numpy as jnp

    def _L0_cond_ref(video, seq, W_z, U_z, C_z, b_z, W_r, U_r, C_r, b_r, W, U, C, b):
        import jax, jax.numpy as jnp
        import numpy as np
        B, T, D_IN, V_IN, E = (64, 128, 256, 256, 256)
        vz = video @ C_z + b_z
        vr = video @ C_r + b_r
        vh = video @ C + b
        xz = jnp.einsum('btd,de->bte', seq, W_z)
        xr = jnp.einsum('btd,de->bte', seq, W_r)
        xh = jnp.einsum('btd,de->bte', seq, W)

        def step(h, xs):
            xzt, xrt, xht = xs
            z = jax.nn.sigmoid(xzt + h @ U_z + vz)
            r = jax.nn.sigmoid(xrt + h @ U_r + vr)
            hh = jnp.tanh(xht + r * h @ U + vh)
            h_new = (1.0 - z) * h + z * hh
            return (h_new, h_new)
        h0 = jnp.zeros((seq.shape[0], U.shape[0]), seq.dtype)
        xs = (jnp.swapaxes(xz, 0, 1), jnp.swapaxes(xr, 0, 1), jnp.swapaxes(xh, 0, 1))
        _, out_t = jax.lax.scan(step, h0, xs)
        return jnp.swapaxes(out_t, 0, 1)

    def _L0_ffn_ref(h, gate_w, w1, b1, w2, b2):
        import jax, jax.numpy as jnp
        import numpy as np
        B, S, D, E, F = (2, 256, 256, 14, 512)
        Bb, Ss, Dd = h.shape
        x = h.reshape(Bb * Ss, Dd)
        logits = x @ gate_w.T
        probs = jax.nn.softmax(logits, axis=-1)
        top2_p, top2_i = jax.lax.top_k(probs, 2)
        w = top2_p / jnp.maximum(top2_p.sum(-1, keepdims=True), 1e-10)
        hh = jnp.einsum('nd,edf->nef', x, w1) + b1
        hh = jax.nn.gelu(hh, approximate=False)
        all_out = jnp.einsum('nef,efd->ned', hh, w2) + b2
        n = jnp.arange(x.shape[0])
        out0 = all_out[n, top2_i[:, 0]]
        out1 = all_out[n, top2_i[:, 1]]
        moe_out = w[:, 0:1] * out0 + w[:, 1:2] * out1
        result = jnp.clip(x + moe_out, -100.0, 100.0).reshape(Bb, Ss, Dd)
        return result

    def _L1_cond_ref(Efou, y, weight):
        import jax, jax.numpy as jnp
        import numpy as np
        import math
        IN_F = 256
        OUT_F = 256
        B = 16
        L = 1024
        b, img_size, in_f = Efou.shape
        out_f = weight.shape[1]
        scale = 1.0 / math.sqrt(in_f)
        w = scale * weight[:, :, :, 0] * y[:, None, :]
        dnorm = jax.lax.rsqrt(jnp.sum(w * w, axis=2, keepdims=True) + 1e-08)
        w = w * dnorm
        E = Efou.reshape(b, in_f, img_size)
        x = jnp.einsum('boi,bil->bol', w, E)
        return x.reshape(b, img_size, out_f)

    def _L1_ffn_ref(x, w_gate, w_up, w_down):
        import jax, jax.numpy as jnp
        import numpy as np
        HIDDEN = 256
        INNER = 1024

        def _weight_quant(w):
            scale = 1.0 / jnp.clip(jnp.mean(jnp.abs(w)), 1e-05)
            wq = jnp.clip(jnp.round(w * scale), -1.0, 1.0) / scale
            return w + jax.lax.stop_gradient(wq - w)

        def _act_quant(x):
            scale = 127.0 / jnp.clip(jnp.max(jnp.abs(x), axis=-1, keepdims=True), 1e-05)
            xq = jnp.clip(jnp.round(x * scale), -128.0, 127.0) / scale
            return x + jax.lax.stop_gradient(xq - x)

        def _bitlinear(x, w):
            return jnp.einsum('bsi,oi->bso', _act_quant(x), _weight_quant(w))
        gate = jax.nn.silu(_bitlinear(x, w_gate))
        up = _bitlinear(x, w_up)
        return _bitlinear(gate * up, w_down)
    x = x + _L0_ffn_ref(_L0_cond_ref(cond_1024, x, L0_cond_W_z, L0_cond_U_z, L0_cond_C_z, L0_cond_b_z, L0_cond_W_r, L0_cond_U_r, L0_cond_C_r, L0_cond_b_r, L0_cond_W, L0_cond_U, L0_cond_C, L0_cond_b), L0_ffn_gate_w, L0_ffn_w1, L0_ffn_b1, L0_ffn_w2, L0_ffn_b2)
    x = x + _L1_ffn_ref(_L1_cond_ref(x, cond_1024, L1_cond_weight), L1_ffn_w_gate, L1_ffn_w_up, L1_ffn_w_down)
    return x

_drawn_inputs = setup_inputs


def setup_inputs(seed=0):
    import zlib

    import numpy as np

    out = dict(_drawn_inputs(seed))
    spreads = {'L0_cond_b_z': (0.0, 0.401),
     'L0_cond_b_r': (0.0, 2.0),
     'L0_cond_b': (0.0, 0.1),
     'L0_ffn_b1': (0.0, 0.1),
     'L0_ffn_b2': (0.0, 0.1)}
    factors = {'L0_cond_U_z': 5.749, 'L0_cond_W_r': 22.122, 'L0_cond_U_r': 42.025, 'L0_cond_C_r': 20.617}
    for name, (base, spread) in spreads.items():
        noise = np.random.default_rng([zlib.crc32(name.encode()), seed]).standard_normal(out[name].shape)
        drawn = base * np.exp(spread * noise) if base else spread * noise
        out[name] = jnp.asarray(drawn.astype(out[name].dtype))
    for name, factor in factors.items():
        out[name] = (out[name] * factor).astype(out[name].dtype)
    return out
```

```python
from contextlib import ExitStack

import concourse.bass as bass
from concourse import mybir

P = 128
NB = 2
T = 1024
D = 256
KD = D // P
NE = 14
FF = 512
KF = FF // P
BS = 4
CS = P // NB
BPC = CS // BS
NCH = T // CS
INNER = 1024
KI = INNER // P
GC = KD * NB
R_, Z_, U_ = 0, 1, 2

H_SCALE = 2.0 ** 14
W_SCALE = 2.0 ** 6
PRE_SCALE = H_SCALE * W_SCALE
GATE_SCALE = (PRE_SCALE, PRE_SCALE, 2 * PRE_SCALE)
WARM_UP = 16
START = 1
ROUND = 1.5 * 2.0 ** 23

F32, F16, BF16 = mybir.dt.float32, mybir.dt.float16, mybir.dt.bfloat16
ALU, ACT, AX = mybir.AluOpType, mybir.ActivationFunctionType, mybir.AxisListType.X


def build(nc, x, cond, W_z, U_z, C_z, b_z, W_r, U_r, C_r, b_r, W, U, C, b,
          gate_w, w1, b1, w2, b2, mix_w, w_gate, w_up, w_down, out):
    ctx = ExitStack()
    with ctx:
        def sb(name, shape, dt=F32):
            return ctx.enter_context(nc.sbuf_tensor(name, shape, dt))

        def pb(name):
            return ctx.enter_context(nc.psum_tensor(name, [P, 512], F32))

        def sem(name):
            return ctx.enter_context(nc.semaphore(name))

        w1_sb = sb("w1_sb", [P, NE, KD, FF])
        w2_sb = sb("w2_sb", [P, NE, KF, D])
        b1_sb = sb("b1_sb", [P, NE, FF])
        b2_sb = sb("b2_sb", [P, D])
        gw_raw = sb("gw_raw", [NE, D])
        gwT = sb("gwT", [P, KD, NE])
        wx = sb("wx", [P, 3, KD, D])
        raw = sb("raw", [P, KD, D])
        split32 = sb("split32", [P, KD, D])
        uh = sb("uh", [P, 3, 2, KD, D], F16)
        condT = sb("condT", [P, KD, NB])
        bias_sb = sb("bias_sb", [P, 3, KD])
        vbias = sb("vbias", [P, 3, KD, NB])
        ident = sb("ident", [P, P])
        ident_bf = sb("ident_bf", [P, P], BF16)
        desc = sb("desc", [P, NE])
        desc_i = sb("desc_i", [P, NE], mybir.dt.int32)

        x_next = sb("x_next", [P, D])
        xT = sb("xT", [P, KD, P])
        xp_next = sb("xp_next", [P, 3, CS * GC])
        xp = sb("xp", [P, 3, CS * GC])
        xa = sb("xa", [P, 3, BS * GC])
        xb = sb("xb", [P, 3, BS * GC])
        xc = sb("xc", [P, 3, BS * GC])
        xi = sb("xi", [P, 3, 3, BS * GC], BF16)

        h32 = sb("h32", [P, BS, GC])
        h_hi = sb("h_hi", [P, GC], F16)
        h_lo = sb("h_lo", [P, GC], F16)
        rg = sb("rg", [P, GC])
        zg = sb("zg", [P, GC])
        zm1 = sb("zm1", [P, GC])
        zh = sb("zh", [P, GC])
        cand = sb("cand", [P, GC])
        rh32 = sb("rh32", [P, GC])
        rh_hi = sb("rh_hi", [P, GC], F16)
        rh_lo = sb("rh_lo", [P, GC], F16)
        negkeep = sb("negkeep", [P, GC])
        znew = sb("znew", [P, GC])

        h_chunk = sb("h_chunk", [P, CS, GC])
        hT = sb("hT", [P, KD, P])
        pre = sb("pre", [P, FF])
        hid = sb("hid", [P, FF])
        hidT = sb("hidT", [P, FF])
        acc = sb("acc", [P, D])
        x_res = sb("x_res", [P, D])
        x1_sb = sb("x1_sb", [P, D])

        lgT = sb("lgT", [NE, P])
        lg = sb("lg", [P, NE])
        dl = sb("dl", [P, NE])
        euler = sb("euler", [P, NE])
        warm = sb("warm", [P, NE])
        ex = sb("ex", [P, NE])
        pr = sb("pr", [P, NE])
        cd = sb("cd", [P, NE])
        sel1 = sb("sel1", [P, NE])
        pr2 = sb("pr2", [P, NE])
        sel = sb("sel", [P, NE])
        gate = sb("gate", [P, NE])
        gateT = sb("gateT", [P, P])
        st = sb("st", [P, 8])

        wgT = sb("wgT", [P, KD, INNER], BF16)
        wuT = sb("wuT", [P, KD, INNER], BF16)
        wdT = sb("wdT", [P, KI, D], BF16)
        mixT = sb("mixT", [P, KD, NB, D])
        ones = sb("ones", [P, P])
        wsum = sb("wsum", [P, 4])
        wscale = sb("wscale", [P, 4])
        msum = sb("msum", [P, NB * KD])
        mnorm = sb("mnorm", [P, NB * KD])
        mhalf = sb("mhalf", [P, NB * KD])
        hq = sb("hq", [P, INNER], BF16)
        hqT = sb("hqT", [P, INNER], BF16)
        NT = NB * T // P
        x_step = sb("x_step", [P, NT])
        x_inv = sb("x_inv", [P, NT])
        x_max = sb("x_max", [P, NT])
        g_step = sb("g_step", [P, NT])
        u_step = sb("u_step", [P, NT])
        h_st = sb("h_st", [P, 4])

        w1_flat = w1_sb[:].rearrange("p e k f -> p (e k f)")
        w2_flat = w2_sb[:].rearrange("p e k f -> p (e k f)")
        b1_flat = b1_sb[:].rearrange("p e f -> p (e f)")
        NW = 2048
        l1_raw = [w1_flat[:, i * NW:(i + 1) * NW] for i in range(3)]
        l1_tmp = [w2_flat[:, i * NW:(i + 1) * NW] for i in range(3)]
        l1_q = [w2_flat[:, (3 + i) * NW:(3 + i) * NW + NW // 2].bitcast(BF16) for i in range(3)]
        mix_raw = w1_flat[:, 3 * NW:3 * NW + KD * D].rearrange("p (k i) -> p k i", k=KD)
        cond_bc = w1_flat[:, 3 * NW + 512:3 * NW + 512 + NB * D].rearrange("p (b i) -> p b i", b=NB)
        mix_w4 = w1_flat[:, 4 * NW:4 * NW + 1024].rearrange("p (b k i) -> p b k i", b=NB, k=KD)
        mix_n4 = w1_flat[:, 4 * NW + 1024:5 * NW].rearrange("p (b k i) -> p b k i", b=NB, k=KD)
        sq_tmp = w1_flat[:, 5 * NW:5 * NW + D]
        x1_mix = b1_flat[:, 0:4096]
        mixed = w1_flat[:, 0:4096]
        out_sb = w1_flat[:, 4096:8192]
        xr = w2_flat[:, 0:512]
        q_all = w2_flat[:, 5120:7168].bitcast(BF16)
        qT_all = w2_flat[:, 7168:9216].bitcast(BF16)
        sg = w2_flat[:, 1024:2048]
        gs = w2_flat[:, 2048:3072]
        hh = w2_flat[:, 3072:4096]
        hr = w2_flat[:, 4096:5120]

        p_gate = [pb("p_r"), pb("p_z"), pb("p_u")]
        p_up = [pb("p_up0"), pb("p_up1")]
        p_tr = pb("p_tr")
        p_dn = pb("p_dn")
        p_misc = pb("p_misc")

        x1_dram = nc.dram_tensor("x1_scratch", (NB, T, D), F32).ap()

        s = {n: sem(n) for n in (
            "ld_small", "ld_u", "ld_w1", "ld_w2", "ld_b1", "ld_xnext", "ld_xres", "x1_stored",
            "const_made", "zeroed", "raw_free", "raw_scaled", "u_split", "p_prep", "e_prep", "vb_made",
            "h_hi_s", "h32_s", "h_lo_s", "r_pre", "z_pre", "u_pre", "r_s", "z_s", "cand_s",
            "rh_hi_s", "rh32_s", "rh_lo_s", "zm1_s", "keep_s", "znew_s",
            "xi_ready", "u_injected", "h_saved", "pool_chain", "pool_waits", "act_waits",
            "hT_made", "xT_made", "xT_copied", "proj_made", "proj_taken", "logits_made", "lgT_copied", "logits_turned",  "gate_made", "gateT_made", "gateT_copied", "base_made", "base_taken", "x1_made",
            "gchain", "gchain2", "clip_made", "xp_copied", "gwT_made", "act_prep",
            "up0_made", "up1_made", "pre0_made", "pre1_made", "hid0_made", "hid1_made",
            "tr_made", "hidT_made", "dn_made", "acc_made",
            "ld_l1", "ones_made", "abs_made", "wsum_made", "wscale_made", "wq1", "wq2", "wq3", "wT_made", "wT_copied",
            "mw_made", "msq_made", "mn_made", "mnorm_made", "mixn_made", "mixT_made", "mixT_copied",
            "ld_mix", "mix_made", "mix_copied",
            "x_chain", "xr_made", "q_made", "qT_made", "qT_copied", "steps_made", "gate_mm", "up_mm",
            "sig1_made", "gs_made", "hh_made", "h_chain", "h_inv_made", "h_step_made", "hr_made", "hq_made", "hqT_made",
            "hqT_copied", "down_mm", "out_made",
            "out_stored")}

        started = ("h_saved", "pre0_made", "pre1_made", "hidT_made", "acc_made", "base_taken", "tr_made", "dn_made",
                   "hid0_made", "hid1_made", "x1_stored", "x1_made", "base_made", "up0_made", "up1_made", "hqT_made",
                   "hqT_copied", "out_made", "down_mm")

        block = ctx.enter_context(nc.Block())
        NG = 14

        @block.sync
        def _(sp):
            xk = lambda a: a.rearrange("(k p) e -> p k e", p=P)

            def token_tile(dst, chunk, sem_):
                for bb in range(NB):
                    sp.dma_start(dst[bb * CS:(bb + 1) * CS, :], x[bb, bass.ds(chunk * CS, CS), :]).then_inc(s[sem_], 16)

            for name in started:
                sp.sem_inc(s[name], START)
            token_tile(x_next, 0, "ld_xnext")
            for g, w in enumerate((W_r, W_z, W)):
                sp.dma_start(wx[:, g], xk(w)).then_inc(s["ld_small"], 16)
            for g, v in enumerate((b_r, b_z, b)):
                sp.dma_start(bias_sb[:, g], v.rearrange("(k p) -> p k", p=P), allow_slow_non_contiguous=True).then_inc(s["ld_small"], 16)
            for k in range(KD):
                sp.dma_start(condT[:, k], cond[:, k * P:(k + 1) * P].rearrange("b p -> p b"),
                             allow_slow_non_contiguous=True).then_inc(s["ld_small"], 16)
            sp.dma_start(gw_raw[:], gate_w).then_inc(s["ld_small"], 16)
            sp.wait_ge(s["zeroed"], 2)
            sp.dma_start(b2_sb[0:NE, :], b2).then_inc(s["ld_small"], 16)
            for i, w in enumerate((C_r, C_z, C, U_r, U_z, U)):
                if i:
                    sp.wait_ge(s["raw_free"], i)
                sp.dma_start(raw[:], xk(w)).then_inc(s["ld_u"], 16)
            for i, w in enumerate((w_gate, w_up, w_down)):
                cols = w.shape[1]
                sp.dma_start(l1_raw[i].rearrange("p (k c) -> p k c", c=cols),
                             w.rearrange("(k p) c -> p k c", p=P)).then_inc(s["ld_l1"], 16)
            sp.dma_start(mix_raw, mix_w.rearrange("a (k p) i c -> p (a k) (i c)", p=P)).then_inc(s["ld_l1"], 16)
            for bb in range(NB):
                sp.dma_start(cond_bc[:, bb], cond[bb, :].partition_broadcast(P)).then_inc(s["ld_l1"], 16)
            sp.wait_ge(s["wT_copied"], 6)
            sp.wait_ge(s["mixT_copied"], KD)
            w1_v = w1.rearrange("e (k p) f -> p (e k) f", p=P)
            w2_v = w2.rearrange("e (k p) d -> p (e k) d", p=P)
            w1_t = w1_sb[:].rearrange("p e k f -> p (e k) f")
            w2_t = w2_sb[:].rearrange("p e k d -> p (e k) d")
            for i in range(0, NE * KD, 7):
                sp.dma_start(w1_t[:, i:i + 7], w1_v[:, i:i + 7]).then_inc(s["ld_w1"], 16)
            for i in range(0, NE * KF, 14):
                sp.dma_start(w2_t[:, i:i + 14], w2_v[:, i:i + 14]).then_inc(s["ld_w2"], 16)
            sp.dma_start(b1_sb[:].rearrange("p e f -> p (e f)"),
                         b1.rearrange("e f -> (e f)").partition_broadcast(P)).then_inc(s["ld_b1"], 16)

            sp.wait_ge(s["xT_made"], 1)
            token_tile(x_next, 1, "ld_xnext")

            def chunk(n, last):
                sp.wait_ge(s["xT_made"], n + 1)
                token_tile(x_next, 0 if last else n + 1, "ld_xnext")
                if not (isinstance(n, int) and n == 1):
                    sp.wait_ge(s["x1_made"], n - 1 + START)
                token_tile(x_res, n - 1, "ld_xres")
                store(n - 1)

            def store(m):
                sp.wait_ge(s["x1_made"], m + 1 + START)
                for bb in range(NB):
                    sp.dma_start(x1_dram[bb, bass.ds(m * CS, CS), :], x1_sb[bb * CS:(bb + 1) * CS, :]).then_inc(s["x1_stored"], 16)

            with sp.Fori(1, NCH - 1) as n:
                chunk(n, False)
            chunk(NCH - 1, True)
            sp.wait_ge(s["x1_made"], NCH - 1 + START)
            token_tile(x_res, NCH - 1, "ld_xres")
            store(NCH - 1)
            sp.wait_ge(s["x1_stored"], 32 * NCH + START)
            x1_v = x1_dram.rearrange("b (k p q) c -> (b k) p (q c)", p=P, q=4)
            out_v = out.rearrange("b (k p q) c -> (b k) p (q c)", p=P, q=4)
            for i in range(NB * KD):
                sp.dma_start(x1_mix[:, i * 1024:(i + 1) * 1024], x1_v[i]).then_inc(s["ld_mix"], 16)
            for i in range(NB * KD):
                sp.wait_ge(s["out_made"], 4 * (i + 1) + START)
                sp.dma_start(out_v[i], out_sb[:, i * 1024:(i + 1) * 1024]).then_inc(s["out_stored"], 16)
            sp.wait_ge(s["out_stored"], 16 * NB * KD)

        @block.gpsimd
        def _(pool):
            g = nc.gpsimd
            g.memset(b2_sb[:], 0.0).then_inc(s["zeroed"], 1)
            g.memset(gateT[:], 0.0).then_inc(s["zeroed"], 1)
            g.memset(ident[:], 0.0).then_inc(s["pool_chain"], 1)
            g.memset(ident_bf[:], 0.0).then_inc(s["pool_chain"], 1)
            g.iota(desc_i[:], pattern=[[-1, NE]], base=NE, channel_multiplier=0).then_inc(s["pool_chain"], 1)
            pool.wait_ge(s["pool_chain"], 3)
            for m in (ident, ident_bf):
                g.affine_select(out=m[:], in_=m[:], compare_op=ALU.not_equal, fill=1.0,
                                base=0, pattern=[[-1, P]], channel_multiplier=1).then_inc(s["const_made"], 1)
            g.tensor_copy(desc[:], desc_i[:]).then_inc(s["const_made"], 1)

            XI_OPS = 5

            def wait(name, value):
                pool.wait_ge(s[name], value)
                pool.sem_inc(s["pool_waits"], 1)

            def split_block(col, done):
                c0 = 3 + done * XI_OPS
                if not (isinstance(done, int) and done == 0):
                    wait("xi_ready", done)
                g.tensor_copy(xa[:], xp[:, :, bass.ds(col, BS * GC)]).then_inc(s["pool_chain"], 1)
                wait("pool_chain", c0 + 1)
                g.tensor_copy(xi[:, 0], xa[:]).then_inc(s["pool_chain"], 1)
                wait("pool_chain", c0 + 2)
                g.tensor_tensor(xb[:], xa[:], xi[:, 0], ALU.subtract).then_inc(s["pool_chain"], 1)
                wait("pool_chain", c0 + 3)
                g.tensor_copy(xi[:, 1], xb[:]).then_inc(s["pool_chain"], 1)
                wait("pool_chain", c0 + 4)
                g.tensor_tensor(xc[:], xb[:], xi[:, 1], ALU.subtract).then_inc(s["pool_chain"], 1)
                wait("pool_chain", c0 + 5)
                g.tensor_copy(xi[:, 2], xc[:]).then_inc(s["xi_ready"], 1)

            def take_projection(n):
                wait("proj_taken", 3 * n + 3)
                g.tensor_copy(xp[:], xp_next[:]).then_inc(s["xp_copied"], 1)
                wait("xp_copied", n + 1)

            def save_states(blk, col):
                wait("h32_s", blk * BS + BS)
                g.tensor_copy(h_chunk[:].rearrange("p t c -> p (t c)")[:, bass.ds(col, BS * GC)],
                              h32[:].rearrange("p t c -> p (t c)")).then_inc(s["h_saved"], 1)

            def make_hT(m):
                wait("h_saved", (m + 1) * BPC + START)
                if not (isinstance(m, int) and m == 0):
                    wait("base_made", m + START)
                    wait("up1_made", m * NE + START)
                g.tensor_scalar(hT[:].rearrange("p k (b t) -> p k b t", b=NB),
                                h_chunk[:].rearrange("p t (k b) -> p k b t", k=KD),
                                1.0 / H_SCALE, None, ALU.mult).then_inc(s["hT_made"], 1)
                wait("hT_made", m + 1)

            g.memset(ones[:], 1.0).then_inc(s["ones_made"], 1)
            g.memset(mhalf[:], -0.5).then_inc(s["ones_made"], 1)
            take_projection(0)
            split_block(0, 0)
            pool.wait_ge(s["mn_made"], 1)
            g.tensor_tensor(mnorm[:], msum[:], mhalf[:], ALU.pow).then_inc(s["mnorm_made"], 1)

            def exponentials(m):
                pool.wait_ge(s["gchain"], m * NG + 3)
                g.tensor_tensor(ex[:], euler[:], dl[:], ALU.pow).then_inc(s["gchain"], 1)

            def chunk(n, m=None):
                def one(k):
                    wait("u_injected", n * BPC + k + 1)
                    split_block((k + 1) * BS * GC, n * BPC + k + 1)
                    if m is not None and isinstance(k, int):
                        exponentials(m)
                    save_states(n * BPC + k, k * BS * GC)
                one(0)
                with pool.Fori(1, BPC - 1) as k:
                    one(k)
                wait("u_injected", n * BPC + BPC)
                take_projection(n + 1)
                split_block(0, n * BPC + BPC)
                save_states(n * BPC + BPC - 1, (BPC - 1) * BS * GC)

            chunk(0)
            with pool.Fori(1, NCH) as n:
                make_hT(n - 1)
                chunk(n, n - 1)
            make_hT(NCH - 1)
            exponentials(NCH - 1)

            with pool.Fori(0, NT) as t:
                wait("h_inv_made", t + 1)
                g.tensor_scalar(hr, hh, h_st[:, 2:3], ROUND, ALU.mult, ALU.add).then_inc(s["hr_made"], 1)
                wait("hr_made", t + 1)
                wait("hqT_made", t + START)
                g.tensor_scalar(hq[:], hr, ROUND, 127.0, ALU.subtract, ALU.min).then_inc(s["hq_made"], 1)

        @block.tensor
        def _(pe):
            mm = nc.tensor.matmul

            def products(gt, part, src, j, name=None, pieces=range(4)):
                for i in pieces:
                    m, k = i // KD, i % KD
                    c = j * GC + m * NB
                    last = mm(p_gate[gt][:, c:c + NB], uh[:, gt, part, k, m * P:(m + 1) * P],
                              src[:, k * NB:(k + 1) * NB], start=False, stop=True, skip_group_check=True)
                if name:
                    last.then_inc(s[name], 1)

            def inject(gt):
                for part in range(3):
                    last = mm(p_gate[gt][:, 0:BS * GC], ident_bf[:], xi[:, part, gt], start=(part == 0), stop=True,
                              skip_group_check=True)
                return last

            def four_steps(blk, after_z, after_u):
                v = [pe.snap(blk * BS + j) if not isinstance(blk, int) else blk * BS + j for j in range(BS + 1)]
                for j in range(BS):
                    pe.wait_ge(s["h_hi_s"], v[j] + 1)
                    products(R_, 0, h_hi, j)
                    products(R_, 1, h_hi, j)
                    products(Z_, 0, h_hi, j, pieces=(0, 1))
                    pe.wait_ge(s["h_lo_s"], v[j] + 1)
                    products(R_, 0, h_lo, j, "r_pre")
                    if j == 0:
                        inject(U_).then_inc(s["u_injected"], 1)
                    products(Z_, 0, h_hi, j, pieces=(2, 3))
                    products(Z_, 1, h_hi, j)
                    products(Z_, 0, h_lo, j, "z_pre")
                    after_z(j)
                    pe.wait_ge(s["rh_hi_s"], v[j + 1])
                    products(U_, 0, rh_hi, j)
                    products(U_, 1, rh_hi, j)
                    pe.wait_ge(s["rh_lo_s"], v[j + 1])
                    products(U_, 0, rh_lo, j, "u_pre")
                    if j == BS - 1:
                        pe.wait_ge(s["z_s"], v[j + 1])
                        pe.wait_ge(s["xi_ready"], blk + 2)
                        inject(R_)
                        inject(Z_)
                    after_u(j)

            def nothing(j):
                pass

            def up(e, cnt, pieces):
                for i in pieces:
                    c, k = i // KD, i % KD
                    if i == 0:
                        pe.wait_ge(s["pre0_made"], cnt + START)
                    if i == 4:
                        pe.wait_ge(s["pre1_made"], cnt + START)
                    last = mm(p_up[c // 2][:, c % 2 * P:(c % 2 + 1) * P], hT[:, k],
                              w1_sb[:, bass.ds(e, 1), k, c * P:(c + 1) * P].rearrange("p a f -> p (a f)")
                              if not isinstance(e, int) else w1_sb[:, e, k, c * P:(c + 1) * P],
                              start=(k == 0), stop=(k == KD - 1), skip_group_check=True)
                    if i == 3:
                        last.then_inc(s["up0_made"], 1)
                    if i == 7:
                        last.then_inc(s["up1_made"], 1)

            def turn(cnt, quarters):
                for c in quarters:
                    if c == 0:
                        pe.wait_ge(s["hid0_made"], cnt + 1 + START)
                        pe.wait_ge(s["hidT_made"], cnt + START)
                    if c == 2:
                        pe.wait_ge(s["hid1_made"], cnt + 1 + START)
                    last = nc.tensor.transpose(p_tr[:, c * P:(c + 1) * P], hid[:, c * P:(c + 1) * P], ident[:])
                    if c == 3:
                        last.then_inc(s["tr_made"], 1)

            def down(e, cnt, pieces, m):
                for i in pieces:
                    f, half = i // 2, i % 2
                    if i == 0:
                        pe.wait_ge(s["hidT_made"], cnt + 1 + START)
                        pe.wait_ge(s["acc_made"], cnt + START)
                        pe.wait_ge(s["base_taken"], m + 1 + START)
                    last = mm(p_dn[:, half * P:(half + 1) * P], hidT[:, f * P:(f + 1) * P],
                              w2_sb[:, bass.ds(e, 1), f, half * P:(half + 1) * P].rearrange("p a f -> p (a f)")
                              if not isinstance(e, int) else w2_sb[:, e, f, half * P:(half + 1) * P],
                              start=(i == 0), stop=(f == KF - 1), skip_group_check=True)
                    if i == 7:
                        last.then_inc(s["dn_made"], 1)

            def turn_x(n):
                pe.wait_ge(s["ld_xnext"], 32 * (n + 1))
                if not (isinstance(n, int) and n < 2):
                    pe.wait_ge(s["base_taken"], n - 2 + START)
                elif n == 1:
                    pe.wait_ge(s["proj_taken"], 3)
                for k in range(KD):
                    last = nc.tensor.transpose(p_misc[:, k * P:(k + 1) * P], x_next[:, k * P:(k + 1) * P], ident[:])
                last.then_inc(s["xT_made"], 1)

            def project(n, pieces, n_experts=None):
                banks = (p_tr, p_dn, p_misc)
                for i in pieces:
                    gt, m, k = i // 4, i // 2 % 2, i % 2
                    if i == 0:
                        pe.wait_ge(s["xT_copied"], n + 1)
                        if n_experts is not None:
                            pe.wait_ge(s["acc_made"], n_experts + START)
                    last = mm(banks[gt][:, m * P:(m + 1) * P], wx[:, gt, k, m * P:(m + 1) * P], xT[:, k],
                              start=(k == 0), stop=(k == KD - 1), skip_group_check=True)
                    if i % 4 == 3:
                        last.then_inc(s["proj_made"], 1)

            def logits(m):
                pe.wait_ge(s["hT_made"], m + 1)
                pe.wait_ge(s["pre0_made"], m * NE + START)
                for k in range(KD):
                    last = mm(p_up[0][0:NE, 0:P], gwT[:, k], hT[:, k], start=(k == 0), stop=(k == KD - 1))
                last.then_inc(s["logits_made"], 1)

            def turn_logits(m):
                nc.tensor.transpose(p_up[1][:, 0:NE], lgT[:, :], ident[0:NE, 0:NE]).then_inc(s["logits_turned"], 1)

            def keep_warm(bank, n, cols=512):
                for _ in range(n):
                    mm(bank[:, 0:cols], ident_bf[:], wgT[:, 0, 0:cols], start=True, stop=True, skip_group_check=True)

            def turn_gate(m):
                pe.wait_ge(s["gate_made"], m + 1)
                mm(p_tr[0:NE, 0:P], gate[:, :], ident[:], start=True, stop=True, is_transpose=True).then_inc(s["gateT_made"], 1)

            def base(m, parts):
                for i in parts:
                    if i < KD:
                        mm(p_misc[:, i * P:(i + 1) * P], hT[:, i], ident[:], start=(i == 0), stop=False,
                           skip_group_check=True)
                    else:
                        pe.wait_ge(s["gateT_copied"], m + 1)
                        mm(p_misc[:, 0:D], gateT[:, :], b2_sb[:, :], start=False, stop=True,
                           skip_group_check=True).then_inc(s["base_made"], 1)

            pe.wait_ge(s["const_made"], 3)
            pe.wait_ge(s["ld_small"], 16 * 10)
            for k in range(KD):
                last = nc.tensor.transpose(p_up[0][:, k * 16:k * 16 + NE], gw_raw[:, k * P:(k + 1) * P], ident[0:NE, 0:NE])
            last.then_inc(s["p_prep"], 1)
            turn_x(0)
            for gt in range(3):
                pe.wait_ge(s["ld_u"], 16 * (gt + 1))
                for m in range(KD):
                    for k in range(KD):
                        last = mm(p_up[1][:, gt * GC + m * NB:gt * GC + (m + 1) * NB], raw[:, k, m * P:(m + 1) * P],
                                  condT[:, k], start=(k == 0), stop=(k == KD - 1), skip_group_check=True)
                last.then_inc(s["raw_free"], 1)
            project(0, range(12))

            pe.wait_ge(s["ones_made"], 2)
            pe.wait_ge(s["abs_made"], 3)
            mm(p_gate[0][:, 0:3], ones[:], wsum[:, 0:3], start=True, stop=True).then_inc(s["wsum_made"], 1)
            banks = (p_gate[1], p_gate[2])
            for n in range(6):
                i, half = n // 2, n % 2
                pe.wait_ge(s["wq3"], i + 1)
                if n > 1:
                    pe.wait_ge(s["wT_copied"], n - 1)
                dst = banks[n % 2][:].bitcast(BF16)
                for o in range(8):
                    if i < 2:
                        src = l1_q[i].rearrange("p (o c) -> p o c", o=8)[:, o, half * P:(half + 1) * P]
                    else:
                        src = l1_q[i].rearrange("p (o c) -> p o c", o=KD)[:, o % KD, (half * 4 + o // KD) * P:(half * 4 + o // KD + 1) * P]
                    last = nc.tensor.transpose(dst[:, o * P:(o + 1) * P], src, ident_bf[:])
                last.then_inc(s["wT_made"], 1)
            pe.wait_ge(s["mixn_made"], 4)
            pe.wait_ge(s["wT_copied"], 6)
            for k in range(KD):
                for bb in range(NB):
                    for o in range(KD):
                        c = (bb * KD + o) * P
                        last = nc.tensor.transpose(banks[k][:, c:c + P], mix_n4[:, bb, o, k * P:(k + 1) * P], ident[:])
                last.then_inc(s["mixT_made"], 1)
            pe.wait_ge(s["mixT_copied"], KD)
            pe.wait_ge(s["wscale_made"], 2)
            pe.wait_ge(s["u_split"], 3)
            pe.wait_ge(s["xi_ready"], 1)
            inject(R_)
            inject(Z_)

            pe.wait_ge(s["gwT_made"], KD)
            with pe.Fori(0, BPC - 2) as k:
                four_steps(k, nothing, nothing)

            def fill_x(n):
                def after_u(j):
                    if j == 0:
                        turn_x(n)
                    else:
                        project(n, range(4 * (j - 1), 4 * j))
                return after_u

            four_steps(BPC - 2, nothing, fill_x(1))
            four_steps(BPC - 1, nothing, nothing)
            pe.wait_ge(s["ld_w1"], 16 * 4)
            pe.wait_ge(s["ld_w2"], 16 * 4)
            keep_warm(p_up[1], WARM_UP)

            def expert_slots(x0, c0, m, warm=True):
                def after_z(j):
                    if j == 0:
                        up(x0, c0, (0,))
                        if warm:
                            pe.wait_ge(s["base_taken"], m + 1 + START)
                    elif j == 1:
                        up(x0, c0, (4,))
                    elif j == 2:
                        down(x0 - 1, c0 - 1, (0,), m)
                    else:
                        down(x0 - 1, c0 - 1, (4,), m)
                    if warm:
                        keep_warm(p_misc, 1, 256)

                def after_u(j):
                    if j == 0:
                        turn(c0 - 1, (0, 1, 2, 3))
                        up(x0, c0, (1, 2, 3))
                    elif j == 1:
                        up(x0, c0, (5, 6, 7))
                    elif j == 2:
                        down(x0 - 1, c0 - 1, (1, 2, 3), m)
                    else:
                        down(x0 - 1, c0 - 1, (5, 6, 7), m)
                return after_z, after_u

            def gating_slots(m, project_too):
                def after_z(j):
                    if j == 0:
                        pe.wait_ge(s["pre1_made"], m * NE + START)
                        if project_too:
                            keep_warm(p_up[1], 1)
                    elif j == 1:
                        pe.wait_ge(s["lgT_copied"], m + 1)
                        if project_too:
                            keep_warm(p_up[0], 1, 256)
                        turn_logits(m)
                        if project_too:
                            project(m + 2, (0,), m * NE)
                    elif project_too:
                        project(m + 2, (4 * (j - 1),))
                    if project_too and j != 1:
                        keep_warm(p_up[0] if j else p_up[1], 1, 256)

                def after_u(j):
                    if j == 0:
                        if project_too:
                            turn_x(m + 2)
                        logits(m)
                        if project_too:
                            keep_warm(p_up[1], 1)
                    elif project_too:
                        project(m + 2, range(4 * j - 3, 4 * j))
                return after_z, after_u

            def first_slots(m, c0, warm=True):
                def after_z(j):
                    if j == 0:
                        up(0, c0, (0,))
                    elif j == 1:
                        pe.wait_ge(s["gchain"], m * NG + 1)
                        up(0, c0, (4,))
                    elif j == 2:
                        pe.wait_ge(s["proj_taken"], base_waits(m))
                        base(m, (0,))
                    else:
                        turn_gate(m)
                        if warm:
                            keep_warm(p_dn, 1)
                    if warm:
                        if j == 0:
                            pe.wait_ge(s["proj_taken"], base_waits(m))
                        keep_warm(p_dn, 1, 256)

                def after_u(j):
                    if j == 0:
                        up(0, c0, (1, 2, 3))
                    elif j == 1:
                        up(0, c0, (5, 6, 7))
                    elif j == 2:
                        base(m, (1,))
                        if warm:
                            keep_warm(p_dn, 2)
                    else:
                        base(m, (2,))
                        if warm:
                            keep_warm(p_dn, 2)
                return after_z, after_u

            def base_waits(m):
                return 3 * (m + 3) if not (isinstance(m, int) and m == NCH - 1) else 3 * (NCH + 1)

            def last_slots(m, cnt, warm=True):
                def after_z(j):
                    if j == 0:
                        turn(cnt, (0, 1))
                        pe.wait_ge(s["pre1_made"], cnt + 1 + START)
                        if warm:
                            keep_warm(p_up[1], 1)
                    elif j == 1:
                        down(NE - 1, cnt, (0,), m)
                    elif j == 2:
                        down(NE - 1, cnt, (4,), m)
                    elif warm:
                        keep_warm(p_up[1], 1)
                    if warm:
                        keep_warm(p_up[1], 1, 256)

                def after_u(j):
                    if j == 0:
                        turn(cnt, (2, 3))
                    elif j == 1:
                        down(NE - 1, cnt, (1, 2, 3), m)
                    elif j == 2:
                        down(NE - 1, cnt, (5, 6, 7), m)
                    if j in (0, 3) and warm:
                        keep_warm(p_up[1], 3)
                return after_z, after_u

            def alone(slots):
                for j in range(BS):
                    slots[0](j)
                    slots[1](j)

            with pe.Fori(1, NCH) as n:
                m = pe.snap(n - 1)
                four_steps(n * BPC, *gating_slots(m, True))
                four_steps(n * BPC + 1, *first_slots(m, m * NE))
                with pe.Fori(1, NE) as e:
                    four_steps(n * BPC + 1 + e, *expert_slots(e, pe.snap(m * NE + e), m))
                four_steps(n * BPC + BPC - 1, *last_slots(m, m * NE + NE - 1))

            m = NCH - 1
            alone(gating_slots(m, False))
            alone(first_slots(m, m * NE, False))
            with pe.Fori(1, NE) as e:
                alone(expert_slots(e, pe.snap(m * NE + e), m, False))
            alone(last_slots(m, m * NE + NE - 1, False))

            pe.wait_ge(s["ld_mix"], 16 * NB * KD)
            mix_banks = (p_up[0], p_up[1])

            def turn_q(n):
                pe.wait_ge(s["q_made"], n + 1)
                if n:
                    pe.wait_ge(s["qT_copied"], n)
                for i in range(4):
                    last = nc.tensor.transpose(p_gate[0][:].bitcast(BF16)[:, i * P:(i + 1) * P],
                                               q_all[:, n * 512 + i * P:n * 512 + (i + 1) * P], ident_bf[:])
                last.then_inc(s["qT_made"], 1)

            for n in range(NB * KD * 2):
                bb, o, half = n // 4, n // 2 % 2, n % 2
                if n > 1:
                    pe.wait_ge(s["mix_copied"], n - 1)
                for k in range(KD):
                    c = (bb * KD + k) * 1024 + half * 512
                    last = mm(mix_banks[n % 2][:], mixT[:, k, bb, o * P:(o + 1) * P], x1_mix[:, c:c + 512],
                              start=(k == 0), stop=(k == KD - 1))
                last.then_inc(s["mix_made"], 1)
                if n > 1:
                    turn_q(n - 2)
            turn_q(NB * KD * 2 - 2)
            turn_q(NB * KD * 2 - 1)

            def gate_and_up(t):
                for banks_, w, read, made in ((p_up, wgT, "gs_made", "gate_mm"), ((p_misc, p_tr), wuT, "hh_made", "up_mm")):
                    pe.wait_ge(s[read], 2 * t)
                    for half in range(2):
                        for k in range(KD):
                            last = mm(banks_[half][:], qT_all[:, bass.ds(t * D + k * P, P)],
                                      w[:, k, half * 512:(half + 1) * 512], start=(k == 0), stop=(k == KD - 1))
                        last.then_inc(s[made], 1)

            def turn_h(t):
                pe.wait_ge(s["hq_made"], t + 1)
                pe.wait_ge(s["hqT_copied"], t + START)
                for k in range(KI):
                    last = nc.tensor.transpose(p_gate[1][:].bitcast(BF16)[:, k * P:(k + 1) * P], hq[:, k * P:(k + 1) * P],
                                               ident_bf[:])
                last.then_inc(s["hqT_made"], 1)

            def down_l1(t):
                pe.wait_ge(s["hqT_copied"], t + 1 + START)
                pe.wait_ge(s["out_made"], t + START)
                for k in range(KI):
                    last = mm(p_gate[2][:, 0:D], hqT[:, k * P:(k + 1) * P], wdT[:, k], start=(k == 0), stop=(k == KI - 1))
                last.then_inc(s["down_mm"], 1)

            pe.wait_ge(s["mix_copied"], 2 * NB * KD)
            pe.wait_ge(s["qT_copied"], 2 * NB * KD)
            gate_and_up(0)
            with pe.Fori(1, NT) as t:
                gate_and_up(t)
                turn_h(t - 1)
                down_l1(t - 1)
            turn_h(NT - 1)
            down_l1(NT - 1)

        @block.scalar
        def _(act):
            A = nc.scalar.activation

            def four_steps(blk, before_cand, after_cand):
                v = [act.snap(blk * BS + j + 1) if not isinstance(blk, int) else blk * BS + j + 1 for j in range(BS)]
                for j in range(BS):
                    cols = slice(j * GC, (j + 1) * GC)
                    act.wait_ge(s["r_pre"], v[j])
                    A(rg[:], p_gate[R_][:, cols], ACT.Tanh, scale=0.5 / PRE_SCALE).then_inc(s["r_s"], 1)
                    act.wait_ge(s["z_pre"], v[j])
                    A(zg[:], p_gate[Z_][:, cols], ACT.Tanh, scale=0.5 / PRE_SCALE).then_inc(s["z_s"], 1)
                    before_cand(j)
                    act.wait_ge(s["u_pre"], v[j])
                    A(cand[:], p_gate[U_][:, cols], ACT.Tanh, scale=0.5 / PRE_SCALE).then_inc(s["cand_s"], 1)
                    after_cand(j)

            def nothing(j):
                pass

            def gelu_half(half, cnt):
                act.wait_ge(s[f"pre{half}_made"], cnt + 1 + START)
                act.wait_ge(s["tr_made"], cnt + START)
                c = slice(half * 256, half * 256 + 256)
                A(hid[:, c], pre[:, c], ACT.Gelu).then_inc(s[f"hid{half}_made"], 1)

            def copy_hidT(cnt):
                act.wait_ge(s["tr_made"], cnt + 1 + START)
                act.wait_ge(s["dn_made"], cnt + START)
                A(hidT[:], p_tr[:], ACT.Copy).then_inc(s["hidT_made"], 1)

            def copy_xT(n):
                act.wait_ge(s["xT_made"], n + 1)
                act.wait_ge(s["proj_made"], 3 * n)
                A(xT[:].rearrange("p k t -> p (k t)"), p_misc[:, 0:D], ACT.Copy).then_inc(s["xT_copied"], 1)

            def copy_gateT(m):
                act.wait_ge(s["gateT_made"], m + 1)
                A(gateT[0:NE, :], p_tr[0:NE, 0:P], ACT.Copy).then_inc(s["gateT_copied"], 1)

            act.wait_ge(s["const_made"], 3)
            A(warm[:], desc[:], ACT.Gelu).then_inc(s["act_prep"], 1)
            act.wait_ge(s["p_prep"], 1)
            for k in range(KD):
                A(gwT[:, k], p_up[0][:, k * 16:k * 16 + NE], ACT.Copy).then_inc(s["gwT_made"], 1)
            copy_xT(0)

            for i in range(3):
                act.wait_ge(s["ld_l1"], 16 * 6)
                A(l1_tmp[i], l1_raw[i], ACT.Abs, accum_out=wsum[:, i:i + 1]).then_inc(s["abs_made"], 1)
            for n in range(NB * KD):
                act.wait_ge(s["mw_made"], n + 1)
                if n:
                    act.wait_ge(s["msq_made"], n)
                A(sq_tmp, mix_w4[:, n // KD, n % KD], ACT.Square, accum_out=msum[:, n:n + 1]).then_inc(s["msq_made"], 1)
            banks = (p_gate[1], p_gate[2])
            for n in range(6):
                i, half = n // 2, n % 2
                dst = (wgT[:, half], wuT[:, half], wdT[:, half * 4:half * 4 + 4].rearrange("p k d -> p (k d)"))[i]
                act.wait_ge(s["wT_made"], n + 1)
                A(dst, banks[n % 2][:].bitcast(BF16), ACT.Copy).then_inc(s["wT_copied"], 1)
            for k in range(KD):
                act.wait_ge(s["mixT_made"], k + 1)
                A(mixT[:, k].rearrange("p b o -> p (b o)"), banks[k][:], ACT.Copy).then_inc(s["mixT_copied"], 1)

            with act.Fori(0, BPC - 2) as k:
                four_steps(k, nothing, nothing)
            four_steps(BPC - 2, nothing, lambda j: copy_xT(1) if j == 0 else None)
            four_steps(BPC - 1, nothing, nothing)

            def gating_slots(m, project_too):
                def after(j):
                    if j == 0 and project_too:
                        copy_xT(m + 2)
                return nothing, after

            def first_slots(m, c0):
                def after(j):
                    if j == 1:
                        gelu_half(0, c0)
                    elif j == 2:
                        gelu_half(1, c0)

                def before(j):
                    if j == 3:
                        copy_gateT(m)
                return before, after

            def expert_slots(c0):
                def after(j):
                    if j == 0:
                        copy_hidT(c0 - 1)
                    elif j == 1:
                        gelu_half(0, c0)
                    elif j == 2:
                        gelu_half(1, c0)
                return nothing, after

            def last_slots(cnt):
                def after(j):
                    if j == 0:
                        copy_hidT(cnt)
                return nothing, after

            def alone(slots):
                for j in range(BS):
                    slots[0](j)
                    slots[1](j)

            with act.Fori(1, NCH) as n:
                m = act.snap(n - 1)
                four_steps(n * BPC, *gating_slots(m, True))
                four_steps(n * BPC + 1, *first_slots(m, m * NE))
                with act.Fori(1, NE) as e:
                    four_steps(n * BPC + 1 + e, *expert_slots(act.snap(m * NE + e)))
                four_steps(n * BPC + BPC - 1, *last_slots(m * NE + NE - 1))
            m = NCH - 1
            alone(gating_slots(m, False))
            alone(first_slots(m, m * NE))
            with act.Fori(1, NE) as e:
                alone(expert_slots(act.snap(m * NE + e)))
            alone(last_slots(m * NE + NE - 1))

            mix_banks = (p_up[0], p_up[1])

            def copy_qT(n):
                act.wait_ge(s["qT_made"], n + 1)
                A(qT_all[:, n * 512:(n + 1) * 512], p_gate[0][:].bitcast(BF16)[:, 0:512], ACT.Copy).then_inc(s["qT_copied"], 1)

            for n in range(NB * KD * 2):
                act.wait_ge(s["mix_made"], n + 1)
                A(mixed[:, n * 512:(n + 1) * 512], mix_banks[n % 2][:], ACT.Copy).then_inc(s["mix_copied"], 1)
                if n > 1:
                    copy_qT(n - 2)
            copy_qT(NB * KD * 2 - 2)
            copy_qT(NB * KD * 2 - 1)

            def sigmoids(t):
                act.wait_ge(s["gs_made"], 2 * t)
                for half in range(2):
                    act.wait_ge(s["gate_mm"], 2 * t + half + 1)
                    act.sem_inc(s["act_waits"], 1)
                    A(sg[:, half * 512:(half + 1) * 512], p_up[half][:], ACT.Sigmoid,
                      scale=g_step[:, bass.ds(t, 1)]).then_inc(s["sig1_made"], 1)

            def copy_hqT(t):
                act.wait_ge(s["hqT_made"], t + 1 + START)
                act.wait_ge(s["down_mm"], t + START)
                A(hqT[:], p_gate[1][:].bitcast(BF16), ACT.Copy).then_inc(s["hqT_copied"], 1)

            act.wait_ge(s["steps_made"], 2)
            sigmoids(0)
            with act.Fori(1, NT) as t:
                sigmoids(t)
                copy_hqT(t - 1)
            copy_hqT(NT - 1)

        @block.vector
        def _(dve):
            V = nc.vector

            def four_steps(blk, after_keep, after_h):
                v = [dve.snap(blk * BS + j + 1) if not isinstance(blk, int) else blk * BS + j + 1 for j in range(BS)]
                for j in range(BS):
                    hp, hn = h32[:, (j - 1) % BS], h32[:, j]
                    dve.wait_ge(s["r_s"], v[j])
                    V.scalar_tensor_tensor(out=rh_hi[:], in0=rg[:], scalar=1.0, in1=hp,
                                           op0=ALU.add, op1=ALU.mult).then_inc(s["rh_hi_s"], 1)
                    V.scalar_tensor_tensor(out=rh32[:], in0=rg[:], scalar=1.0, in1=hp,
                                           op0=ALU.add, op1=ALU.mult).then_inc(s["rh32_s"], 1)
                    dve.wait_ge(s["rh32_s"], v[j])
                    V.tensor_tensor(rh_lo[:], rh32[:], rh_hi[:], ALU.subtract).then_inc(s["rh_lo_s"], 1)
                    dve.wait_ge(s["z_s"], v[j])
                    V.tensor_scalar(zh[:], zg[:], H_SCALE / 2, H_SCALE / 2, ALU.mult, ALU.add)
                    V.tensor_scalar(zm1[:], zg[:], 0.5, 0.5, ALU.mult, ALU.subtract).then_inc(s["zm1_s"], 1)
                    dve.wait_ge(s["zm1_s"], v[j])
                    V.tensor_tensor(negkeep[:], zm1[:], hp, ALU.mult).then_inc(s["keep_s"], 1)
                    after_keep(j)
                    dve.wait_ge(s["cand_s"], v[j])
                    V.tensor_tensor(znew[:], cand[:], zh[:], ALU.mult).then_inc(s["znew_s"], 1)
                    if j == 0:
                        dve.wait_ge(s["h_saved"], blk + START)
                    dve.wait_ge(s["znew_s"], v[j])
                    V.tensor_tensor(h_hi[:], znew[:], negkeep[:], ALU.subtract).then_inc(s["h_hi_s"], 1)
                    V.tensor_tensor(hn, znew[:], negkeep[:], ALU.subtract).then_inc(s["h32_s"], 1)
                    dve.wait_ge(s["h32_s"], v[j])
                    V.tensor_tensor(h_lo[:], hn, h_hi[:], ALU.subtract).then_inc(s["h_lo_s"], 1)
                    after_h(j)

            def nothing(j):
                pass

            def add_b1(half, e, cnt):
                dve.wait_ge(s[f"up{half}_made"], cnt + 1 + START)
                dve.wait_ge(s[f"hid{half}_made"], cnt + START)
                c = slice(half * 256, half * 256 + 256)
                bias = (b1_sb[:, e, c] if isinstance(e, int)
                        else b1_sb[:, bass.ds(e, 1), c].rearrange("p a f -> p (a f)"))
                V.tensor_tensor(pre[:, c], p_up[half][:, 0:256], bias, ALU.add).then_inc(s[f"pre{half}_made"], 1)

            def accumulate(e, cnt):
                dve.wait_ge(s["dn_made"], cnt + 1 + START)
                w = gate[:, e:e + 1] if isinstance(e, int) else gate[:, bass.ds(e, 1)]
                V.scalar_tensor_tensor(out=acc[:], in0=p_dn[:, 0:D], scalar=w, in1=acc[:],
                                       op0=ALU.mult, op1=ALU.add).then_inc(s["acc_made"], 1)

            def take_projection(n, gt):
                banks = (p_tr, p_dn, p_misc)
                dve.wait_ge(s["proj_made"], 3 * n + gt + 1)
                if gt == 0 and not (isinstance(n, int) and n == 0):
                    dve.wait_ge(s["xp_copied"], n)
                V.scalar_tensor_tensor(
                    out=xp_next[:, gt].rearrange("p (t m b) -> p m b t", m=KD, b=NB),
                    in0=banks[gt][:, 0:D].rearrange("p (m b t) -> p m b t", m=KD, b=NB), scalar=GATE_SCALE[gt],
                    in1=vbias[:, gt].unsqueeze(3).broadcast_to([P, KD, NB, CS]),
                    op0=ALU.mult, op1=ALU.add).then_inc(s["proj_taken"], 1)

            def gating(m, part):
                gc = lambda k: m * NG + k
                q = s["gchain"]
                if part == -1:
                    dve.wait_ge(s["logits_made"], m + 1)
                    V.tensor_copy(lgT[:], p_up[0][0:NE, 0:P]).then_inc(s["lgT_copied"], 1)
                elif part == 0:
                    dve.wait_ge(s["logits_turned"], m + 1)
                    V.tensor_copy(lg[:], p_up[1][:, 0:NE]).then_inc(q, 1)
                    dve.wait_ge(q, gc(1))
                    V.reduce_max(st[:, 0:1], lg[:], AX).then_inc(q, 1)
                    dve.wait_ge(q, gc(2))
                    V.tensor_scalar(dl[:], lg[:], st[:, 0:1], None, ALU.subtract).then_inc(q, 1)
                elif part == 1:
                    dve.wait_ge(q, gc(4))
                    V.reduce_sum(st[:, 1:2], ex[:], AX).then_inc(q, 1)
                elif part == 2:
                    dve.wait_ge(q, gc(5))
                    V.reciprocal(st[:, 2:3], st[:, 1:2]).then_inc(q, 1)
                    dve.wait_ge(q, gc(6))
                    V.tensor_scalar(pr[:], ex[:], st[:, 2:3], None, ALU.mult).then_inc(q, 1)
                    dve.wait_ge(q, gc(7))
                    V.reduce_max(st[:, 3:4], pr[:], AX).then_inc(q, 1)
                elif part == 3:
                    dve.wait_ge(q, gc(8))
                    V.scalar_tensor_tensor(out=cd[:], in0=pr[:], scalar=st[:, 3:4], in1=desc[:],
                                           op0=ALU.is_equal, op1=ALU.mult).then_inc(q, 1)
                    dve.wait_ge(q, gc(9))
                    V.reduce_max(st[:, 4:5], cd[:], AX).then_inc(q, 1)
                    dve.wait_ge(q, gc(10))
                    V.tensor_scalar(sel1[:], desc[:], st[:, 4:5], None, ALU.is_equal).then_inc(q, 1)
                elif part == 4:
                    dve.wait_ge(q, gc(11))
                    V.scalar_tensor_tensor(out=pr2[:], in0=sel1[:], scalar=-2.0, in1=pr[:],
                                           op0=ALU.mult, op1=ALU.add).then_inc(q, 1)
                    dve.wait_ge(q, gc(12))
                    V.reduce_max(st[:, 5:6], pr2[:], AX).then_inc(q, 1)
                    dve.wait_ge(q, gc(13))
                    V.scalar_tensor_tensor(out=cd[:], in0=pr2[:], scalar=st[:, 5:6], in1=desc[:],
                                           op0=ALU.is_equal, op1=ALU.mult).then_inc(q, 1)
                elif part == 5:
                    r = s["gchain2"]
                    dve.wait_ge(q, gc(14))
                    V.reduce_max(st[:, 6:7], cd[:], AX).then_inc(r, 1)
                    dve.wait_ge(r, m * 4 + 1)
                    V.scalar_tensor_tensor(out=sel[:], in0=desc[:], scalar=st[:, 6:7], in1=sel1[:],
                                           op0=ALU.is_equal, op1=ALU.add).then_inc(r, 1)
                    V.tensor_scalar(st[:, 7:8], st[:, 3:4], st[:, 5:6], 1e-10, ALU.add, ALU.max).then_inc(r, 1)
                    dve.wait_ge(r, m * 4 + 3)
                    V.reciprocal(st[:, 7:8], st[:, 7:8]).then_inc(r, 1)
                elif part == 6:
                    dve.wait_ge(s["gchain2"], m * 4 + 4)
                    V.scalar_tensor_tensor(out=gate[:], in0=pr[:], scalar=st[:, 7:8], in1=sel[:],
                                           op0=ALU.mult, op1=ALU.mult).then_inc(s["gate_made"], 1)

            def take_base(m):
                dve.wait_ge(s["base_made"], m + 1 + START)
                V.tensor_copy(acc[:], p_misc[:, 0:D]).then_inc(s["base_taken"], 1)

            def finish_chunk(m, cnt):
                dve.wait_ge(s["acc_made"], cnt + 1 + START)
                V.tensor_scalar(acc[:], acc[:], -100.0, 100.0, ALU.max, ALU.min).then_inc(s["clip_made"], 1)
                dve.wait_ge(s["clip_made"], m + 1)
                dve.wait_ge(s["ld_xres"], 32 * (m + 1))
                dve.wait_ge(s["x1_stored"], 32 * m + START)
                V.tensor_tensor(x1_sb[:], x_res[:], acc[:], ALU.add).then_inc(s["x1_made"], 1)

            V.memset(h32[:], 0.0).then_inc(s["e_prep"], 1)
            V.memset(euler[:], 2.718281828459045).then_inc(s["e_prep"], 1)
            V.memset(h_hi[:], 0.0).then_inc(s["h_hi_s"], 1)
            V.memset(h_lo[:], 0.0).then_inc(s["h_lo_s"], 1)
            dve.wait_ge(s["raw_free"], 3)
            for gt in range(3):
                last = V.tensor_tensor(vbias[:, gt], p_up[1][:, gt * GC:(gt + 1) * GC].rearrange("p (m b) -> p m b", b=NB),
                                       bias_sb[:, gt].unsqueeze(2).broadcast_to([P, KD, NB]), ALU.add)
            last.then_inc(s["e_prep"], 1)
            dve.wait_ge(s["e_prep"], 3)
            for gt in range(3):
                V.tensor_scalar(vbias[:, gt], vbias[:, gt], GATE_SCALE[gt], None, ALU.mult).then_inc(s["vb_made"], 1)
            dve.wait_ge(s["vb_made"], 3)
            for gt in range(3):
                take_projection(0, gt)
            for i in range(3):
                dve.wait_ge(s["ld_u"], 16 * (4 + i))
                V.tensor_scalar(split32[:], raw[:], W_SCALE, None, ALU.mult).then_inc(s["raw_free"], 1)
                dve.wait_ge(s["raw_free"], 4 + i)
                V.tensor_copy(uh[:, i, 0], split32[:]).then_inc(s["raw_scaled"], 1)
                dve.wait_ge(s["raw_scaled"], i + 1)
                V.tensor_tensor(uh[:, i, 1], split32[:], uh[:, i, 0], ALU.subtract).then_inc(s["u_split"], 1)
                dve.wait_ge(s["u_split"], i + 1)

            dve.wait_ge(s["wsum_made"], 1)
            V.tensor_scalar(wsum[:, 0:3], p_gate[0][:, 0:3], 1.0 / (INNER * D), 1e-5, ALU.mult, ALU.max).then_inc(s["wscale_made"], 1)
            dve.wait_ge(s["wscale_made"], 1)
            V.reciprocal(wscale[:, 0:3], wsum[:, 0:3]).then_inc(s["wscale_made"], 1)
            dve.wait_ge(s["wscale_made"], 2)
            for i in range(3):
                V.tensor_scalar(l1_tmp[i], l1_raw[i], wscale[:, i:i + 1], ROUND, ALU.mult, ALU.add).then_inc(s["wq1"], 1)
                dve.wait_ge(s["wq1"], i + 1)
                V.tensor_scalar(l1_tmp[i], l1_tmp[i], ROUND, 1.0, ALU.subtract, ALU.min).then_inc(s["wq2"], 1)
                dve.wait_ge(s["wq2"], i + 1)
                V.tensor_scalar(l1_q[i], l1_tmp[i], -1.0, None, ALU.max).then_inc(s["wq3"], 1)
            for n in range(NB * KD):
                bb, k = n // KD, n % KD
                V.scalar_tensor_tensor(out=mix_w4[:, bb, k], in0=mix_raw[:, k], scalar=D ** -0.5, in1=cond_bc[:, bb],
                                       op0=ALU.mult, op1=ALU.mult).then_inc(s["mw_made"], 1)
            dve.wait_ge(s["msq_made"], NB * KD)
            V.tensor_scalar(msum[:], msum[:], 1e-8, None, ALU.add).then_inc(s["mn_made"], 1)
            dve.wait_ge(s["mnorm_made"], 1)
            for n in range(NB * KD):
                bb, k = n // KD, n % KD
                V.tensor_scalar(mix_n4[:, bb, k], mix_w4[:, bb, k], mnorm[:, n:n + 1], None, ALU.mult).then_inc(s["mixn_made"], 1)

            with dve.Fori(0, BPC - 2) as k:
                four_steps(k, nothing, nothing)
            four_steps(BPC - 2, nothing, nothing)
            four_steps(BPC - 1, nothing, lambda j: take_projection(1, j) if j < 3 else None)
            dve.wait_ge(s["ld_b1"], 16)

            def gating_slots(m, project_too):
                def after_keep(j):
                    if j == 2:
                        gating(m, 1)
                    elif j == 3:
                        gating(m, 2)

                def after_h(j):
                    if j == 0:
                        gating(m, -1)
                    elif j == 1:
                        gating(m, 0)
                    if j and project_too:
                        take_projection(m + 2, j - 1)
                return after_keep, after_h

            def first_slots(m, c0):
                def after_keep(j):
                    if j == 0:
                        gating(m, 3)
                    elif j == 1:
                        gating(m, 4)
                    elif j == 2:
                        gating(m, 6)

                def after_h(j):
                    if j == 0:
                        add_b1(0, 0, c0)
                    elif j == 1:
                        add_b1(1, 0, c0)
                        gating(m, 5)
                    elif j == 3:
                        take_base(m)
                return after_keep, after_h

            def expert_slots(x0, c0):
                def after_h(j):
                    if j < 2:
                        add_b1(j, x0, c0)
                    elif j == 3:
                        accumulate(x0 - 1, c0 - 1)
                return nothing, after_h

            def last_slots(m, cnt):
                def after_h(j):
                    if j == 2:
                        accumulate(NE - 1, cnt)
                    elif j == 3:
                        finish_chunk(m, cnt)
                return nothing, after_h

            def alone(slots):
                for j in range(BS):
                    slots[0](j)
                    slots[1](j)

            with dve.Fori(1, NCH) as n:
                m = dve.snap(n - 1)
                four_steps(n * BPC, *gating_slots(m, True))
                four_steps(n * BPC + 1, *first_slots(m, m * NE))
                with dve.Fori(1, NE) as e:
                    four_steps(n * BPC + 1 + e, *expert_slots(e, dve.snap(m * NE + e)))
                four_steps(n * BPC + BPC - 1, *last_slots(m, m * NE + NE - 1))
            m = NCH - 1
            alone(gating_slots(m, False))
            alone(first_slots(m, m * NE))
            with dve.Fori(1, NE) as e:
                alone(expert_slots(e, dve.snap(m * NE + e)))
            alone(last_slots(m, m * NE + NE - 1))

            for n in range(NB * KD * 2):
                c = slice(n * 512, (n + 1) * 512)
                two = slice(2 * n, 2 * n + 2)
                dve.wait_ge(s["mix_copied"], n + 1)
                V.tensor_reduce(x_max[:, two], mixed[:, c].rearrange("p (t i) -> p t i", t=2), AX, ALU.max,
                                apply_absolute_value=True).then_inc(s["x_chain"], 1)
                dve.wait_ge(s["x_chain"], 3 * n + 1)
                V.tensor_scalar(x_step[:, two], x_max[:, two], 1e-5, 1.0 / 127.0, ALU.max, ALU.mult).then_inc(s["x_chain"], 1)
                dve.wait_ge(s["x_chain"], 3 * n + 2)
                V.reciprocal(x_inv[:, two], x_step[:, two]).then_inc(s["x_chain"], 1)
                dve.wait_ge(s["x_chain"], 3 * n + 3)
                if n:
                    dve.wait_ge(s["q_made"], n)
                for i in range(2):
                    V.tensor_scalar(xr[:, i * D:(i + 1) * D], mixed[:, n * 512 + i * D:n * 512 + (i + 1) * D],
                                    x_inv[:, 2 * n + i:2 * n + i + 1], ROUND, ALU.mult, ALU.add).then_inc(s["xr_made"], 1)
                dve.wait_ge(s["xr_made"], 2 * n + 2)
                V.tensor_scalar(q_all[:, c], xr, ROUND, 127.0, ALU.subtract, ALU.min).then_inc(s["q_made"], 1)
            for i, st_ in enumerate((g_step, u_step)):
                V.tensor_scalar(st_[:], x_step[:], wsum[:, i:i + 1], None, ALU.mult).then_inc(s["steps_made"], 1)
            dve.wait_ge(s["steps_made"], 2)

            def silu_times_up(t):
                for half in range(2):
                    c = slice(half * 512, (half + 1) * 512)
                    dve.wait_ge(s["sig1_made"], 2 * t + half + 1)
                    V.scalar_tensor_tensor(out=gs[:, c], in0=p_up[half][:], scalar=g_step[:, bass.ds(t, 1)], in1=sg[:, c],
                                           op0=ALU.mult, op1=ALU.mult).then_inc(s["gs_made"], 1)
                dve.wait_ge(s["hr_made"], t)
                for half in range(2):
                    c = slice(half * 512, (half + 1) * 512)
                    dve.wait_ge(s["up_mm"], 2 * t + half + 1)
                    dve.wait_ge(s["gs_made"], 2 * t + half + 1)
                    V.scalar_tensor_tensor(out=hh[:, c], in0=(p_misc, p_tr)[half][:], scalar=u_step[:, bass.ds(t, 1)],
                                           in1=gs[:, c], op0=ALU.mult, op1=ALU.mult).then_inc(s["hh_made"], 1)
                dve.wait_ge(s["hh_made"], 2 * t + 2)
                V.tensor_reduce(h_st[:, 0:1], hh, AX, ALU.max, apply_absolute_value=True).then_inc(s["h_chain"], 1)

            def h_scales(t):
                dve.wait_ge(s["h_chain"], 2 * t + 1)
                V.tensor_scalar(h_st[:, 1:2], h_st[:, 0:1], 1e-5, 1.0 / 127.0, ALU.max, ALU.mult).then_inc(s["h_chain"], 1)
                dve.wait_ge(s["h_chain"], 2 * t + 2)
                V.reciprocal(h_st[:, 2:3], h_st[:, 1:2]).then_inc(s["h_inv_made"], 1)

            def finish(t):
                dve.wait_ge(s["down_mm"], t + 1 + START)
                V.scalar_tensor_tensor(out=out_sb[:, bass.ds(t * D, D)], in0=p_gate[2][:, 0:D], scalar=h_st[:, 3:4],
                                       in1=x1_mix[:, bass.ds(t * D, D)], op0=ALU.mult, op1=ALU.add).then_inc(s["out_made"], 1)

            def h_step(t):
                V.tensor_scalar(h_st[:, 3:4], h_st[:, 1:2], wsum[:, 2:3], None, ALU.mult).then_inc(s["h_step_made"], 1)
                dve.wait_ge(s["h_step_made"], t + 1)

            silu_times_up(0)
            h_scales(0)
            with dve.Fori(1, NT) as t:
                h_step(t - 1)
                silu_times_up(t)
                finish(t - 1)
                h_scales(t)
            h_step(NT - 1)
            finish(NT - 1)


_INS = ["x", "cond_1024", "L0_cond_W_z", "L0_cond_U_z", "L0_cond_C_z", "L0_cond_b_z", "L0_cond_W_r", "L0_cond_U_r",
        "L0_cond_C_r", "L0_cond_b_r", "L0_cond_W", "L0_cond_U", "L0_cond_C", "L0_cond_b", "L0_ffn_gate_w",
        "L0_ffn_w1", "L0_ffn_b1", "L0_ffn_w2", "L0_ffn_b2", "L1_cond_weight", "L1_ffn_w_gate", "L1_ffn_w_up",
        "L1_ffn_w_down"]


def kernel(**inputs):
    import numpy as np
    import concourse.bacc as bacc
    from concourse.bass_utils import run_bass_kernel_spmd

    nc = bacc.Bacc("TRN2", target_bir_lowering=False, num_devices=1)
    arrays, args = {}, []
    for name in _INS:
        a = np.ascontiguousarray(inputs[name])
        arrays["in_" + name] = a
        args.append(nc.dram_tensor("in_" + name, a.shape, mybir.dt.from_np(a.dtype), kind="ExternalInput").ap())
    out = nc.dram_tensor("out", (NB, T, D), F32, kind="ExternalOutput").ap()
    build(nc, *args, out)
    return run_bass_kernel_spmd(nc, [arrays], core_ids=[0]).results[0]["out"]
```

```python
from contextlib import ExitStack

import concourse.bass as bass
from concourse import mybir

P = 128
NB = 2
T = 1024
D = 256
KD = D // P
NE = 14
FF = 512
KF = FF // P
BS = 4
CS = P // NB
BPC = CS // BS
NCH = T // CS
INNER = 1024
KI = INNER // P
GC = KD * NB
R_, Z_, U_ = 0, 1, 2

H_SCALE = 2.0 ** 14
W_SCALE = 2.0 ** 6
PRE_SCALE = H_SCALE * W_SCALE
GATE_SCALE = (PRE_SCALE, PRE_SCALE, 2 * PRE_SCALE)
WARM_UP = 16
START = 1
ROUND = 1.5 * 2.0 ** 23

F32, F16, BF16 = mybir.dt.float32, mybir.dt.float16, mybir.dt.bfloat16
ALU, ACT, AX = mybir.AluOpType, mybir.ActivationFunctionType, mybir.AxisListType.X


def build(nc, x, cond, W_z, U_z, C_z, b_z, W_r, U_r, C_r, b_r, W, U, C, b,
          gate_w, w1, b1, w2, b2, mix_w, w_gate, w_up, w_down, out):
    ctx = ExitStack()
    with ctx:
        def sb(name, shape, dt=F32):
            return ctx.enter_context(nc.sbuf_tensor(name, shape, dt))

        def pb(name):
            return ctx.enter_context(nc.psum_tensor(name, [P, 512], F32))

        def sem(name):
            return ctx.enter_context(nc.semaphore(name))

        w1_sb = sb("w1_sb", [P, NE, KD, FF])
        w2_sb = sb("w2_sb", [P, NE, KF, D])
        b1_sb = sb("b1_sb", [P, NE, FF])
        b2_sb = sb("b2_sb", [P, D])
        gw_raw = sb("gw_raw", [NE, D])
        gwT = sb("gwT", [P, KD, NE])
        wx = sb("wx", [P, 3, KD, D])
        raw = sb("raw", [P, KD, D])
        split32 = sb("split32", [P, KD, D])
        uh = sb("uh", [P, 3, 2, KD, D], F16)
        condT = sb("condT", [P, KD, NB])
        bias_sb = sb("bias_sb", [P, 3, KD])
        vbias = sb("vbias", [P, 3, KD, NB])
        ident = sb("ident", [P, P])
        ident_bf = sb("ident_bf", [P, P], BF16)
        desc = sb("desc", [P, NE])
        desc_i = sb("desc_i", [P, NE], mybir.dt.int32)

        x_next = sb("x_next", [P, D])
        xT = sb("xT", [P, KD, P])
        xp_next = sb("xp_next", [P, 3, CS * GC])
        xp = sb("xp", [P, 3, CS * GC])
        xa = sb("xa", [P, 3, BS * GC])
        xb = sb("xb", [P, 3, BS * GC])
        xc = sb("xc", [P, 3, BS * GC])
        xi = sb("xi", [P, 3, 3, BS * GC], BF16)

        h32 = sb("h32", [P, BS, GC])
        h_hi = sb("h_hi", [P, GC], F16)
        h_lo = sb("h_lo", [P, GC], F16)
        rg = sb("rg", [P, GC])
        zg = sb("zg", [P, GC])
        zm1 = sb("zm1", [P, GC])
        zh = sb("zh", [P, GC])
        cand = sb("cand", [P, GC])
        rh32 = sb("rh32", [P, GC])
        rh_hi = sb("rh_hi", [P, GC], F16)
        rh_lo = sb("rh_lo", [P, GC], F16)
        negkeep = sb("negkeep", [P, GC])
        znew = sb("znew", [P, GC])

        h_chunk = sb("h_chunk", [P, CS, GC])
        hT = sb("hT", [P, KD, P])
        pre = sb("pre", [P, FF])
        hid = sb("hid", [P, FF])
        hidT = sb("hidT", [P, FF])
        acc = sb("acc", [P, D])
        weighted = sb("weighted", [P, D])
        x_res = sb("x_res", [P, D])
        x1_sb = sb("x1_sb", [P, D])

        lgT = sb("lgT", [NE, P])
        lg = sb("lg", [P, NE])
        dl = sb("dl", [P, NE])
        euler = sb("euler", [P, NE])
        warm = sb("warm", [P, NE])
        ex = sb("ex", [P, NE])
        pr = sb("pr", [P, NE])
        cd = sb("cd", [P, NE])
        sel1 = sb("sel1", [P, NE])
        pr2 = sb("pr2", [P, NE])
        sel = sb("sel", [P, NE])
        gate = sb("gate", [P, NE])
        gateT = sb("gateT", [P, P])
        st = sb("st", [P, 8])

        wgT = sb("wgT", [P, KD, INNER], BF16)
        wuT = sb("wuT", [P, KD, INNER], BF16)
        wdT = sb("wdT", [P, KI, D], BF16)
        mixT = sb("mixT", [P, KD, NB, D])
        ones = sb("ones", [P, P])
        wsum = sb("wsum", [P, 4])
        wscale = sb("wscale", [P, 4])
        msum = sb("msum", [P, NB * KD])
        mnorm = sb("mnorm", [P, NB * KD])
        mhalf = sb("mhalf", [P, NB * KD])
        hqT = sb("hqT", [P, INNER], BF16)
        NT = NB * T // P
        x_step = sb("x_step", [P, NT])
        x_inv = sb("x_inv", [P, NT])
        x_max = sb("x_max", [P, NT])
        g_step = sb("g_step", [P, NT])
        u_step = sb("u_step", [P, NT])
        h_max = sb("h_max", [P, 1])
        h_step = sb("h_step", [P, 1])
        h_inv = sb("h_inv", [P, 2])
        d_step = sb("d_step", [P, NT])

        w1_flat = w1_sb[:].rearrange("p e k f -> p (e k f)")
        w2_flat = w2_sb[:].rearrange("p e k f -> p (e k f)")
        b1_flat = b1_sb[:].rearrange("p e f -> p (e f)")
        NW = 2048
        l1_raw = [w1_flat[:, i * NW:(i + 1) * NW] for i in range(3)]
        l1_tmp = [w2_flat[:, i * NW:(i + 1) * NW] for i in range(3)]
        l1_q = [w2_flat[:, (3 + i) * NW:(3 + i) * NW + NW // 2].bitcast(BF16) for i in range(3)]
        mix_raw = w1_flat[:, 3 * NW:3 * NW + KD * D].rearrange("p (k i) -> p k i", k=KD)
        cond_bc = w1_flat[:, 3 * NW + 512:3 * NW + 512 + NB * D].rearrange("p (b i) -> p b i", b=NB)
        mix_w4 = w1_flat[:, 4 * NW:4 * NW + 1024].rearrange("p (b k i) -> p b k i", b=NB, k=KD)
        mix_n4 = w1_flat[:, 4 * NW + 1024:5 * NW].rearrange("p (b k i) -> p b k i", b=NB, k=KD)
        sq_tmp = w1_flat[:, 5 * NW:5 * NW + D]
        x1_mix = b1_flat[:, 0:4096]
        mixed = w1_flat[:, 0:4096]
        out_sb = w1_flat[:, 4096:8192]
        xr = w2_flat[:, 0:512]
        q_all = w2_flat[:, 5120:7168].bitcast(BF16)
        qT_all = w2_flat[:, 7168:9216].bitcast(BF16)
        pair = lambda c: [w2_flat[:, c + i * INNER:c + (i + 1) * INNER] for i in range(2)]
        sg = pair(1024)
        gs = pair(3072)
        hh = pair(9216)
        hr = pair(11264)
        hq = [w2_flat[:, 13312 + i * 512:13824 + i * 512].bitcast(BF16) for i in range(2)]

        p_gate = [pb("p_r"), pb("p_z"), pb("p_u")]
        p_up = [pb("p_up0"), pb("p_up1")]
        p_tr = pb("p_tr")
        p_dn = pb("p_dn")
        p_misc = pb("p_misc")

        x1_dram = nc.dram_tensor("x1_scratch", (NB, T, D), F32).ap()

        s = {n: sem(n) for n in (
            "ld_small", "ld_u", "ld_w1", "ld_w2", "ld_b1", "ld_xnext", "ld_xres", "x1_stored",
            "const_made", "zeroed", "raw_free", "raw_scaled", "u_split", "p_prep", "e_prep", "vb_made",
            "h_hi_s", "h32_s", "h_lo_s", "r_pre", "z_pre", "u_pre", "r_s", "z_s", "cand_s",
            "rh_hi_s", "rh32_s", "rh_lo_s", "zm1_s", "keep_s", "znew_s",
            "xi_ready", "u_injected", "h_saved", "pool_chain", "pool_waits", "act_waits",
            "hT_made", "xT_made", "xT_copied", "proj_made", "proj_taken", "logits_made", "lgT_copied", "logits_turned",  "gate_made", "gateT_made", "gateT_copied", "base_made", "base_taken", "x1_made",
            "gchain", "gsum_made", "second_found", "ginv_made", "sel_made", "clip_made", "xp_copied", "gwT_made", "act_prep",
            "up0_made", "up1_made", "pre0_made", "pre1_made", "hid0_made", "hid1_made",
            "tr_made", "hidT_made", "dn_made", "weighted_made", "acc_made",
            "ld_l1", "ones_made", "abs_made", "wsum_made", "wscale_made", "wq1", "wq2", "wq3", "wT_made", "wT_copied",
            "mw_made", "msq_made", "mn_made", "mnorm_made", "mixn_made", "mixT_made", "mixT_copied",
            "ld_mix", "mix_made", "mix_copied",
            "x_chain", "xr_made", "q_made", "qT_made", "qT_copied", "steps_made", "gate_mm", "up_mm",
            "av_made", "gs_made", "hh_made", "h_chain", "h_inv_made", "hr_made", "hq_made", "hqT_made",
            "hqT_copied", "down_mm", "out_made",
            "out_stored")}

        started = ("weighted_made", "h_saved", "pre0_made", "pre1_made", "hidT_made", "acc_made", "base_taken", "tr_made", "dn_made",
                   "hid0_made", "hid1_made", "x1_stored", "x1_made", "base_made", "up0_made", "up1_made", "hqT_made",
                   "hqT_copied", "out_made", "down_mm")

        block = ctx.enter_context(nc.Block())
        NG = 14

        @block.sync
        def _(sp):
            xk = lambda a: a.rearrange("(k p) e -> p k e", p=P)

            def token_tile(dst, chunk, sem_):
                for bb in range(NB):
                    sp.dma_start(dst[bb * CS:(bb + 1) * CS, :], x[bb, bass.ds(chunk * CS, CS), :]).then_inc(s[sem_], 16)

            for name in started:
                sp.sem_inc(s[name], START)
            token_tile(x_next, 0, "ld_xnext")
            for g, w in enumerate((W_r, W_z, W)):
                sp.dma_start(wx[:, g], xk(w)).then_inc(s["ld_small"], 16)
            for g, v in enumerate((b_r, b_z, b)):
                sp.dma_start(bias_sb[:, g], v.rearrange("(k p) -> p k", p=P), allow_slow_non_contiguous=True).then_inc(s["ld_small"], 16)
            for k in range(KD):
                sp.dma_start(condT[:, k], cond[:, k * P:(k + 1) * P].rearrange("b p -> p b"),
                             allow_slow_non_contiguous=True).then_inc(s["ld_small"], 16)
            sp.dma_start(gw_raw[:], gate_w).then_inc(s["ld_small"], 16)
            sp.wait_ge(s["zeroed"], 2)
            sp.dma_start(b2_sb[0:NE, :], b2).then_inc(s["ld_small"], 16)
            for i, w in enumerate((C_r, C_z, C, U_r, U_z, U)):
                if i:
                    sp.wait_ge(s["raw_free"], i)
                sp.dma_start(raw[:], xk(w)).then_inc(s["ld_u"], 16)
            for i, w in enumerate((w_gate, w_up, w_down)):
                cols = w.shape[1]
                sp.dma_start(l1_raw[i].rearrange("p (k c) -> p k c", c=cols),
                             w.rearrange("(k p) c -> p k c", p=P)).then_inc(s["ld_l1"], 16)
            sp.dma_start(mix_raw, mix_w.rearrange("a (k p) i c -> p (a k) (i c)", p=P)).then_inc(s["ld_l1"], 16)
            for bb in range(NB):
                sp.dma_start(cond_bc[:, bb], cond[bb, :].partition_broadcast(P)).then_inc(s["ld_l1"], 16)
            sp.wait_ge(s["wT_copied"], 6)
            sp.wait_ge(s["mixT_copied"], KD)
            w1_v = w1.rearrange("e (k p) f -> p (e k) f", p=P)
            w2_v = w2.rearrange("e (k p) d -> p (e k) d", p=P)
            w1_t = w1_sb[:].rearrange("p e k f -> p (e k) f")
            w2_t = w2_sb[:].rearrange("p e k d -> p (e k) d")
            for i in range(0, NE * KD, 7):
                sp.dma_start(w1_t[:, i:i + 7], w1_v[:, i:i + 7]).then_inc(s["ld_w1"], 16)
            for i in range(0, NE * KF, 14):
                sp.dma_start(w2_t[:, i:i + 14], w2_v[:, i:i + 14]).then_inc(s["ld_w2"], 16)
            sp.dma_start(b1_sb[:].rearrange("p e f -> p (e f)"),
                         b1.rearrange("e f -> (e f)").partition_broadcast(P)).then_inc(s["ld_b1"], 16)

            def next_x(n, chunk):
                sp.wait_ge(s["xT_made"], n)
                token_tile(x_next, chunk, "ld_xnext")

            next_x(1, 1)
            next_x(2, 2)

            def chunk(n, coming):
                if not (isinstance(n, int) and n == 1):
                    sp.wait_ge(s["x1_made"], n - 1 + START)
                token_tile(x_res, n - 1, "ld_xres")
                if coming is not None:
                    next_x(n + 2, coming)
                store(n - 1)

            def store(m):
                sp.wait_ge(s["x1_made"], m + 1 + START)
                for bb in range(NB):
                    sp.dma_start(x1_dram[bb, bass.ds(m * CS, CS), :], x1_sb[bb * CS:(bb + 1) * CS, :]).then_inc(s["x1_stored"], 16)

            with sp.Fori(1, NCH - 2) as n:
                chunk(n, n + 2)
            chunk(NCH - 2, 0)
            chunk(NCH - 1, None)
            chunk(NCH, None)
            sp.wait_ge(s["x1_stored"], 32 * NCH + START)
            x1_v = x1_dram.rearrange("b (k p q) c -> (b k) p (q c)", p=P, q=4)
            out_v = out.rearrange("b (k p q) c -> (b k) p (q c)", p=P, q=4)
            for i in range(NB * KD):
                sp.dma_start(x1_mix[:, i * 1024:(i + 1) * 1024], x1_v[i]).then_inc(s["ld_mix"], 16)
            for i in range(NB * KD):
                sp.wait_ge(s["out_made"], 4 * (i + 1) + START)
                sp.dma_start(out_v[i], out_sb[:, i * 1024:(i + 1) * 1024]).then_inc(s["out_stored"], 16)
            sp.wait_ge(s["out_stored"], 16 * NB * KD)

        @block.gpsimd
        def _(pool):
            g = nc.gpsimd
            g.memset(b2_sb[:], 0.0).then_inc(s["zeroed"], 1)
            g.memset(gateT[:], 0.0).then_inc(s["zeroed"], 1)
            g.memset(ident[:], 0.0).then_inc(s["pool_chain"], 1)
            g.memset(ident_bf[:], 0.0).then_inc(s["pool_chain"], 1)
            g.iota(desc_i[:], pattern=[[-1, NE]], base=NE, channel_multiplier=0).then_inc(s["pool_chain"], 1)
            pool.wait_ge(s["pool_chain"], 3)
            for m in (ident, ident_bf):
                g.affine_select(out=m[:], in_=m[:], compare_op=ALU.not_equal, fill=1.0,
                                base=0, pattern=[[-1, P]], channel_multiplier=1).then_inc(s["const_made"], 1)
            g.tensor_copy(desc[:], desc_i[:]).then_inc(s["const_made"], 1)

            XI_OPS = 5

            def wait(name, value):
                pool.wait_ge(s[name], value)
                pool.sem_inc(s["pool_waits"], 1)

            def split_block(col, done):
                c0 = 3 + done * XI_OPS
                if not (isinstance(done, int) and done == 0):
                    wait("xi_ready", done)
                g.tensor_copy(xa[:], xp[:, :, bass.ds(col, BS * GC)]).then_inc(s["pool_chain"], 1)
                wait("pool_chain", c0 + 1)
                g.tensor_copy(xi[:, 0], xa[:]).then_inc(s["pool_chain"], 1)
                wait("pool_chain", c0 + 2)
                g.tensor_tensor(xb[:], xa[:], xi[:, 0], ALU.subtract).then_inc(s["pool_chain"], 1)
                wait("pool_chain", c0 + 3)
                g.tensor_copy(xi[:, 1], xb[:]).then_inc(s["pool_chain"], 1)
                wait("pool_chain", c0 + 4)
                g.tensor_tensor(xc[:], xb[:], xi[:, 1], ALU.subtract).then_inc(s["pool_chain"], 1)
                wait("pool_chain", c0 + 5)
                g.tensor_copy(xi[:, 2], xc[:]).then_inc(s["xi_ready"], 1)

            def take_projection(n):
                wait("proj_taken", 3 * n + 3)
                for gt in range(3):
                    last = g.tensor_tensor(xp[:, gt].rearrange("p (t c) -> p t c", c=GC),
                                           xp_next[:, gt].rearrange("p (t c) -> p t c", c=GC),
                                           vbias[:, gt].rearrange("p m b -> p (m b)").unsqueeze(1).broadcast_to([P, CS, GC]),
                                           ALU.add)
                last.then_inc(s["xp_copied"], 1)
                wait("xp_copied", n + 1)

            def save_states(blk, col):
                wait("h32_s", blk * BS + BS)
                g.tensor_copy(h_chunk[:].rearrange("p t c -> p (t c)")[:, bass.ds(col, BS * GC)],
                              h32[:].rearrange("p t c -> p (t c)")).then_inc(s["h_saved"], 1)

            def make_hT(m):
                wait("h_saved", (m + 1) * BPC + START)
                if not (isinstance(m, int) and m == 0):
                    wait("base_made", m + START)
                    wait("up1_made", m * NE + START)
                g.tensor_scalar(hT[:].rearrange("p k (b t) -> p k b t", b=NB),
                                h_chunk[:].rearrange("p t (k b) -> p k b t", k=KD),
                                1.0 / H_SCALE, None, ALU.mult).then_inc(s["hT_made"], 1)
                wait("hT_made", m + 1)

            g.memset(ones[:], 1.0).then_inc(s["ones_made"], 1)
            g.memset(mhalf[:], -0.5).then_inc(s["ones_made"], 1)
            pool.wait_ge(s["vb_made"], 3)
            take_projection(0)
            split_block(0, 0)
            pool.wait_ge(s["mn_made"], 1)
            g.tensor_tensor(mnorm[:], msum[:], mhalf[:], ALU.pow).then_inc(s["mnorm_made"], 1)

            def exponentials(m):
                pool.wait_ge(s["gchain"], m * NG + 3)
                g.tensor_tensor(ex[:], euler[:], dl[:], ALU.pow).then_inc(s["gchain"], 1)

            def accumulate(cnt):
                wait("weighted_made", cnt + 1 + START)
                g.tensor_tensor(acc[:], acc[:], weighted[:], ALU.add).then_inc(s["acc_made"], 1)

            def finish_chunk(m):
                accumulate(m * NE + NE - 1)
                wait("acc_made", (m + 1) * NE + START)
                g.tensor_scalar(acc[:], acc[:], -100.0, 100.0, ALU.max, ALU.min).then_inc(s["clip_made"], 1)
                wait("clip_made", m + 1)
                wait("ld_xres", 32 * m + 32)
                wait("x1_stored", 32 * m + START)
                g.tensor_tensor(x1_sb[:], x_res[:], acc[:], ALU.add).then_inc(s["x1_made"], 1)

            def next_block(n, k):
                wait("u_injected", n * BPC + k + 1)
                split_block((k + 1) * BS * GC, n * BPC + k + 1)

            def chunk_ends(n):
                wait("u_injected", n * BPC + BPC)
                take_projection(n + 1)
                split_block(0, n * BPC + BPC)

            def save(n, k):
                save_states(n * BPC + k, k * BS * GC)

            with pool.Fori(0, BPC - 1) as k:
                next_block(0, k)
                save(0, k)
            chunk_ends(0)
            save(0, BPC - 1)

            def gating_block(n, m, first):
                make_hT(m)
                next_block(n, 0)
                exponentials(m)
                if not first:
                    finish_chunk(m - 1)
                save(n, 0)

            def rest_of_chunk(n, m):
                for k in (1, 2):
                    next_block(n, k)
                    save(n, k)
                with pool.Fori(3, BPC - 1) as k:
                    next_block(n, k)
                    accumulate(m * NE + k - 3)
                    save(n, k)
                chunk_ends(n)
                accumulate(m * NE + NE - 2)
                save(n, BPC - 1)

            gating_block(1, 0, True)
            rest_of_chunk(1, 0)
            with pool.Fori(2, NCH) as n:
                m = pool.snap(n - 1)
                gating_block(n, m, False)
                rest_of_chunk(n, m)
            m = NCH - 1
            make_hT(m)
            exponentials(m)
            finish_chunk(m - 1)
            with pool.Fori(0, NE - 1) as e:
                accumulate(m * NE + e)
            finish_chunk(m)

            def gated(t, par):
                wait("av_made", 2 * t + 2)
                g.tensor_tensor(gs[par], gs[par], sg[par], ALU.mult).then_inc(s["gs_made"], 1)

            def scale_h(t, par):
                wait("h_inv_made", t + 1)
                g.tensor_scalar(hr[par], hh[par], h_inv[:, par:par + 1], ROUND, ALU.mult, ALU.add).then_inc(s["hr_made"], 1)

            def iteration(i, par=None):
                par, tile = (i % 2, lambda lag: 0 <= i - lag < NT) if par is None else (par, lambda lag: True)
                if tile(0):
                    gated(i, par)
                if tile(1):
                    scale_h(i - 1, 1 - par)

            for i in range(4):
                iteration(i)
            with pool.Fori(2, NT // 2) as k:
                for parity in range(2):
                    iteration(pool.snap(2 * k + parity), parity)
            for i in range(NT, NT + 3):
                iteration(i)

        @block.tensor
        def _(pe):
            mm = nc.tensor.matmul

            def products(gt, part, src, j, name=None, pieces=range(4)):
                for i in pieces:
                    m, k = i // KD, i % KD
                    c = j * GC + m * NB
                    last = mm(p_gate[gt][:, c:c + NB], uh[:, gt, part, k, m * P:(m + 1) * P],
                              src[:, k * NB:(k + 1) * NB], start=False, stop=True, skip_group_check=True)
                if name:
                    last.then_inc(s[name], 1)

            def inject(gt):
                for part in range(3):
                    last = mm(p_gate[gt][:, 0:BS * GC], ident_bf[:], xi[:, part, gt], start=(part == 0), stop=True,
                              skip_group_check=True)
                return last

            def four_steps(blk, after_z, after_u):
                v = [pe.snap(blk * BS + j) if not isinstance(blk, int) else blk * BS + j for j in range(BS + 1)]
                for j in range(BS):
                    pe.wait_ge(s["h_hi_s"], v[j] + 1)
                    products(R_, 0, h_hi, j)
                    products(R_, 1, h_hi, j)
                    products(Z_, 0, h_hi, j, pieces=(0, 1))
                    pe.wait_ge(s["h_lo_s"], v[j] + 1)
                    products(R_, 0, h_lo, j, "r_pre")
                    if j == 0:
                        inject(U_).then_inc(s["u_injected"], 1)
                    products(Z_, 0, h_hi, j, pieces=(2, 3))
                    products(Z_, 1, h_hi, j)
                    products(Z_, 0, h_lo, j, "z_pre")
                    after_z(j)
                    pe.wait_ge(s["rh_hi_s"], v[j + 1])
                    products(U_, 0, rh_hi, j)
                    products(U_, 1, rh_hi, j)
                    pe.wait_ge(s["rh_lo_s"], v[j + 1])
                    products(U_, 0, rh_lo, j, "u_pre")
                    if j == BS - 1:
                        pe.wait_ge(s["z_s"], v[j + 1])
                        pe.wait_ge(s["xi_ready"], blk + 2)
                        inject(R_)
                        inject(Z_)
                    after_u(j)

            def nothing(j):
                pass

            def up(e, cnt, pieces):
                for i in pieces:
                    c, k = i // KD, i % KD
                    if i == 0:
                        pe.wait_ge(s["pre0_made"], cnt + START)
                    if i == 4:
                        pe.wait_ge(s["pre1_made"], cnt + START)
                    last = mm(p_up[c // 2][:, c % 2 * P:(c % 2 + 1) * P], hT[:, k],
                              w1_sb[:, bass.ds(e, 1), k, c * P:(c + 1) * P].rearrange("p a f -> p (a f)")
                              if not isinstance(e, int) else w1_sb[:, e, k, c * P:(c + 1) * P],
                              start=(k == 0), stop=(k == KD - 1), skip_group_check=True)
                    if i == 3:
                        last.then_inc(s["up0_made"], 1)
                    if i == 7:
                        last.then_inc(s["up1_made"], 1)

            def turn(cnt, quarters):
                for c in quarters:
                    if c == 0:
                        pe.wait_ge(s["hid0_made"], cnt + 1 + START)
                        pe.wait_ge(s["hidT_made"], cnt + START)
                    if c == 2:
                        pe.wait_ge(s["hid1_made"], cnt + 1 + START)
                    last = nc.tensor.transpose(p_tr[:, c * P:(c + 1) * P], hid[:, c * P:(c + 1) * P], ident[:])
                    if c == 3:
                        last.then_inc(s["tr_made"], 1)

            def down(e, cnt, pieces):
                for i in pieces:
                    f, half = i // 2, i % 2
                    if i == 0:
                        pe.wait_ge(s["hidT_made"], cnt + 1 + START)
                        pe.wait_ge(s["weighted_made"], cnt + START)
                    last = mm(p_dn[:, half * P:(half + 1) * P], hidT[:, f * P:(f + 1) * P],
                              w2_sb[:, bass.ds(e, 1), f, half * P:(half + 1) * P].rearrange("p a f -> p (a f)")
                              if not isinstance(e, int) else w2_sb[:, e, f, half * P:(half + 1) * P],
                              start=(i == 0), stop=(f == KF - 1), skip_group_check=True)
                    if i == 7:
                        last.then_inc(s["dn_made"], 1)

            def turn_x(n):
                pe.wait_ge(s["ld_xnext"], 32 * (n + 1))
                if not (isinstance(n, int) and n < 2):
                    pe.wait_ge(s["base_taken"], n - 2 + START)
                elif n == 1:
                    pe.wait_ge(s["proj_taken"], 3)
                for k in range(KD):
                    last = nc.tensor.transpose(p_misc[:, k * P:(k + 1) * P], x_next[:, k * P:(k + 1) * P], ident[:])
                last.then_inc(s["xT_made"], 1)

            def project(n, pieces, n_experts=None):
                banks = (p_tr, p_dn, p_misc)
                for i in pieces:
                    gt, m, k = i // 4, i // 2 % 2, i % 2
                    if i == 0:
                        pe.wait_ge(s["xT_copied"], n + 1)
                        if n_experts is not None:
                            pe.wait_ge(s["weighted_made"], n_experts + START)
                    last = mm(banks[gt][:, m * P:(m + 1) * P], wx[:, gt, k, m * P:(m + 1) * P], xT[:, k],
                              start=(k == 0), stop=(k == KD - 1), skip_group_check=True)
                    if i % 4 == 3:
                        last.then_inc(s["proj_made"], 1)

            def logits(m):
                pe.wait_ge(s["hT_made"], m + 1)
                pe.wait_ge(s["pre0_made"], m * NE + START)
                for k in range(KD):
                    last = mm(p_up[0][0:NE, 0:P], gwT[:, k], hT[:, k], start=(k == 0), stop=(k == KD - 1))
                last.then_inc(s["logits_made"], 1)

            def turn_logits(m):
                nc.tensor.transpose(p_up[1][:, 0:NE], lgT[:, :], ident[0:NE, 0:NE]).then_inc(s["logits_turned"], 1)

            def keep_warm(bank, n, cols=512):
                for _ in range(n):
                    mm(bank[:, 0:cols], ident_bf[:], wgT[:, 0, 0:cols], start=True, stop=True, skip_group_check=True)

            def turn_gate(m):
                pe.wait_ge(s["gate_made"], m + 1)
                mm(p_dn[0:NE, 0:P], gate[:, :], ident[:], start=True, stop=True, is_transpose=True).then_inc(s["gateT_made"], 1)

            def base(m, parts):
                for i in parts:
                    if i < KD:
                        mm(p_misc[:, i * P:(i + 1) * P], hT[:, i], ident[:], start=(i == 0), stop=False,
                           skip_group_check=True)
                    else:
                        pe.wait_ge(s["gateT_copied"], m + 1)
                        mm(p_misc[:, 0:D], gateT[:, :], b2_sb[:, :], start=False, stop=True,
                           skip_group_check=True).then_inc(s["base_made"], 1)

            pe.wait_ge(s["const_made"], 3)
            pe.wait_ge(s["ld_small"], 16 * 10)
            for k in range(KD):
                last = nc.tensor.transpose(p_up[0][:, k * 16:k * 16 + NE], gw_raw[:, k * P:(k + 1) * P], ident[0:NE, 0:NE])
            last.then_inc(s["p_prep"], 1)
            turn_x(0)
            for gt in range(3):
                pe.wait_ge(s["ld_u"], 16 * (gt + 1))
                for m in range(KD):
                    for k in range(KD):
                        last = mm(p_up[1][:, gt * GC + m * NB:gt * GC + (m + 1) * NB], raw[:, k, m * P:(m + 1) * P],
                                  condT[:, k], start=(k == 0), stop=(k == KD - 1), skip_group_check=True)
                last.then_inc(s["raw_free"], 1)
            project(0, range(12))

            pe.wait_ge(s["ones_made"], 2)
            pe.wait_ge(s["abs_made"], 3)
            mm(p_gate[0][:, 0:3], ones[:], wsum[:, 0:3], start=True, stop=True).then_inc(s["wsum_made"], 1)
            banks = (p_gate[1], p_gate[2])
            for n in range(6):
                i, half = n // 2, n % 2
                pe.wait_ge(s["wq3"], i + 1)
                if n > 1:
                    pe.wait_ge(s["wT_copied"], n - 1)
                dst = banks[n % 2][:].bitcast(BF16)
                for o in range(8):
                    if i < 2:
                        src = l1_q[i].rearrange("p (o c) -> p o c", o=8)[:, o, half * P:(half + 1) * P]
                    else:
                        src = l1_q[i].rearrange("p (o c) -> p o c", o=KD)[:, o % KD, (half * 4 + o // KD) * P:(half * 4 + o // KD + 1) * P]
                    last = nc.tensor.transpose(dst[:, o * P:(o + 1) * P], src, ident_bf[:])
                last.then_inc(s["wT_made"], 1)
            pe.wait_ge(s["mixn_made"], 4)
            pe.wait_ge(s["wT_copied"], 6)
            for k in range(KD):
                for bb in range(NB):
                    for o in range(KD):
                        c = (bb * KD + o) * P
                        last = nc.tensor.transpose(banks[k][:, c:c + P], mix_n4[:, bb, o, k * P:(k + 1) * P], ident[:])
                last.then_inc(s["mixT_made"], 1)
            pe.wait_ge(s["mixT_copied"], KD)
            pe.wait_ge(s["wscale_made"], 2)
            pe.wait_ge(s["u_split"], 3)
            pe.wait_ge(s["xi_ready"], 1)
            inject(R_)
            inject(Z_)

            pe.wait_ge(s["gwT_made"], KD)
            with pe.Fori(0, BPC - 2) as k:
                four_steps(k, nothing, nothing)

            def fill_x(n):
                def after_u(j):
                    if j == 0:
                        turn_x(n)
                    else:
                        project(n, range(4 * (j - 1), 4 * j))
                return after_u

            four_steps(BPC - 2, nothing, fill_x(1))
            four_steps(BPC - 1, nothing, nothing)
            pe.wait_ge(s["ld_w1"], 16 * 4)
            pe.wait_ge(s["ld_w2"], 16 * 4)
            keep_warm(p_up[1], WARM_UP)

            def expert_slots(x0, c0, m, warm=True):
                def after_z(j):
                    if j == 0:
                        up(x0, c0, (0,))
                        turn(c0 - 1, (3,))
                    elif j == 1:
                        up(x0, c0, (4,))
                    elif j == 2:
                        down(x0 - 1, c0 - 1, (0,))
                    else:
                        down(x0 - 1, c0 - 1, (5,))
                        turn(c0, (0,))
                    if j in (1, 2) and warm:
                        keep_warm(p_misc, 1, 256)

                def after_u(j):
                    if j == 0:
                        up(x0, c0, (1, 2, 3))
                        if warm:
                            pe.wait_ge(s["base_taken"], m + 1 + START)
                    elif j == 1:
                        up(x0, c0, (5, 6, 7))
                    elif j == 2:
                        down(x0 - 1, c0 - 1, (1, 2, 3, 4))
                    else:
                        down(x0 - 1, c0 - 1, (6, 7))
                        turn(c0, (1, 2))
                    if j < 2 and warm:
                        keep_warm(p_misc, 1, 256)
                return after_z, after_u

            def gating_slots(m, project_too):
                def after_z(j):
                    if j == 0:
                        pe.wait_ge(s["pre1_made"], m * NE + START)
                        if project_too:
                            keep_warm(p_up[1], 1)
                    elif j == 1:
                        pe.wait_ge(s["lgT_copied"], m + 1)
                        if project_too:
                            keep_warm(p_up[0], 1, 256)
                        turn_logits(m)
                        if project_too:
                            project(m + 2, (0,), m * NE)
                    elif project_too:
                        project(m + 2, (4 * (j - 1),))
                    if project_too and j != 1:
                        keep_warm(p_up[0] if j else p_up[1], 1, 256)

                def after_u(j):
                    if j == 0:
                        if project_too:
                            turn_x(m + 2)
                        logits(m)
                        if project_too:
                            keep_warm(p_up[1], 1)
                    elif project_too:
                        project(m + 2, range(4 * j - 3, 4 * j))
                return after_z, after_u

            def first_slots(m, c0, warm=True):
                def after_z(j):
                    if j == 0:
                        up(0, c0, (0,))
                    elif j == 1:
                        pe.wait_ge(s["gchain"], m * NG + 1)
                        up(0, c0, (4,))
                    elif j == 2:
                        pe.wait_ge(s["proj_taken"], base_waits(m))
                        base(m, (0,))
                    if warm:
                        if j == 0:
                            pe.wait_ge(s["proj_taken"], base_waits(m))
                        keep_warm(p_dn, (1, 3, 2, 2)[j], 256)
                    if j == 3:
                        turn_gate(m)
                        turn(c0, (0,))

                def after_u(j):
                    if j == 0:
                        up(0, c0, (1, 2, 3))
                    elif j == 1:
                        up(0, c0, (5, 6, 7))
                    if j < 2 and warm:
                        keep_warm(p_dn, 1, 256)
                    if j == 2:
                        base(m, (1,))
                        if warm:
                            keep_warm(p_dn, 2)
                    elif j == 3:
                        base(m, (2,))
                        turn(c0, (1, 2))
                return after_z, after_u

            def base_waits(m):
                return 3 * (m + 3) if not (isinstance(m, int) and m == NCH - 1) else 3 * (NCH + 1)

            def last_slots(cnt, warm=True):
                def after_z(j):
                    if j == 0:
                        turn(cnt, (3,))
                        pe.wait_ge(s["pre1_made"], cnt + 1 + START)
                        if warm:
                            keep_warm(p_up[1], 1)
                    elif j == 1:
                        down(NE - 1, cnt, (0,))
                    elif j == 2:
                        down(NE - 1, cnt, (4,))
                    elif warm:
                        keep_warm(p_up[1], 1)
                    if warm and j:
                        keep_warm(p_up[1], 1, 256)

                def after_u(j):
                    if j == 1:
                        down(NE - 1, cnt, (1, 2, 3))
                    elif j == 2:
                        down(NE - 1, cnt, (5, 6, 7))
                    elif warm:
                        keep_warm(p_up[1], 3)
                return after_z, after_u

            def alone(slots):
                for j in range(BS):
                    slots[0](j)
                    slots[1](j)

            with pe.Fori(1, NCH) as n:
                m = pe.snap(n - 1)
                four_steps(n * BPC, *gating_slots(m, True))
                four_steps(n * BPC + 1, *first_slots(m, m * NE))
                with pe.Fori(1, NE) as e:
                    four_steps(n * BPC + 1 + e, *expert_slots(e, pe.snap(m * NE + e), m))
                four_steps(n * BPC + BPC - 1, *last_slots(m * NE + NE - 1))

            m = NCH - 1
            alone(gating_slots(m, False))
            alone(first_slots(m, m * NE, False))
            with pe.Fori(1, NE) as e:
                alone(expert_slots(e, pe.snap(m * NE + e), m, False))
            alone(last_slots(m * NE + NE - 1, False))

            pe.wait_ge(s["ld_mix"], 16 * NB * KD)
            mix_banks = (p_up[0], p_up[1])

            def turn_q(n):
                pe.wait_ge(s["q_made"], n + 1)
                if n:
                    pe.wait_ge(s["qT_copied"], n)
                for i in range(4):
                    last = nc.tensor.transpose(p_gate[0][:].bitcast(BF16)[:, i * P:(i + 1) * P],
                                               q_all[:, n * 512 + i * P:n * 512 + (i + 1) * P], ident_bf[:])
                last.then_inc(s["qT_made"], 1)

            for n in range(NB * KD * 2):
                bb, o, half = n // 4, n // 2 % 2, n % 2
                if n > 1:
                    pe.wait_ge(s["mix_copied"], n - 1)
                for k in range(KD):
                    c = (bb * KD + k) * 1024 + half * 512
                    last = mm(mix_banks[n % 2][:], mixT[:, k, bb, o * P:(o + 1) * P], x1_mix[:, c:c + 512],
                              start=(k == 0), stop=(k == KD - 1))
                last.then_inc(s["mix_made"], 1)
                if n > 1:
                    turn_q(n - 2)
            turn_q(NB * KD * 2 - 2)
            turn_q(NB * KD * 2 - 1)

            def integer_product(t, banks, w, read, made):
                for half in range(2):
                    if not (isinstance(t, int) and t == 0):
                        pe.wait_ge(s[read], 2 * t - 1 + half)
                    for k in range(KD):
                        last = mm(banks[half][:], qT_all[:, bass.ds(t * D + k * P, P)],
                                  w[:, k, half * 512:(half + 1) * 512], start=(k == 0), stop=(k == KD - 1))
                    last.then_inc(s[made], 1)

            def turn_h(t, par):
                pe.wait_ge(s["hq_made"], t + 1)
                pe.wait_ge(s["hqT_copied"], t + START)
                for k in range(KI):
                    last = nc.tensor.transpose(p_gate[1][:].bitcast(BF16)[:, k * P:(k + 1) * P], hq[par][:, k * P:(k + 1) * P],
                                               ident_bf[:])
                last.then_inc(s["hqT_made"], 1)

            def down_l1(t):
                pe.wait_ge(s["hqT_copied"], t + 1 + START)
                pe.wait_ge(s["out_made"], t + START)
                for k in range(KI):
                    last = mm(p_gate[2][:, 0:D], hqT[:, k * P:(k + 1) * P], wdT[:, k], start=(k == 0), stop=(k == KI - 1))
                last.then_inc(s["down_mm"], 1)

            pe.wait_ge(s["mix_copied"], 2 * NB * KD)
            pe.wait_ge(s["qT_copied"], 2 * NB * KD)

            def iteration(i, par=None):
                par, tile = (i % 2, lambda lag: 0 <= i - lag < NT) if par is None else (par, lambda lag: True)
                if tile(3):
                    turn_h(i - 3, 1 - par)
                if tile(0):
                    integer_product(i, p_up, wgT, "av_made", "gate_mm")
                if tile(1):
                    integer_product(i - 1, (p_misc, p_tr), wuT, "hh_made", "up_mm")
                if tile(3):
                    down_l1(i - 3)

            for i in range(4):
                iteration(i)
            with pe.Fori(2, NT // 2) as k:
                for parity in range(2):
                    iteration(pe.snap(2 * k + parity), parity)
            for i in range(NT, NT + 3):
                iteration(i)

        @block.scalar
        def _(act):
            A = nc.scalar.activation

            def four_steps(blk, before_cand, after_cand):
                v = [act.snap(blk * BS + j + 1) if not isinstance(blk, int) else blk * BS + j + 1 for j in range(BS)]
                for j in range(BS):
                    cols = slice(j * GC, (j + 1) * GC)
                    act.wait_ge(s["r_pre"], v[j])
                    A(rg[:], p_gate[R_][:, cols], ACT.Tanh, scale=0.5 / PRE_SCALE).then_inc(s["r_s"], 1)
                    act.wait_ge(s["z_pre"], v[j])
                    A(zg[:], p_gate[Z_][:, cols], ACT.Tanh, scale=0.5 / PRE_SCALE).then_inc(s["z_s"], 1)
                    before_cand(j)
                    act.wait_ge(s["u_pre"], v[j])
                    A(cand[:], p_gate[U_][:, cols], ACT.Tanh, scale=0.5 / PRE_SCALE).then_inc(s["cand_s"], 1)
                    after_cand(j)

            def nothing(j):
                pass

            def gelu_half(half, cnt):
                act.wait_ge(s[f"pre{half}_made"], cnt + 1 + START)
                act.wait_ge(s["tr_made"], cnt + START)
                c = slice(half * 256, half * 256 + 256)
                A(hid[:, c], pre[:, c], ACT.Gelu).then_inc(s[f"hid{half}_made"], 1)

            def copy_hidT(cnt):
                act.wait_ge(s["tr_made"], cnt + 1 + START)
                act.wait_ge(s["dn_made"], cnt + START)
                A(hidT[:], p_tr[:], ACT.Copy).then_inc(s["hidT_made"], 1)

            def copy_xT(n):
                act.wait_ge(s["xT_made"], n + 1)
                act.wait_ge(s["proj_made"], 3 * n)
                A(xT[:].rearrange("p k t -> p (k t)"), p_misc[:, 0:D], ACT.Copy).then_inc(s["xT_copied"], 1)

            def take_projection(n, gt):
                banks = (p_tr, p_dn, p_misc)
                act.wait_ge(s["proj_made"], 3 * n + gt + 1)
                if gt == 0 and not (isinstance(n, int) and n == 0):
                    act.wait_ge(s["xp_copied"], n)
                A(xp_next[:, gt].rearrange("p (t m b) -> p m b t", m=KD, b=NB),
                  banks[gt][:, 0:D].rearrange("p (m b t) -> p m b t", m=KD, b=NB), ACT.Copy,
                  scale=GATE_SCALE[gt]).then_inc(s["proj_taken"], 1)

            def weigh(e, cnt):
                act.wait_ge(s["acc_made"], cnt + START)
                act.sem_inc(s["act_waits"], 1)
                act.wait_ge(s["dn_made"], cnt + 1 + START)
                act.sem_inc(s["act_waits"], 1)
                w = gate[:, e:e + 1] if isinstance(e, int) else gate[:, bass.ds(e, 1)]
                A(weighted[:], p_dn[:, 0:D], ACT.Copy, scale=w).then_inc(s["weighted_made"], 1)

            def take_base(m):
                act.wait_ge(s["base_made"], m + 1 + START)
                act.wait_ge(s["x1_made"], m + START)
                A(acc[:], p_misc[:, 0:D], ACT.Copy).then_inc(s["base_taken"], 1)

            def copy_gateT(m):
                act.wait_ge(s["gateT_made"], m + 1)
                A(gateT[0:NE, :], p_dn[0:NE, 0:P], ACT.Copy).then_inc(s["gateT_copied"], 1)

            act.wait_ge(s["const_made"], 3)
            A(warm[:], desc[:], ACT.Gelu).then_inc(s["act_prep"], 1)
            act.wait_ge(s["p_prep"], 1)
            for k in range(KD):
                A(gwT[:, k], p_up[0][:, k * 16:k * 16 + NE], ACT.Copy).then_inc(s["gwT_made"], 1)
            copy_xT(0)
            for gt in range(3):
                take_projection(0, gt)

            for i in range(3):
                act.wait_ge(s["ld_l1"], 16 * 6)
                A(l1_tmp[i], l1_raw[i], ACT.Abs, accum_out=wsum[:, i:i + 1]).then_inc(s["abs_made"], 1)
            for n in range(NB * KD):
                act.wait_ge(s["mw_made"], n + 1)
                if n:
                    act.wait_ge(s["msq_made"], n)
                A(sq_tmp, mix_w4[:, n // KD, n % KD], ACT.Square, accum_out=msum[:, n:n + 1]).then_inc(s["msq_made"], 1)
            banks = (p_gate[1], p_gate[2])
            for n in range(6):
                i, half = n // 2, n % 2
                dst = (wgT[:, half], wuT[:, half], wdT[:, half * 4:half * 4 + 4].rearrange("p k d -> p (k d)"))[i]
                act.wait_ge(s["wT_made"], n + 1)
                A(dst, banks[n % 2][:].bitcast(BF16), ACT.Copy).then_inc(s["wT_copied"], 1)
            for k in range(KD):
                act.wait_ge(s["mixT_made"], k + 1)
                A(mixT[:, k].rearrange("p b o -> p (b o)"), banks[k][:], ACT.Copy).then_inc(s["mixT_copied"], 1)

            with act.Fori(0, BPC - 2) as k:
                four_steps(k, nothing, nothing)
            four_steps(BPC - 2, nothing, lambda j: copy_xT(1) if j == 0 else None)
            four_steps(BPC - 1, nothing, lambda j: take_projection(1, j) if j < 3 else None)

            def gating_slots(m, project_too):
                def after(j):
                    if project_too:
                        take_projection(m + 2, j - 1) if j else copy_xT(m + 2)
                return nothing, after

            def first_slots(m, c0):
                def after(j):
                    if j == 1:
                        gelu_half(0, c0)
                    elif j == 2:
                        gelu_half(1, c0)

                def before(j):
                    if j == 3:
                        copy_gateT(m)
                return before, after

            def expert_slots(first, c0):
                def after(j):
                    if j == 0:
                        first()
                        copy_hidT(c0 - 1)
                    elif j == 1:
                        gelu_half(0, c0)
                    elif j == 2:
                        gelu_half(1, c0)
                return nothing, after

            def last_slots(cnt):
                def after(j):
                    if j == 0:
                        weigh(NE - 2, cnt - 1)
                        copy_hidT(cnt)
                    elif j == 3:
                        weigh(NE - 1, cnt)
                return nothing, after

            def alone(slots):
                for j in range(BS):
                    slots[0](j)
                    slots[1](j)

            with act.Fori(1, NCH) as n:
                m = act.snap(n - 1)
                four_steps(n * BPC, *gating_slots(m, True))
                four_steps(n * BPC + 1, *first_slots(m, m * NE))
                four_steps(n * BPC + 2, *expert_slots(lambda: take_base(m), m * NE + 1))
                with act.Fori(2, NE) as e:
                    c0 = act.snap(m * NE + e)
                    four_steps(n * BPC + 1 + e, *expert_slots(lambda: weigh(e - 2, c0 - 2), c0))
                four_steps(n * BPC + BPC - 1, *last_slots(m * NE + NE - 1))
            m = NCH - 1
            alone(gating_slots(m, False))
            alone(first_slots(m, m * NE))
            alone(expert_slots(lambda: take_base(m), m * NE + 1))
            with act.Fori(2, NE) as e:
                c0 = act.snap(m * NE + e)
                alone(expert_slots(lambda: weigh(e - 2, c0 - 2), c0))
            alone(last_slots(m * NE + NE - 1))

            mix_banks = (p_up[0], p_up[1])

            def copy_qT(n):
                act.wait_ge(s["qT_made"], n + 1)
                A(qT_all[:, n * 512:(n + 1) * 512], p_gate[0][:].bitcast(BF16)[:, 0:512], ACT.Copy).then_inc(s["qT_copied"], 1)

            for n in range(NB * KD * 2):
                act.wait_ge(s["mix_made"], n + 1)
                A(mixed[:, n * 512:(n + 1) * 512], mix_banks[n % 2][:], ACT.Copy).then_inc(s["mix_copied"], 1)
                if n > 1:
                    copy_qT(n - 2)
            copy_qT(NB * KD * 2 - 2)
            copy_qT(NB * KD * 2 - 1)

            def gates(t, par):
                if not (isinstance(t, int) and t < 2):
                    act.wait_ge(s["gs_made"], t - 1)
                    act.sem_inc(s["act_waits"], 1)
                    act.wait_ge(s["hh_made"], 2 * t - 2)
                    act.sem_inc(s["act_waits"], 1)
                for half in range(2):
                    c = slice(half * 512, (half + 1) * 512)
                    act.wait_ge(s["gate_mm"], 2 * t + half + 1)
                    act.sem_inc(s["act_waits"], 1)
                    A(sg[par][:, c], p_up[half][:], ACT.Sigmoid, scale=g_step[:, bass.ds(t, 1)])
                    A(gs[par][:, c], p_up[half][:], ACT.Copy, scale=g_step[:, bass.ds(t, 1)]).then_inc(s["av_made"], 1)

            def copy_hqT(t):
                act.wait_ge(s["hqT_made"], t + 1 + START)
                act.wait_ge(s["down_mm"], t + START)
                A(hqT[:], p_gate[1][:].bitcast(BF16), ACT.Copy).then_inc(s["hqT_copied"], 1)

            act.wait_ge(s["steps_made"], 2)

            def iteration(i, par=None):
                par, tile = (i % 2, lambda lag: 0 <= i - lag < NT) if par is None else (par, lambda lag: True)
                if tile(3):
                    copy_hqT(i - 3)
                if tile(0):
                    gates(i, par)

            for i in range(4):
                iteration(i)
            with act.Fori(2, NT // 2) as k:
                for parity in range(2):
                    iteration(act.snap(2 * k + parity), parity)
            for i in range(NT, NT + 3):
                iteration(i)

        @block.vector
        def _(dve):
            V = nc.vector

            def four_steps(blk, after_keep, after_h):
                v = [dve.snap(blk * BS + j + 1) if not isinstance(blk, int) else blk * BS + j + 1 for j in range(BS)]
                for j in range(BS):
                    hp, hn = h32[:, (j - 1) % BS], h32[:, j]
                    dve.wait_ge(s["r_s"], v[j])
                    V.scalar_tensor_tensor(out=rh_hi[:], in0=rg[:], scalar=1.0, in1=hp,
                                           op0=ALU.add, op1=ALU.mult).then_inc(s["rh_hi_s"], 1)
                    V.scalar_tensor_tensor(out=rh32[:], in0=rg[:], scalar=1.0, in1=hp,
                                           op0=ALU.add, op1=ALU.mult).then_inc(s["rh32_s"], 1)
                    dve.wait_ge(s["rh32_s"], v[j])
                    V.tensor_tensor(rh_lo[:], rh32[:], rh_hi[:], ALU.subtract).then_inc(s["rh_lo_s"], 1)
                    dve.wait_ge(s["z_s"], v[j])
                    V.tensor_scalar(zh[:], zg[:], H_SCALE / 2, H_SCALE / 2, ALU.mult, ALU.add)
                    V.tensor_scalar(zm1[:], zg[:], 0.5, 0.5, ALU.mult, ALU.subtract).then_inc(s["zm1_s"], 1)
                    dve.wait_ge(s["zm1_s"], v[j])
                    V.tensor_tensor(negkeep[:], zm1[:], hp, ALU.mult).then_inc(s["keep_s"], 1)
                    after_keep(j)
                    dve.wait_ge(s["cand_s"], v[j])
                    V.tensor_tensor(znew[:], cand[:], zh[:], ALU.mult).then_inc(s["znew_s"], 1)
                    if j == 0:
                        dve.wait_ge(s["h_saved"], blk + START)
                    dve.wait_ge(s["znew_s"], v[j])
                    V.tensor_tensor(h_hi[:], znew[:], negkeep[:], ALU.subtract).then_inc(s["h_hi_s"], 1)
                    V.tensor_tensor(hn, znew[:], negkeep[:], ALU.subtract).then_inc(s["h32_s"], 1)
                    dve.wait_ge(s["h32_s"], v[j])
                    V.tensor_tensor(h_lo[:], hn, h_hi[:], ALU.subtract).then_inc(s["h_lo_s"], 1)
                    after_h(j)

            def nothing(j):
                pass

            def add_b1(half, e, cnt):
                dve.wait_ge(s[f"up{half}_made"], cnt + 1 + START)
                dve.wait_ge(s[f"hid{half}_made"], cnt + START)
                c = slice(half * 256, half * 256 + 256)
                bias = (b1_sb[:, e, c] if isinstance(e, int)
                        else b1_sb[:, bass.ds(e, 1), c].rearrange("p a f -> p (a f)"))
                V.tensor_tensor(pre[:, c], p_up[half][:, 0:256], bias, ALU.add).then_inc(s[f"pre{half}_made"], 1)

            def gating(m, part):
                gc = lambda k: m * NG + k
                q = s["gchain"]
                if part == -1:
                    dve.wait_ge(s["logits_made"], m + 1)
                    V.tensor_copy(lgT[:], p_up[0][0:NE, 0:P]).then_inc(s["lgT_copied"], 1)
                elif part == 0:
                    dve.wait_ge(s["logits_turned"], m + 1)
                    V.tensor_copy(lg[:], p_up[1][:, 0:NE]).then_inc(q, 1)
                    dve.wait_ge(q, gc(1))
                    V.reduce_max(st[:, 0:1], lg[:], AX).then_inc(q, 1)
                    dve.wait_ge(q, gc(2))
                    V.tensor_scalar(dl[:], lg[:], st[:, 0:1], None, ALU.subtract).then_inc(q, 1)
                elif part == 1:
                    dve.wait_ge(q, gc(4))
                    V.reduce_sum(st[:, 1:2], ex[:], AX).then_inc(q, 1)
                elif part == 2:
                    dve.wait_ge(q, gc(5))
                    V.reciprocal(st[:, 2:3], st[:, 1:2]).then_inc(q, 1)
                    dve.wait_ge(q, gc(6))
                    V.tensor_scalar(pr[:], ex[:], st[:, 2:3], None, ALU.mult).then_inc(q, 1)
                    dve.wait_ge(q, gc(7))
                    V.reduce_max(st[:, 3:4], pr[:], AX).then_inc(q, 1)
                elif part == 3:
                    dve.wait_ge(q, gc(8))
                    V.scalar_tensor_tensor(out=cd[:], in0=pr[:], scalar=st[:, 3:4], in1=desc[:],
                                           op0=ALU.is_equal, op1=ALU.mult).then_inc(q, 1)
                    dve.wait_ge(q, gc(9))
                    V.reduce_max(st[:, 4:5], cd[:], AX).then_inc(q, 1)
                    dve.wait_ge(q, gc(10))
                    V.tensor_scalar(sel1[:], desc[:], st[:, 4:5], None, ALU.is_equal).then_inc(q, 1)
                elif part == 4:
                    dve.wait_ge(q, gc(11))
                    V.scalar_tensor_tensor(out=pr2[:], in0=sel1[:], scalar=-2.0, in1=pr[:],
                                           op0=ALU.mult, op1=ALU.add).then_inc(q, 1)
                elif part == 5:
                    dve.wait_ge(q, gc(12))
                    V.reduce_max(st[:, 5:6], pr2[:], AX).then_inc(q, 1)
                    dve.wait_ge(q, gc(13))
                    V.tensor_scalar(st[:, 7:8], st[:, 3:4], st[:, 5:6], 1e-10, ALU.add, ALU.max).then_inc(s["gsum_made"], 1)
                    V.scalar_tensor_tensor(out=cd[:], in0=pr2[:], scalar=st[:, 5:6], in1=desc[:],
                                           op0=ALU.is_equal, op1=ALU.mult).then_inc(q, 1)
                elif part == 6:
                    dve.wait_ge(q, gc(14))
                    V.reduce_max(st[:, 6:7], cd[:], AX).then_inc(s["second_found"], 1)
                elif part == 7:
                    dve.wait_ge(s["gsum_made"], m + 1)
                    V.reciprocal(st[:, 7:8], st[:, 7:8]).then_inc(s["ginv_made"], 1)
                    dve.wait_ge(s["second_found"], m + 1)
                    V.scalar_tensor_tensor(out=sel[:], in0=desc[:], scalar=st[:, 6:7], in1=sel1[:],
                                           op0=ALU.is_equal, op1=ALU.add).then_inc(s["sel_made"], 1)
                    dve.wait_ge(s["ginv_made"], m + 1)
                    dve.wait_ge(s["sel_made"], m + 1)
                    dve.wait_ge(s["weighted_made"], m * NE + START)
                    V.scalar_tensor_tensor(out=gate[:], in0=pr[:], scalar=st[:, 7:8], in1=sel[:],
                                           op0=ALU.mult, op1=ALU.mult).then_inc(s["gate_made"], 1)

            V.memset(h32[:], 0.0).then_inc(s["e_prep"], 1)
            V.memset(euler[:], 2.718281828459045).then_inc(s["e_prep"], 1)
            V.memset(h_hi[:], 0.0).then_inc(s["h_hi_s"], 1)
            V.memset(h_lo[:], 0.0).then_inc(s["h_lo_s"], 1)
            dve.wait_ge(s["raw_free"], 3)
            for gt in range(3):
                last = V.tensor_tensor(vbias[:, gt], p_up[1][:, gt * GC:(gt + 1) * GC].rearrange("p (m b) -> p m b", b=NB),
                                       bias_sb[:, gt].unsqueeze(2).broadcast_to([P, KD, NB]), ALU.add)
            last.then_inc(s["e_prep"], 1)
            dve.wait_ge(s["e_prep"], 3)
            for gt in range(3):
                V.tensor_scalar(vbias[:, gt], vbias[:, gt], GATE_SCALE[gt], None, ALU.mult).then_inc(s["vb_made"], 1)
            for i in range(3):
                dve.wait_ge(s["ld_u"], 16 * (4 + i))
                V.tensor_scalar(split32[:], raw[:], W_SCALE, None, ALU.mult).then_inc(s["raw_free"], 1)
                dve.wait_ge(s["raw_free"], 4 + i)
                V.tensor_copy(uh[:, i, 0], split32[:]).then_inc(s["raw_scaled"], 1)
                dve.wait_ge(s["raw_scaled"], i + 1)
                V.tensor_tensor(uh[:, i, 1], split32[:], uh[:, i, 0], ALU.subtract).then_inc(s["u_split"], 1)
                dve.wait_ge(s["u_split"], i + 1)

            dve.wait_ge(s["wsum_made"], 1)
            V.tensor_scalar(wsum[:, 0:3], p_gate[0][:, 0:3], 1.0 / (INNER * D), 1e-5, ALU.mult, ALU.max).then_inc(s["wscale_made"], 1)
            dve.wait_ge(s["wscale_made"], 1)
            V.reciprocal(wscale[:, 0:3], wsum[:, 0:3]).then_inc(s["wscale_made"], 1)
            dve.wait_ge(s["wscale_made"], 2)
            for i in range(3):
                V.tensor_scalar(l1_tmp[i], l1_raw[i], wscale[:, i:i + 1], ROUND, ALU.mult, ALU.add).then_inc(s["wq1"], 1)
                dve.wait_ge(s["wq1"], i + 1)
                V.tensor_scalar(l1_tmp[i], l1_tmp[i], ROUND, 1.0, ALU.subtract, ALU.min).then_inc(s["wq2"], 1)
                dve.wait_ge(s["wq2"], i + 1)
                V.tensor_scalar(l1_q[i], l1_tmp[i], -1.0, None, ALU.max).then_inc(s["wq3"], 1)
            for n in range(NB * KD):
                bb, k = n // KD, n % KD
                V.scalar_tensor_tensor(out=mix_w4[:, bb, k], in0=mix_raw[:, k], scalar=D ** -0.5, in1=cond_bc[:, bb],
                                       op0=ALU.mult, op1=ALU.mult).then_inc(s["mw_made"], 1)
            dve.wait_ge(s["msq_made"], NB * KD)
            V.tensor_scalar(msum[:], msum[:], 1e-8, None, ALU.add).then_inc(s["mn_made"], 1)
            dve.wait_ge(s["mnorm_made"], 1)
            for n in range(NB * KD):
                bb, k = n // KD, n % KD
                V.tensor_scalar(mix_n4[:, bb, k], mix_w4[:, bb, k], mnorm[:, n:n + 1], None, ALU.mult).then_inc(s["mixn_made"], 1)

            with dve.Fori(0, BPC - 2) as k:
                four_steps(k, nothing, nothing)
            four_steps(BPC - 2, nothing, nothing)
            four_steps(BPC - 1, nothing, nothing)
            dve.wait_ge(s["ld_b1"], 16)

            def gating_slots(m):
                def after_keep(j):
                    if j == 3:
                        gating(m, 1)

                def after_h(j):
                    if j != 2:
                        gating(m, {0: -1, 1: 0, 3: 2}[j])
                return after_keep, after_h

            def first_slots(m, c0):
                def after_keep(j):
                    if j in (1, 2):
                        gating(m, {1: 4, 2: 6}[j])

                def after_h(j):
                    if j < 2:
                        add_b1(j, 0, c0)
                    if j < 3:
                        gating(m, {0: 3, 1: 5, 2: 7}[j])
                return after_keep, after_h

            def expert_slots(x0, c0):
                def after_h(j):
                    if j < 2:
                        add_b1(j, x0, c0)
                return nothing, after_h

            def alone(slots):
                for j in range(BS):
                    slots[0](j)
                    slots[1](j)

            with dve.Fori(1, NCH) as n:
                m = dve.snap(n - 1)
                four_steps(n * BPC, *gating_slots(m))
                four_steps(n * BPC + 1, *first_slots(m, m * NE))
                with dve.Fori(1, NE) as e:
                    four_steps(n * BPC + 1 + e, *expert_slots(e, dve.snap(m * NE + e)))
                four_steps(n * BPC + BPC - 1, nothing, nothing)
            m = NCH - 1
            alone(gating_slots(m))
            alone(first_slots(m, m * NE))
            with dve.Fori(1, NE) as e:
                alone(expert_slots(e, dve.snap(m * NE + e)))

            for n in range(NB * KD * 2):
                c = slice(n * 512, (n + 1) * 512)
                two = slice(2 * n, 2 * n + 2)
                dve.wait_ge(s["mix_copied"], n + 1)
                V.tensor_reduce(x_max[:, two], mixed[:, c].rearrange("p (t i) -> p t i", t=2), AX, ALU.max,
                                apply_absolute_value=True).then_inc(s["x_chain"], 1)
                dve.wait_ge(s["x_chain"], 3 * n + 1)
                V.tensor_scalar(x_step[:, two], x_max[:, two], 1e-5, 1.0 / 127.0, ALU.max, ALU.mult).then_inc(s["x_chain"], 1)
                dve.wait_ge(s["x_chain"], 3 * n + 2)
                V.reciprocal(x_inv[:, two], x_step[:, two]).then_inc(s["x_chain"], 1)
                dve.wait_ge(s["x_chain"], 3 * n + 3)
                if n:
                    dve.wait_ge(s["q_made"], n)
                for i in range(2):
                    V.tensor_scalar(xr[:, i * D:(i + 1) * D], mixed[:, n * 512 + i * D:n * 512 + (i + 1) * D],
                                    x_inv[:, 2 * n + i:2 * n + i + 1], ROUND, ALU.mult, ALU.add).then_inc(s["xr_made"], 1)
                dve.wait_ge(s["xr_made"], 2 * n + 2)
                V.tensor_scalar(q_all[:, c], xr, ROUND, 127.0, ALU.subtract, ALU.min).then_inc(s["q_made"], 1)
            for i, st_ in enumerate((g_step, u_step)):
                V.tensor_scalar(st_[:], x_step[:], wsum[:, i:i + 1], None, ALU.mult).then_inc(s["steps_made"], 1)
            dve.wait_ge(s["steps_made"], 2)

            def times_up(t, par):
                for half in range(2):
                    c = slice(half * 512, (half + 1) * 512)
                    if half == 0:
                        dve.wait_ge(s["gs_made"], t + 1)
                    dve.wait_ge(s["up_mm"], 2 * t + half + 1)
                    V.scalar_tensor_tensor(out=hh[par][:, c], in0=(p_misc, p_tr)[half][:], scalar=u_step[:, bass.ds(t, 1)],
                                           in1=gs[par][:, c], op0=ALU.mult, op1=ALU.mult).then_inc(s["hh_made"], 1)

            def round_h(t, par):
                dve.wait_ge(s["hr_made"], t + 1)
                if not (isinstance(t, int) and t < 2):
                    dve.wait_ge(s["hqT_made"], t - 1 + START)
                V.tensor_scalar(hq[par], hr[par], ROUND, 127.0, ALU.subtract, ALU.min).then_inc(s["hq_made"], 1)

            def h_scales(t, par):
                dve.wait_ge(s["hh_made"], 2 * t + 2)
                V.tensor_reduce(h_max[:], hh[par], AX, ALU.max, apply_absolute_value=True).then_inc(s["h_chain"], 1)
                dve.wait_ge(s["h_chain"], 3 * t + 1)
                V.tensor_scalar(h_step[:], h_max[:], 1e-5, 1.0 / 127.0, ALU.max, ALU.mult).then_inc(s["h_chain"], 1)
                dve.wait_ge(s["h_chain"], 3 * t + 2)
                V.reciprocal(h_inv[:, par:par + 1], h_step[:]).then_inc(s["h_inv_made"], 1)
                V.tensor_scalar(d_step[:, bass.ds(t, 1)], h_step[:], wsum[:, 2:3], None, ALU.mult).then_inc(s["h_chain"], 1)

            def finish(t):
                dve.wait_ge(s["h_chain"], 3 * t + 3)
                dve.wait_ge(s["down_mm"], t + 1 + START)
                V.scalar_tensor_tensor(out=out_sb[:, bass.ds(t * D, D)], in0=p_gate[2][:, 0:D], scalar=d_step[:, bass.ds(t, 1)],
                                       in1=x1_mix[:, bass.ds(t * D, D)], op0=ALU.mult, op1=ALU.add).then_inc(s["out_made"], 1)

            def iteration(i, par=None):
                par, tile = (i % 2, lambda lag: 0 <= i - lag < NT) if par is None else (par, lambda lag: True)
                if tile(1):
                    times_up(i - 1, 1 - par)
                if tile(2):
                    round_h(i - 2, par)
                if tile(1):
                    h_scales(i - 1, 1 - par)
                if tile(3):
                    finish(i - 3)

            for i in range(4):
                iteration(i)
            with dve.Fori(2, NT // 2) as k:
                for parity in range(2):
                    iteration(dve.snap(2 * k + parity), parity)
            for i in range(NT, NT + 3):
                iteration(i)


_INS = ["x", "cond_1024", "L0_cond_W_z", "L0_cond_U_z", "L0_cond_C_z", "L0_cond_b_z", "L0_cond_W_r", "L0_cond_U_r",
        "L0_cond_C_r", "L0_cond_b_r", "L0_cond_W", "L0_cond_U", "L0_cond_C", "L0_cond_b", "L0_ffn_gate_w",
        "L0_ffn_w1", "L0_ffn_b1", "L0_ffn_w2", "L0_ffn_b2", "L1_cond_weight", "L1_ffn_w_gate", "L1_ffn_w_up",
        "L1_ffn_w_down"]


def kernel(**inputs):
    import numpy as np
    import concourse.bacc as bacc
    from concourse.bass_utils import run_bass_kernel_spmd

    nc = bacc.Bacc("TRN2", target_bir_lowering=False, num_devices=1)
    arrays, args = {}, []
    for name in _INS:
        a = np.ascontiguousarray(inputs[name])
        arrays["in_" + name] = a
        args.append(nc.dram_tensor("in_" + name, a.shape, mybir.dt.from_np(a.dtype), kind="ExternalInput").ap())
    out = nc.dram_tensor("out", (NB, T, D), F32, kind="ExternalOutput").ap()
    build(nc, *args, out)
    return run_bass_kernel_spmd(nc, [arrays], core_ids=[0]).results[0]["out"]
```

```python
from contextlib import ExitStack

import concourse.bass as bass
from concourse import mybir

P = 128
NB = 2
T = 1024
D = 256
KD = D // P
NE = 14
FF = 512
KF = FF // P
BS = 4
CS = P // NB
BPC = CS // BS
NCH = T // CS
INNER = 1024
KI = INNER // P
GC = KD * NB
R_, Z_, U_ = 0, 1, 2

H_SCALE = 2.0 ** 14
W_SCALE = 2.0 ** 6
PRE_SCALE = H_SCALE * W_SCALE
GATE_SCALE = (PRE_SCALE, PRE_SCALE, 2 * PRE_SCALE)
WARM_UP = 16
WARM_MIX = 24
START = 1
ROUND = 1.5 * 2.0 ** 23

F32, F16, BF16 = mybir.dt.float32, mybir.dt.float16, mybir.dt.bfloat16
ALU, ACT, AX = mybir.AluOpType, mybir.ActivationFunctionType, mybir.AxisListType.X


def build(nc, x, cond, W_z, U_z, C_z, b_z, W_r, U_r, C_r, b_r, W, U, C, b,
          gate_w, w1, b1, w2, b2, mix_w, w_gate, w_up, w_down, out):
    ctx = ExitStack()
    with ctx:
        def sb(name, shape, dt=F32):
            return ctx.enter_context(nc.sbuf_tensor(name, shape, dt))

        def pb(name):
            return ctx.enter_context(nc.psum_tensor(name, [P, 512], F32))

        def sem(name):
            return ctx.enter_context(nc.semaphore(name))

        w1_sb = sb("w1_sb", [P, NE, KD, FF])
        w2_sb = sb("w2_sb", [P, NE, KF, D])
        b1_sb = sb("b1_sb", [P, NE, FF])
        b2_sb = sb("b2_sb", [P, D])
        gw_raw = sb("gw_raw", [NE, D])
        gwT = sb("gwT", [P, KD, NE])
        wx = sb("wx", [P, 3, KD, D])
        split32 = sb("split32", [P, KD, D])
        uh = sb("uh", [P, 3, 2, KD, D], F16)
        condT = sb("condT", [P, KD, NB])
        bias_sb = sb("bias_sb", [P, 3, KD])
        vbias = sb("vbias", [P, 3, KD, NB])
        ident = sb("ident", [P, P])
        ident_bf = sb("ident_bf", [P, P], BF16)
        desc = sb("desc", [P, NE])
        desc_i = sb("desc_i", [P, NE], mybir.dt.int32)

        x_next = sb("x_next", [P, D])
        xT = sb("xT", [P, KD, P])
        xp_next = sb("xp_next", [P, 3, CS * GC])
        xp = sb("xp", [P, 3, CS * GC])
        xa = sb("xa", [P, 3, BS * GC])
        xb = sb("xb", [P, 3, BS * GC])
        xc = sb("xc", [P, 3, BS * GC])
        xi = sb("xi", [P, 3, 3, BS * GC], BF16)

        second = lambda a: a.rearrange("p (c two) -> p c two", two=2)[:, :, 1]
        zero_z = sb("zero_z", [P, 2 * GC])
        cand_keep = sb("cand_keep", [P, 2 * GC])
        h32_pairs = sb("h32_pairs", [P, BS, 2 * GC])
        h32 = h32_pairs[:].rearrange("p t (c two) -> p t c two", two=2)[:, :, :, 1]
        h_hi_pairs = sb("h_hi_pairs", [P, 2 * GC], F16)
        h_hi = second(h_hi_pairs[:])
        h_lo = sb("h_lo", [P, GC], F16)
        rg = sb("rg", [P, GC])
        zg = sb("zg", [P, GC])
        not_z = sb("not_z", [P, GC])
        rh32 = sb("rh32", [P, GC])
        rh_hi = sb("rh_hi", [P, GC], F16)
        rh_lo = sb("rh_lo", [P, GC], F16)

        h_chunk = sb("h_chunk", [P, CS, GC])
        hT = sb("hT", [P, KD, P])
        pre = sb("pre", [P, FF])
        hid = sb("hid", [P, FF])
        hidT = sb("hidT", [P, FF])
        acc = sb("acc", [P, D])
        weighted = sb("weighted", [P, D])
        x_res = sb("x_res", [P, D])
        x1_sb = sb("x1_sb", [P, D])

        lgT = sb("lgT", [NE, P])
        lg = sb("lg", [P, NE])
        dl = sb("dl", [P, NE])
        euler = sb("euler", [P, NE])
        warm = sb("warm", [P, NE])
        ex = sb("ex", [P, NE])
        pr = sb("pr", [P, NE])
        cd = sb("cd", [P, NE])
        sel1 = sb("sel1", [P, NE])
        pr2 = sb("pr2", [P, NE])
        sel = sb("sel", [P, NE])
        gate = sb("gate", [P, NE])
        gateT = sb("gateT", [P, P])
        st = sb("st", [P, 8])

        wgT = sb("wgT", [P, KD, INNER], BF16)
        wuT = sb("wuT", [P, KD, INNER], BF16)
        wdT = sb("wdT", [P, KI, D], BF16)
        mixT = sb("mixT", [P, KD, NB, D])
        ones = sb("ones", [P, P])
        wsum = sb("wsum", [P, 4])
        wscale = sb("wscale", [P, 4])
        msum = sb("msum", [P, NB * KD])
        mnorm = sb("mnorm", [P, NB * KD])
        mhalf = sb("mhalf", [P, NB * KD])
        hqT = sb("hqT", [P, INNER], BF16)
        NT = NB * T // P
        x_step = sb("x_step", [P, NT])
        x_inv = sb("x_inv", [P, NT])
        x_max = sb("x_max", [P, NT])
        g_step = sb("g_step", [P, NT])
        u_step = sb("u_step", [P, NT])
        h_max = sb("h_max", [P, 1])
        h_step = sb("h_step", [P, 1])
        h_inv = sb("h_inv", [P, 2])
        d_step = sb("d_step", [P, NT])

        w1_flat = w1_sb[:].rearrange("p e k f -> p (e k f)")
        w2_flat = w2_sb[:].rearrange("p e k f -> p (e k f)")
        b1_flat = b1_sb[:].rearrange("p e f -> p (e f)")
        NW = 2048
        l1_raw = [w1_flat[:, i * NW:(i + 1) * NW] for i in range(3)]
        raw = [b1_flat[:, i * KD * D:(i + 1) * KD * D].rearrange("p (k d) -> p k d", k=KD) for i in range(6)]
        l1_q = [b1_flat[:, 3072 + i * NW // 2:3072 + (i + 1) * NW // 2].bitcast(BF16) for i in range(3)]
        mix_raw = w1_flat[:, 3 * NW:3 * NW + KD * D].rearrange("p (k i) -> p k i", k=KD)
        cond_bc = w1_flat[:, 3 * NW + 512:3 * NW + 512 + NB * D].rearrange("p (b i) -> p b i", b=NB)
        mix_w4 = w1_flat[:, 4 * NW:4 * NW + 1024].rearrange("p (b k i) -> p b k i", b=NB, k=KD)
        mix_n4 = w1_flat[:, 4 * NW + 1024:5 * NW].rearrange("p (b k i) -> p b k i", b=NB, k=KD)
        sq_tmp = w1_flat[:, 5 * NW:5 * NW + D]
        x1_mix = b1_flat[:, 0:4096]
        mixed = w1_flat[:, 0:4096]
        out_sb = w1_flat[:, 4096:8192]
        xr = w2_flat[:, 0:512]
        q_all = w2_flat[:, 5120:7168].bitcast(BF16)
        qT_all = w2_flat[:, 7168:9216].bitcast(BF16)
        pair = lambda c: [w2_flat[:, c + i * INNER:c + (i + 1) * INNER] for i in range(2)]
        sg = pair(1024)
        gs = pair(3072)
        hh = pair(9216)
        hr = pair(11264)
        hq = [w2_flat[:, 13312 + i * 512:13824 + i * 512].bitcast(BF16) for i in range(2)]

        p_gate = [pb("p_r"), pb("p_z"), pb("p_u")]
        p_up = [pb("p_up0"), pb("p_up1")]
        p_tr = pb("p_tr")
        p_dn = pb("p_dn")
        p_misc = pb("p_misc")

        x1_dram = nc.dram_tensor("x1_scratch", (NB, T, D), F32).ap()

        s = {n: sem(n) for n in (
            "ld_small", "ld_c", "ld_u", "ld_w1", "ld_w2", "ld_b1", "ld_xnext", "ld_xres", "x1_stored",
            "const_made", "zeroed", "condC_made", "u_scaled", "u_hi_made", "u_split", "p_prep", "e_prep", "vb_made",
            "h_hi_s", "h32_s", "h_lo_s", "r_pre", "z_pre", "u_pre", "r_s", "z_s", "cand_s",
            "rh_hi_s", "rh32_s", "rh_lo_s", "not_z_s", "keep_s",
            "xi_ready", "u_injected", "h_saved", "pool_chain",
            "pool_waits", "act_waits", "table_loaded",
            "hT_started", "hT_made", "xT_made", "xT_copied", "proj_made", "proj_taken", "xp_copied", "gwT_made",
            "logits_made", "lgT_copied", "logits_turned", "gchain", "gsum_made", "second_found", "ginv_made",
            "sel_made", "gate_made", "gateT_made", "gateT_copied", "base_made", "base_taken", "clip_made", "x1_made",
            "up0_made", "up1_made", "pre0_made", "pre1_made", "hid0_made", "hid1_made",
            "tr_made", "hidT_made", "dn_made", "weighted_made", "acc_made",
            "ld_l1", "ones_made", "abs_made", "wsum_made", "wscale_made", "wq1", "wq2", "wq3", "wT_made", "wT_copied",
            "mw_made", "msq_made", "mn_made", "mnorm_made", "mixn_made", "mixT_made", "mixT_copied",
            "ld_mix", "mix_made", "mix_copied",
            "x_chain", "xr_made", "q_made", "qT_made", "qT_copied", "steps_made", "gate_mm", "up_mm",
            "av_made", "gs_made", "hh_made", "h_chain", "h_inv_made", "hr_made", "hq_made", "hqT_made",
            "hqT_copied", "down_mm", "out_made",
            "out_stored")}

        started = ("weighted_made", "h_saved", "pre0_made", "pre1_made", "hidT_made", "acc_made", "base_taken",
                   "tr_made", "dn_made", "hid0_made", "hid1_made", "x1_stored", "x1_made", "base_made", "up0_made", "up1_made", "hqT_made",
                   "hqT_copied", "out_made", "down_mm")

        block = ctx.enter_context(nc.Block())
        NG = 14

        @block.sync
        def _(sp):
            xk = lambda a: a.rearrange("(k p) e -> p k e", p=P)

            def token_tile(dst, chunk, sem_):
                for bb in range(NB):
                    sp.dma_start(dst[bb * CS:(bb + 1) * CS, :], x[bb, bass.ds(chunk * CS, CS), :]).then_inc(s[sem_], 16)

            for name in started:
                sp.sem_inc(s[name], START)
            token_tile(x_next, 0, "ld_xnext")
            for i, w in enumerate((C_r, C_z, C)):
                sp.dma_start(raw[i], xk(w)).then_inc(s["ld_c"], 16)
            for k in range(KD):
                sp.dma_start(condT[:, k], cond[:, k * P:(k + 1) * P].rearrange("b p -> p b"),
                             allow_slow_non_contiguous=True).then_inc(s["ld_small"], 16)
            for g, w in enumerate((W_r, W_z, W)):
                sp.dma_start(wx[:, g], xk(w)).then_inc(s["ld_small"], 16)
            for g, v in enumerate((b_r, b_z, b)):
                sp.dma_start(bias_sb[:, g], v.rearrange("(k p) -> p k", p=P), allow_slow_non_contiguous=True).then_inc(s["ld_small"], 16)
            for i, w in enumerate((U_r, U_z, U)):
                sp.dma_start(raw[3 + i], xk(w)).then_inc(s["ld_u"], 16)
            sp.dma_start(gw_raw[:], gate_w).then_inc(s["ld_small"], 16)
            sp.wait_ge(s["zeroed"], 2)
            sp.dma_start(b2_sb[0:NE, :], b2).then_inc(s["ld_small"], 16)
            for i, w in enumerate((w_gate, w_up, w_down)):
                cols = w.shape[1]
                sp.dma_start(l1_raw[i].rearrange("p (k c) -> p k c", c=cols),
                             w.rearrange("(k p) c -> p k c", p=P)).then_inc(s["ld_l1"], 16)
            sp.dma_start(mix_raw, mix_w.rearrange("a (k p) i c -> p (a k) (i c)", p=P)).then_inc(s["ld_l1"], 16)
            for bb in range(NB):
                sp.dma_start(cond_bc[:, bb], cond[bb, :].partition_broadcast(P)).then_inc(s["ld_l1"], 16)

            def next_x(n, chunk):
                sp.wait_ge(s["xT_made"], n)
                token_tile(x_next, chunk, "ld_xnext")

            next_x(1, 1)

            w1_v = w1.rearrange("e (k p) f -> p (e k) f", p=P)
            w2_v = w2.rearrange("e (k p) d -> p (e k) d", p=P)
            w1_t = w1_sb[:].rearrange("p e k f -> p (e k) f")
            w2_t = w2_sb[:].rearrange("p e k d -> p (e k) d")
            for i in range(0, NE * KF, 14):
                sp.dma_start(w2_t[:, i:i + 14], w2_v[:, i:i + 14]).then_inc(s["ld_w2"], 16)
            for i in (21, 0, 7, 14):
                if i == 0:
                    sp.wait_ge(s["wT_copied"], 6)
                    sp.wait_ge(s["mixT_copied"], KD)
                sp.dma_start(w1_t[:, i:i + 7], w1_v[:, i:i + 7]).then_inc(s["ld_w1"], 16)
            sp.wait_ge(s["condC_made"], 3)
            sp.wait_ge(s["u_split"], 3)
            sp.dma_start(b1_sb[:].rearrange("p e f -> p (e f)"),
                         b1.rearrange("e f -> (e f)").partition_broadcast(P)).then_inc(s["ld_b1"], 16)
            next_x(2, 2)

            def chunk(n, coming):
                if not (isinstance(n, int) and n == 1):
                    sp.wait_ge(s["x1_made"], n - 1 + START)
                token_tile(x_res, n - 1, "ld_xres")
                if coming is not None:
                    next_x(n + 2, coming)
                store(n - 1)

            def store(m):
                sp.wait_ge(s["x1_made"], m + 1 + START)
                for bb in range(NB):
                    sp.dma_start(x1_dram[bb, bass.ds(m * CS, CS), :], x1_sb[bb * CS:(bb + 1) * CS, :]).then_inc(s["x1_stored"], 16)

            with sp.Fori(1, NCH - 2) as n:
                chunk(n, n + 2)
            chunk(NCH - 2, 0)
            chunk(NCH - 1, None)
            sp.wait_ge(s["x1_made"], NCH - 1 + START)
            token_tile(x_res, NCH - 1, "ld_xres")
            x1_v = x1_dram.rearrange("b (k p q) c -> (b k) p (q c)", p=P, q=4)
            out_v = out.rearrange("b (k p q) c -> (b k) p (q c)", p=P, q=4)
            late = P - CS // 4
            sp.wait_ge(s["x1_stored"], 32 * (NCH - 1) + START)
            sp.wait_ge(s["pre0_made"], NCH * NE + START)
            sp.wait_ge(s["pre1_made"], NCH * NE + START)
            for i in range(NB * KD):
                rows = P if i % KD < KD - 1 else late
                sp.dma_start(x1_mix[0:rows, i * 1024:(i + 1) * 1024], x1_v[i, 0:rows]).then_inc(s["ld_mix"], 16)
            store(NCH - 1)
            sp.wait_ge(s["x1_stored"], 32 * NCH + START)
            for i in range(KD - 1, NB * KD, KD):
                sp.dma_start(x1_mix[late:P, i * 1024:(i + 1) * 1024], x1_v[i, late:P]).then_inc(s["ld_mix"], 16)
            for i in range(NB * KD):
                sp.wait_ge(s["out_made"], 4 * (i + 1) + START)
                sp.dma_start(out_v[i], out_sb[:, i * 1024:(i + 1) * 1024]).then_inc(s["out_stored"], 16)
            sp.wait_ge(s["out_stored"], 16 * NB * KD)

        @block.gpsimd
        def _(pool):
            g = nc.gpsimd
            g.memset(b2_sb[:], 0.0).then_inc(s["zeroed"], 1)
            g.memset(gateT[:], 0.0).then_inc(s["zeroed"], 1)
            g.memset(ident[:], 0.0).then_inc(s["pool_chain"], 1)
            g.memset(ident_bf[:], 0.0).then_inc(s["pool_chain"], 1)
            g.iota(desc_i[:], pattern=[[-1, NE]], base=NE, channel_multiplier=0).then_inc(s["pool_chain"], 1)
            pool.wait_ge(s["pool_chain"], 3)
            for m in (ident, ident_bf):
                g.affine_select(out=m[:], in_=m[:], compare_op=ALU.not_equal, fill=1.0,
                                base=0, pattern=[[-1, P]], channel_multiplier=1).then_inc(s["const_made"], 1)
            g.tensor_copy(desc[:], desc_i[:]).then_inc(s["const_made"], 1)

            XI_OPS = 5

            def wait(name, value):
                pool.wait_ge(s[name], value)
                pool.sem_inc(s["pool_waits"], 1)

            def split_block(col, done):
                c0 = 3 + done * XI_OPS
                if not (isinstance(done, int) and done == 0):
                    wait("xi_ready", done)
                g.tensor_copy(xa[:], xp[:, :, bass.ds(col, BS * GC)]).then_inc(s["pool_chain"], 1)
                wait("pool_chain", c0 + 1)
                g.tensor_copy(xi[:, 0], xa[:]).then_inc(s["pool_chain"], 1)
                wait("pool_chain", c0 + 2)
                g.tensor_tensor(xb[:], xa[:], xi[:, 0], ALU.subtract).then_inc(s["pool_chain"], 1)
                wait("pool_chain", c0 + 3)
                g.tensor_copy(xi[:, 1], xb[:]).then_inc(s["pool_chain"], 1)
                wait("pool_chain", c0 + 4)
                g.tensor_tensor(xc[:], xb[:], xi[:, 1], ALU.subtract).then_inc(s["pool_chain"], 1)
                wait("pool_chain", c0 + 5)
                g.tensor_copy(xi[:, 2], xc[:]).then_inc(s["xi_ready"], 1)

            def take_projection(n):
                wait("proj_taken", 3 * n + 3)
                for gt in range(3):
                    last = g.tensor_tensor(xp[:, gt].rearrange("p (t c) -> p t c", c=GC),
                                           xp_next[:, gt].rearrange("p (t c) -> p t c", c=GC),
                                           vbias[:, gt].rearrange("p m b -> p (m b)").unsqueeze(1).broadcast_to([P, CS, GC]),
                                           ALU.add)
                last.then_inc(s["xp_copied"], 1)
                wait("xp_copied", n + 1)

            def save_states(blk, col):
                wait("h32_s", blk * BS + BS)
                g.tensor_copy(h_chunk[:].rearrange("p t c -> p (t c)")[:, bass.ds(col, BS * GC)],
                              h32_pairs[:].rearrange("p t (c two) -> p (t c) two", two=2)[:, :, 1]).then_inc(s["h_saved"], 1)

            def scale_states(t0, t1):
                return g.tensor_scalar(hT[:].rearrange("p k (b t) -> p k b t", b=NB)[:, :, :, t0:t1],
                                       h_chunk[:].rearrange("p t (k b) -> p k b t", k=KD)[:, :, :, t0:t1],
                                       1.0 / H_SCALE, None, ALU.mult)

            def start_hT(m):
                wait("h_saved", m * BPC + BPC - 1 + START)
                if not (isinstance(m, int) and m == 0):
                    wait("base_made", m + START)
                    wait("up1_made", m * NE + START)
                scale_states(0, CS - BS).then_inc(s["hT_started"], 1)

            def finish_hT(m):
                wait("h_saved", (m + 1) * BPC + START)
                wait("hT_started", m + 1)
                scale_states(CS - BS, CS).then_inc(s["hT_made"], 1)
                wait("hT_made", m + 1)

            g.memset(ones[:], 1.0).then_inc(s["ones_made"], 1)
            g.memset(mhalf[:], -0.5).then_inc(s["ones_made"], 1)
            pool.wait_ge(s["vb_made"], 3)
            take_projection(0)
            split_block(0, 0)
            def exponentials(m):
                pool.wait_ge(s["gchain"], m * NG + 3)
                g.tensor_tensor(ex[:], euler[:], dl[:], ALU.pow).then_inc(s["gchain"], 1)

            def accumulate(cnt):
                wait("weighted_made", cnt + 1 + START)
                g.tensor_tensor(acc[:], acc[:], weighted[:], ALU.add).then_inc(s["acc_made"], 1)

            def finish_chunk(m):
                accumulate(m * NE + NE - 1)
                wait("acc_made", (m + 1) * NE + START)
                g.tensor_scalar(acc[:], acc[:], -100.0, 100.0, ALU.max, ALU.min).then_inc(s["clip_made"], 1)
                wait("clip_made", m + 1)
                wait("ld_xres", 32 * m + 32)
                wait("x1_stored", 32 * m + START)
                g.tensor_tensor(x1_sb[:], x_res[:], acc[:], ALU.add).then_inc(s["x1_made"], 1)

            def next_block(n, k):
                wait("u_injected", n * BPC + k + 1)
                split_block((k + 1) * BS * GC, n * BPC + k + 1)

            def chunk_ends(n):
                wait("u_injected", n * BPC + BPC)
                take_projection(n + 1)
                split_block(0, n * BPC + BPC)

            def save(n, k):
                save_states(n * BPC + k, k * BS * GC)

            for k in range(4):
                next_block(0, k)
                if k == 3:
                    pool.wait_ge(s["mn_made"], 1)
                    g.tensor_tensor(mnorm[:], msum[:], mhalf[:], ALU.pow).then_inc(s["mnorm_made"], 1)
                save(0, k)
            with pool.Fori(4, BPC - 1) as k:
                next_block(0, k)
                save(0, k)
            chunk_ends(0)
            start_hT(0)
            save(0, BPC - 1)
            finish_hT(0)

            def gating_blocks(n, m, first):
                for k in range(3):
                    next_block(n, k)
                    if k == 0:
                        exponentials(m)
                    if k == 1 and not first:
                        finish_chunk(m - 1)
                    save(n, k)

            def rest_of_chunk(n, m):
                with pool.Fori(3, BPC - 1) as k:
                    next_block(n, k)
                    accumulate(m * NE + k - 3)
                    save(n, k)
                chunk_ends(n)
                accumulate(m * NE + NE - 2)
                start_hT(n)
                save(n, BPC - 1)
                finish_hT(n)

            gating_blocks(1, 0, True)
            rest_of_chunk(1, 0)
            with pool.Fori(2, NCH) as n:
                m = pool.snap(n - 1)
                gating_blocks(n, m, False)
                rest_of_chunk(n, m)
            m = NCH - 1
            exponentials(m)
            finish_chunk(m - 1)
            with pool.Fori(0, NE - 1) as e:
                accumulate(m * NE + e)
            finish_chunk(m)

            def gated(t, par):
                wait("av_made", 2 * t + 2)
                g.tensor_tensor(gs[par], gs[par], sg[par], ALU.mult).then_inc(s["gs_made"], 1)

            def scale_h(t, par):
                wait("h_inv_made", t + 1)
                g.tensor_scalar(hr[par], hh[par], h_inv[:, par:par + 1], ROUND, ALU.mult, ALU.add).then_inc(s["hr_made"], 1)

            def iteration(i, par=None):
                par, tile = (i % 2, lambda lag: 0 <= i - lag < NT) if par is None else (par, lambda lag: True)
                if tile(0):
                    gated(i, par)
                if tile(1):
                    scale_h(i - 1, 1 - par)

            for i in range(4):
                iteration(i)
            with pool.Fori(2, NT // 2) as k:
                for parity in range(2):
                    iteration(pool.snap(2 * k + parity), parity)
            for i in range(NT, NT + 3):
                iteration(i)

        @block.tensor
        def _(pe):
            mm = nc.tensor.matmul

            def products(gt, part, src, j, name=None, pieces=range(4)):
                for i in pieces:
                    m, k = i // KD, i % KD
                    c = j * GC + m * NB
                    last = mm(p_gate[gt][:, c:c + NB], uh[:, gt, part, k, m * P:(m + 1) * P],
                              src[:, k * NB:(k + 1) * NB], start=False, stop=True, skip_group_check=True)
                if name:
                    last.then_inc(s[name], 1)

            def inject(gt):
                for part in range(3):
                    last = mm(p_gate[gt][:, 0:BS * GC], ident_bf[:], xi[:, part, gt], start=(part == 0), stop=True,
                              skip_group_check=True)
                return last

            def four_steps(blk, after_z, after_u):
                v = [pe.snap(blk * BS + j) if not isinstance(blk, int) else blk * BS + j for j in range(BS + 1)]
                for j in range(BS):
                    pe.wait_ge(s["h_hi_s"], v[j] + 1)
                    products(R_, 0, h_hi, j)
                    products(R_, 1, h_hi, j)
                    products(Z_, 0, h_hi, j, pieces=(0, 1))
                    pe.wait_ge(s["h_lo_s"], v[j] + 1)
                    products(R_, 0, h_lo, j, "r_pre")
                    if j == 0:
                        inject(U_).then_inc(s["u_injected"], 1)
                    products(Z_, 0, h_hi, j, pieces=(2, 3))
                    products(Z_, 1, h_hi, j)
                    products(Z_, 0, h_lo, j, "z_pre")
                    after_z(j)
                    pe.wait_ge(s["rh_hi_s"], v[j + 1])
                    products(U_, 0, rh_hi, j)
                    products(U_, 1, rh_hi, j)
                    pe.wait_ge(s["rh_lo_s"], v[j + 1])
                    products(U_, 0, rh_lo, j, "u_pre")
                    if j == BS - 1:
                        pe.wait_ge(s["z_s"], v[j + 1])
                        pe.wait_ge(s["xi_ready"], blk + 2)
                        inject(R_)
                        inject(Z_)
                    after_u(j)

            def nothing(j):
                pass

            def up(e, cnt, pieces):
                for i in pieces:
                    c, k = i // KD, i % KD
                    if i == 0:
                        pe.wait_ge(s["pre0_made"], cnt + START)
                    if i == 4:
                        pe.wait_ge(s["pre1_made"], cnt + START)
                    last = mm(p_up[c // 2][:, c % 2 * P:(c % 2 + 1) * P], hT[:, k],
                              w1_sb[:, bass.ds(e, 1), k, c * P:(c + 1) * P].rearrange("p a f -> p (a f)")
                              if not isinstance(e, int) else w1_sb[:, e, k, c * P:(c + 1) * P],
                              start=(k == 0), stop=(k == KD - 1), skip_group_check=True)
                    if i == 3:
                        last.then_inc(s["up0_made"], 1)
                    if i == 7:
                        last.then_inc(s["up1_made"], 1)

            def turn(cnt, quarters):
                for c in quarters:
                    if c == 0:
                        pe.wait_ge(s["hid0_made"], cnt + 1 + START)
                        pe.wait_ge(s["hidT_made"], cnt + START)
                    if c == 2:
                        pe.wait_ge(s["hid1_made"], cnt + 1 + START)
                    last = nc.tensor.transpose(p_tr[:, c * P:(c + 1) * P], hid[:, c * P:(c + 1) * P], ident[:])
                    if c == 3:
                        last.then_inc(s["tr_made"], 1)

            def down(e, cnt, pieces):
                for i in pieces:
                    f, half = i // 2, i % 2
                    if i == 0:
                        pe.wait_ge(s["hidT_made"], cnt + 1 + START)
                        pe.wait_ge(s["weighted_made"], cnt + START)
                    last = mm(p_dn[:, half * P:(half + 1) * P], hidT[:, f * P:(f + 1) * P],
                              w2_sb[:, bass.ds(e, 1), f, half * P:(half + 1) * P].rearrange("p a f -> p (a f)")
                              if not isinstance(e, int) else w2_sb[:, e, f, half * P:(half + 1) * P],
                              start=(i == 0), stop=(f == KF - 1), skip_group_check=True)
                    if i == 7:
                        last.then_inc(s["dn_made"], 1)

            def turn_x(n):
                pe.wait_ge(s["ld_xnext"], 32 * (n + 1))
                if not (isinstance(n, int) and n < 2):
                    pe.wait_ge(s["base_taken"], n - 2 + START)
                elif n == 1:
                    pe.wait_ge(s["proj_taken"], 3)
                for k in range(KD):
                    last = nc.tensor.transpose(p_misc[:, k * P:(k + 1) * P], x_next[:, k * P:(k + 1) * P], ident[:])
                last.then_inc(s["xT_made"], 1)

            def project(n, pieces, n_experts=None):
                banks = (p_tr, p_dn, p_misc)
                for i in pieces:
                    gt, m, k = i // 4, i // 2 % 2, i % 2
                    if i == 0:
                        pe.wait_ge(s["xT_copied"], n + 1)
                        if n_experts is not None:
                            pe.wait_ge(s["weighted_made"], n_experts + START)
                    last = mm(banks[gt][:, m * P:(m + 1) * P], wx[:, gt, k, m * P:(m + 1) * P], xT[:, k],
                              start=(k == 0), stop=(k == KD - 1), skip_group_check=True)
                    if i % 4 == 3:
                        last.then_inc(s["proj_made"], 1)

            def logits(m):
                pe.wait_ge(s["hT_made"], m + 1)
                pe.wait_ge(s["pre0_made"], m * NE + START)
                for k in range(KD):
                    last = mm(p_up[0][0:NE, 0:P], gwT[:, k], hT[:, k], start=(k == 0), stop=(k == KD - 1))
                last.then_inc(s["logits_made"], 1)

            def turn_logits(m):
                nc.tensor.transpose(p_up[1][:, 0:NE], lgT[:, :], ident[0:NE, 0:NE]).then_inc(s["logits_turned"], 1)

            def keep_warm(bank, n, cols=512):
                for _ in range(n):
                    mm(bank[:, 0:cols], ident_bf[:], wgT[:, 0, 0:cols], start=True, stop=True, skip_group_check=True)

            def turn_gate(m):
                pe.wait_ge(s["gate_made"], m + 1)
                mm(p_dn[0:NE, 0:P], gate[:, :], ident[:], start=True, stop=True, is_transpose=True).then_inc(s["gateT_made"], 1)

            def base(m, parts):
                for i in parts:
                    if i < KD:
                        mm(p_misc[:, i * P:(i + 1) * P], hT[:, i], ident[:], start=(i == 0), stop=False,
                           skip_group_check=True)
                    else:
                        pe.wait_ge(s["gateT_copied"], m + 1)
                        mm(p_misc[:, 0:D], gateT[:, :], b2_sb[:, :], start=False, stop=True,
                           skip_group_check=True).then_inc(s["base_made"], 1)

            def keep_warm_first():
                for _ in range(8):
                    mm(p_gate[U_][:, 0:P], ident_bf[:], ident_bf[:], start=True, stop=True, skip_group_check=True)

            pe.wait_ge(s["const_made"], 3)
            turn_x(0)
            with pe.Fori(0, 12):
                keep_warm_first()
            pe.wait_ge(s["ld_small"], 16 * 10)
            pe.wait_ge(s["ld_c"], 16 * 3)
            for gt in range(3):
                for m in range(KD):
                    for k in range(KD):
                        last = mm(p_up[1][:, gt * GC + m * NB:gt * GC + (m + 1) * NB], raw[gt][:, k, m * P:(m + 1) * P],
                                  condT[:, k], start=(k == 0), stop=(k == KD - 1), skip_group_check=True)
                last.then_inc(s["condC_made"], 1)
            project(0, range(12))
            for k in range(KD):
                last = nc.tensor.transpose(p_up[0][:, k * 16:k * 16 + NE], gw_raw[:, k * P:(k + 1) * P], ident[0:NE, 0:NE])
            last.then_inc(s["p_prep"], 1)
            with pe.Fori(0, 10):
                keep_warm_first()
            pe.wait_ge(s["u_split"], 3)
            pe.wait_ge(s["xi_ready"], 1)
            inject(R_)
            inject(Z_)

            def project_next(q):
                if q == 0:
                    turn_x(1)
                elif q < 7:
                    project(1, range(2 * (q - 1), 2 * q))

            l1_banks = (p_up[0], p_up[1])

            def turn_weights(n):
                i, half = n // 2, n % 2
                pe.wait_ge(s["wq3"], 2 * (i + 1))
                if n > 1:
                    pe.wait_ge(s["wT_copied"], n - 1)
                dst = l1_banks[n % 2][:].bitcast(BF16)
                for o in range(8):
                    if i < 2:
                        src = l1_q[i].rearrange("p (o c) -> p o c", o=8)[:, o, half * P:(half + 1) * P]
                    else:
                        src = l1_q[i].rearrange("p (o c) -> p o c", o=KD)[:, o % KD, (half * 4 + o // KD) * P:(half * 4 + o // KD + 1) * P]
                    last = nc.tensor.transpose(dst[:, o * P:(o + 1) * P], src, ident_bf[:])
                last.then_inc(s["wT_made"], 1)

            def turn_mix(k):
                pe.wait_ge(s["mixn_made"], 4)
                pe.wait_ge(s["wT_copied"], 5 + k)
                for bb in range(NB):
                    for o in range(KD):
                        c = (bb * KD + o) * P
                        last = nc.tensor.transpose(l1_banks[k][:, c:c + P], mix_n4[:, bb, o, k * P:(k + 1) * P], ident[:])
                last.then_inc(s["mixT_made"], 1)

            def prepare_l1(q):
                if q == 3:
                    pe.wait_ge(s["gwT_made"], KD)
                    pe.wait_ge(s["e_prep"], 3)
                    pe.wait_ge(s["ones_made"], 2)
                    pe.wait_ge(s["abs_made"], 3)
                    mm(p_up[0][:, 0:3], ones[:], wsum[:, 0:3], start=True, stop=True).then_inc(s["wsum_made"], 1)
                elif q in (11, 12, 17, 18, 23, 24):
                    turn_weights((q - 11) // 6 * 2 + (q - 11) % 6)
                elif q in (25, 26):
                    turn_mix(q - 25)

            for blk in range(2):
                four_steps(blk, nothing, lambda j: project_next(4 * blk + j))
            for blk in range(2, 9):
                four_steps(blk, nothing, lambda j: prepare_l1(4 * (blk - 2) + j))
            with pe.Fori(9, BPC - 1) as k:
                four_steps(k, nothing, nothing)
            four_steps(BPC - 1, nothing, nothing)
            pe.wait_ge(s["ld_w1"], 16 * 4)
            pe.wait_ge(s["ld_w2"], 16 * 4)
            keep_warm(p_up[1], WARM_UP)

            def expert_slots(x0, c0, m, warm=True):
                def after_z(j):
                    if j == 0:
                        up(x0, c0, (0, 1))
                    elif j == 1:
                        up(x0, c0, (5,))
                        if warm:
                            pe.wait_ge(s["base_taken"], m + 1 + START)
                            keep_warm(p_misc, 1, 256)
                    elif j == 2:
                        down(x0 - 1, c0 - 1, (1,))
                        turn(c0, (0,))
                    else:
                        down(x0 - 1, c0 - 1, (5,))
                        turn(c0, (1,))

                def after_u(j):
                    if j == 0:
                        turn(c0 - 1, (3,))
                        up(x0, c0, (2, 3, 4))
                    elif j == 1:
                        up(x0, c0, (6, 7))
                        down(x0 - 1, c0 - 1, (0,))
                    elif j == 2:
                        down(x0 - 1, c0 - 1, (2, 3, 4))
                    else:
                        down(x0 - 1, c0 - 1, (6, 7))
                        turn(c0, (2,))
                return after_z, after_u

            def gating_slots(m, project_too):
                def after_z(j):
                    if j == 0:
                        pe.wait_ge(s["pre1_made"], m * NE + START)
                        if project_too:
                            keep_warm(p_up[1], 1)
                    elif j == 1:
                        pe.wait_ge(s["lgT_copied"], m + 1)
                        if project_too:
                            keep_warm(p_up[0], 1, 256)
                        turn_logits(m)
                        if project_too:
                            project(m + 2, (0,), m * NE)
                    elif project_too:
                        project(m + 2, (4 * (j - 1),))
                    if project_too and j != 1:
                        keep_warm(p_up[0] if j else p_up[1], 1, 256)

                def after_u(j):
                    if j == 0:
                        if project_too:
                            turn_x(m + 2)
                        logits(m)
                        if project_too:
                            keep_warm(p_up[1], 1, 256)
                    elif project_too:
                        project(m + 2, range(4 * j - 3, 4 * j))
                return after_z, after_u

            def base_waits(m):
                return 3 * (m + 3) if not (isinstance(m, int) and m == NCH - 1) else 3 * (NCH + 1)

            def first_slots(m, c0, warm=True):
                def after_z(j):
                    if j == 0:
                        up(0, c0, (0,))
                    elif j == 1:
                        pe.wait_ge(s["gchain"], m * NG + 1)
                        up(0, c0, (4,))
                    elif j == 2:
                        pe.wait_ge(s["proj_taken"], base_waits(m))
                        base(m, (0,))
                        turn(c0, (0,))
                    if warm:
                        if j == 0:
                            pe.wait_ge(s["proj_taken"], base_waits(m))
                        keep_warm(p_dn, (1, 3, 1, 2)[j], 256)
                    if j == 3:
                        turn_gate(m)
                        turn(c0, (1,))

                def after_u(j):
                    if j == 0:
                        up(0, c0, (1, 2, 3))
                    elif j == 1:
                        up(0, c0, (5, 6, 7))
                    if j < 2 and warm:
                        keep_warm(p_dn, 1, 256)
                    if j == 2:
                        base(m, (1,))
                        if warm:
                            keep_warm(p_dn, 2)
                    elif j == 3:
                        base(m, (2,))
                        turn(c0, (2,))
                return after_z, after_u

            def last_slots(cnt, warm=True):
                def after_z(j):
                    if j == 0:
                        turn(cnt, (3,))
                        pe.wait_ge(s["pre1_made"], cnt + 1 + START)
                        if warm:
                            keep_warm(p_up[1], 1)
                    elif j == 1:
                        down(NE - 1, cnt, (0,))
                    elif j == 2:
                        down(NE - 1, cnt, (4,))
                    elif warm:
                        keep_warm(p_up[1], 1)
                    if warm:
                        keep_warm(p_up[1], 1, 256)

                def after_u(j):
                    if j == 1:
                        down(NE - 1, cnt, (1, 2, 3))
                    elif j == 2:
                        down(NE - 1, cnt, (5, 6, 7))
                    elif warm:
                        keep_warm(p_up[1], 3)
                return after_z, after_u

            def alone(slots):
                for j in range(BS):
                    slots[0](j)
                    slots[1](j)

            with pe.Fori(1, NCH) as n:
                m = pe.snap(n - 1)
                four_steps(n * BPC, *gating_slots(m, True))
                four_steps(n * BPC + 1, *first_slots(m, m * NE))
                with pe.Fori(1, NE) as e:
                    four_steps(n * BPC + 1 + e, *expert_slots(e, pe.snap(m * NE + e), m))
                four_steps(n * BPC + BPC - 1, *last_slots(m * NE + NE - 1))

            m = NCH - 1
            pe.wait_ge(s["weighted_made"], m * NE + START)
            keep_warm(p_dn, WARM_UP)
            alone(gating_slots(m, False))
            alone(first_slots(m, m * NE, False))
            with pe.Fori(1, NE) as e:
                alone(expert_slots(e, pe.snap(m * NE + e), m, False))
            alone(last_slots(m * NE + NE - 1, False))

            keep_warm(p_tr, WARM_MIX)
            pe.wait_ge(s["ld_mix"], 16 * (NB * KD + NB))
            mix_banks = (p_up[0], p_up[1])

            def turn_q(n):
                pe.wait_ge(s["q_made"], n + 1)
                if n:
                    pe.wait_ge(s["qT_copied"], n)
                for i in range(4):
                    last = nc.tensor.transpose(p_gate[0][:].bitcast(BF16)[:, i * P:(i + 1) * P],
                                               q_all[:, n * 512 + i * P:n * 512 + (i + 1) * P], ident_bf[:])
                last.then_inc(s["qT_made"], 1)

            for n in range(NB * KD * 2):
                bb, o, half = n // 4, n // 2 % 2, n % 2
                if n > 1:
                    pe.wait_ge(s["mix_copied"], n - 1)
                for k in range(KD):
                    c = (bb * KD + k) * 1024 + half * 512
                    last = mm(mix_banks[n % 2][:], mixT[:, k, bb, o * P:(o + 1) * P], x1_mix[:, c:c + 512],
                              start=(k == 0), stop=(k == KD - 1))
                last.then_inc(s["mix_made"], 1)
                if n > 1:
                    turn_q(n - 2)
            turn_q(NB * KD * 2 - 2)
            turn_q(NB * KD * 2 - 1)

            def integer_product(t, banks, w, read, made):
                for half in range(2):
                    if not (isinstance(t, int) and t == 0):
                        pe.wait_ge(s[read], 2 * t - 1 + half)
                    for k in range(KD):
                        last = mm(banks[half][:], qT_all[:, bass.ds(t * D + k * P, P)],
                                  w[:, k, half * 512:(half + 1) * 512], start=(k == 0), stop=(k == KD - 1))
                    last.then_inc(s[made], 1)

            def turn_h(t, par):
                pe.wait_ge(s["hq_made"], t + 1)
                pe.wait_ge(s["hqT_copied"], t + START)
                for k in range(KI):
                    last = nc.tensor.transpose(p_gate[1][:].bitcast(BF16)[:, k * P:(k + 1) * P], hq[par][:, k * P:(k + 1) * P],
                                               ident_bf[:])
                last.then_inc(s["hqT_made"], 1)

            def down_l1(t):
                pe.wait_ge(s["hqT_copied"], t + 1 + START)
                pe.wait_ge(s["out_made"], t + START)
                for k in range(KI):
                    last = mm(p_gate[2][:, 0:D], hqT[:, k * P:(k + 1) * P], wdT[:, k], start=(k == 0), stop=(k == KI - 1))
                last.then_inc(s["down_mm"], 1)

            pe.wait_ge(s["mix_copied"], 2 * NB * KD)
            pe.wait_ge(s["qT_copied"], 2 * NB * KD)

            def iteration(i, par=None):
                par, tile = (i % 2, lambda lag: 0 <= i - lag < NT) if par is None else (par, lambda lag: True)
                if tile(3):
                    turn_h(i - 3, 1 - par)
                if tile(0):
                    integer_product(i, p_up, wgT, "av_made", "gate_mm")
                if tile(1):
                    integer_product(i - 1, (p_misc, p_tr), wuT, "hh_made", "up_mm")
                if tile(3):
                    down_l1(i - 3)

            for i in range(4):
                iteration(i)
            with pe.Fori(2, NT // 2) as k:
                for parity in range(2):
                    iteration(pe.snap(2 * k + parity), parity)
            for i in range(NT, NT + 3):
                iteration(i)

        @block.scalar
        def _(act):
            A = nc.scalar.activation

            def four_steps(blk, before_cand, after_cand):
                v = [act.snap(blk * BS + j + 1) if not isinstance(blk, int) else blk * BS + j + 1 for j in range(BS)]
                for j in range(BS):
                    cols = slice(j * GC, (j + 1) * GC)
                    act.wait_ge(s["r_pre"], v[j])
                    A(rg[:], p_gate[R_][:, cols], ACT.Tanh, scale=0.5 / PRE_SCALE).then_inc(s["r_s"], 1)
                    act.wait_ge(s["z_pre"], v[j])
                    A(zg[:], p_gate[Z_][:, cols], ACT.Tanh, scale=0.5 / PRE_SCALE).then_inc(s["z_s"], 1)
                    before_cand(j)
                    act.wait_ge(s["u_pre"], v[j])
                    A(cand_keep[:].rearrange("p (c two) -> p c two", two=2)[:, :, 0], p_gate[U_][:, cols], ACT.Tanh, scale=0.5 / PRE_SCALE).then_inc(s["cand_s"], 1)
                    after_cand(j)

            def nothing(j):
                pass

            def gelu_half(half, cnt):
                act.wait_ge(s[f"pre{half}_made"], cnt + 1 + START)
                act.wait_ge(s["tr_made"], cnt + START)
                c = slice(half * 256, half * 256 + 256)
                A(hid[:, c], pre[:, c], ACT.Gelu).then_inc(s[f"hid{half}_made"], 1)

            def copy_hidT(cnt):
                act.wait_ge(s["tr_made"], cnt + 1 + START)
                act.wait_ge(s["dn_made"], cnt + START)
                A(hidT[:], p_tr[:], ACT.Copy).then_inc(s["hidT_made"], 1)

            def copy_xT(n):
                act.wait_ge(s["xT_made"], n + 1)
                act.wait_ge(s["proj_made"], 3 * n)
                A(xT[:].rearrange("p k t -> p (k t)"), p_misc[:, 0:D], ACT.Copy).then_inc(s["xT_copied"], 1)

            def take_projection(n, gt):
                banks = (p_tr, p_dn, p_misc)
                act.wait_ge(s["proj_made"], 3 * n + gt + 1)
                if gt == 0 and not (isinstance(n, int) and n == 0):
                    act.wait_ge(s["xp_copied"], n)
                A(xp_next[:, gt].rearrange("p (t m b) -> p m b t", m=KD, b=NB),
                  banks[gt][:, 0:D].rearrange("p (m b t) -> p m b t", m=KD, b=NB), ACT.Copy,
                  scale=GATE_SCALE[gt]).then_inc(s["proj_taken"], 1)

            def weigh(e, cnt):
                act.wait_ge(s["acc_made"], cnt + START)
                act.sem_inc(s["act_waits"], 1)
                act.wait_ge(s["dn_made"], cnt + 1 + START)
                act.sem_inc(s["act_waits"], 1)
                w = gate[:, e:e + 1] if isinstance(e, int) else gate[:, bass.ds(e, 1)]
                A(weighted[:], p_dn[:, 0:D], ACT.Copy, scale=w).then_inc(s["weighted_made"], 1)

            def take_base(m):
                act.wait_ge(s["base_made"], m + 1 + START)
                act.wait_ge(s["x1_made"], m + START)
                A(acc[:], p_misc[:, 0:D], ACT.Copy).then_inc(s["base_taken"], 1)

            def copy_gateT(m):
                act.wait_ge(s["gateT_made"], m + 1)
                A(gateT[0:NE, :], p_dn[0:NE, 0:P], ACT.Copy).then_inc(s["gateT_copied"], 1)

            act.wait_ge(s["const_made"], 3)
            A(warm[:], desc[:], ACT.Gelu).then_inc(s["table_loaded"], 1)
            copy_xT(0)
            for gt in range(3):
                take_projection(0, gt)
            act.wait_ge(s["p_prep"], 1)
            for k in range(KD):
                A(gwT[:, k], p_up[0][:, k * 16:k * 16 + NE], ACT.Copy).then_inc(s["gwT_made"], 1)

            l1_banks = (p_up[0], p_up[1])

            def prepare_l1(q):
                if q < 3:
                    act.wait_ge(s["ld_l1"], 16 * 6)
                    A(l1_q[q], l1_raw[q], ACT.Abs, accum_out=wsum[:, q:q + 1]).then_inc(s["abs_made"], 1)
                elif q in (3, 4):
                    for n in (2 * (q - 3), 2 * (q - 3) + 1):
                        act.wait_ge(s["mw_made"], n + 1)
                        if n:
                            act.wait_ge(s["msq_made"], n)
                        A(sq_tmp, mix_w4[:, n // KD, n % KD], ACT.Square, accum_out=msum[:, n:n + 1]).then_inc(s["msq_made"], 1)
                elif q in (12, 13, 18, 19, 24, 25):
                    n = (q - 12) // 6 * 2 + (q - 12) % 6
                    i, half = n // 2, n % 2
                    dst = (wgT[:, half], wuT[:, half], wdT[:, half * 4:half * 4 + 4].rearrange("p k d -> p (k d)"))[i]
                    act.wait_ge(s["wT_made"], n + 1)
                    A(dst, l1_banks[n % 2][:].bitcast(BF16), ACT.Copy).then_inc(s["wT_copied"], 1)
                elif q in (26, 27):
                    k = q - 26
                    act.wait_ge(s["mixT_made"], k + 1)
                    A(mixT[:, k].rearrange("p b o -> p (b o)"), l1_banks[k][:], ACT.Copy).then_inc(s["mixT_copied"], 1)

            def take_next(q):
                if q == 0:
                    copy_xT(1)
                elif q in (3, 5, 7):
                    take_projection(1, (q - 3) // 2)

            for blk in range(2):
                four_steps(blk, nothing, lambda j: take_next(4 * blk + j))
            for blk in range(2, 9):
                four_steps(blk, nothing, lambda j: prepare_l1(4 * (blk - 2) + j))
            with act.Fori(9, BPC) as k:
                four_steps(k, nothing, nothing)

            def gating_slots(m, project_too):
                def after(j):
                    if project_too:
                        take_projection(m + 2, j - 1) if j else copy_xT(m + 2)
                return nothing, after

            def first_slots(m, c0):
                def after(j):
                    if j == 1:
                        gelu_half(0, c0)
                    elif j == 2:
                        gelu_half(1, c0)

                def before(j):
                    if j == 3:
                        copy_gateT(m)
                return before, after

            def expert_slots(first, c0):
                def after(j):
                    if j == 0:
                        first()
                        copy_hidT(c0 - 1)
                    elif j == 1:
                        gelu_half(0, c0)
                    elif j == 2:
                        gelu_half(1, c0)
                return nothing, after

            def last_slots(cnt):
                def after(j):
                    if j == 0:
                        weigh(NE - 2, cnt - 1)
                        copy_hidT(cnt)
                    elif j == 3:
                        weigh(NE - 1, cnt)
                return nothing, after

            def alone(slots):
                for j in range(BS):
                    slots[0](j)
                    slots[1](j)

            with act.Fori(1, NCH) as n:
                m = act.snap(n - 1)
                four_steps(n * BPC, *gating_slots(m, True))
                four_steps(n * BPC + 1, *first_slots(m, m * NE))
                four_steps(n * BPC + 2, *expert_slots(lambda: take_base(m), m * NE + 1))
                with act.Fori(2, NE) as e:
                    c0 = act.snap(m * NE + e)
                    four_steps(n * BPC + 1 + e, *expert_slots(lambda: weigh(e - 2, c0 - 2), c0))
                four_steps(n * BPC + BPC - 1, *last_slots(m * NE + NE - 1))
            m = NCH - 1
            alone(gating_slots(m, False))
            alone(first_slots(m, m * NE))
            alone(expert_slots(lambda: take_base(m), m * NE + 1))
            with act.Fori(2, NE) as e:
                c0 = act.snap(m * NE + e)
                alone(expert_slots(lambda: weigh(e - 2, c0 - 2), c0))
            alone(last_slots(m * NE + NE - 1))

            mix_banks = (p_up[0], p_up[1])

            def copy_qT(n):
                act.wait_ge(s["qT_made"], n + 1)
                A(qT_all[:, n * 512:(n + 1) * 512], p_gate[0][:].bitcast(BF16)[:, 0:512], ACT.Copy).then_inc(s["qT_copied"], 1)

            for n in range(NB * KD * 2):
                act.wait_ge(s["mix_made"], n + 1)
                A(mixed[:, n * 512:(n + 1) * 512], mix_banks[n % 2][:], ACT.Copy).then_inc(s["mix_copied"], 1)
                if n > 1:
                    copy_qT(n - 2)
            copy_qT(NB * KD * 2 - 2)
            copy_qT(NB * KD * 2 - 1)

            def gates(t, par):
                if not (isinstance(t, int) and t < 2):
                    act.wait_ge(s["gs_made"], t - 1)
                    act.sem_inc(s["act_waits"], 1)
                    act.wait_ge(s["hh_made"], 2 * t - 2)
                    act.sem_inc(s["act_waits"], 1)
                for half in range(2):
                    c = slice(half * 512, (half + 1) * 512)
                    act.wait_ge(s["gate_mm"], 2 * t + half + 1)
                    act.sem_inc(s["act_waits"], 1)
                    A(sg[par][:, c], p_up[half][:], ACT.Sigmoid, scale=g_step[:, bass.ds(t, 1)])
                    A(gs[par][:, c], p_up[half][:], ACT.Copy, scale=g_step[:, bass.ds(t, 1)]).then_inc(s["av_made"], 1)

            def copy_hqT(t):
                act.wait_ge(s["hqT_made"], t + 1 + START)
                act.wait_ge(s["down_mm"], t + START)
                A(hqT[:], p_gate[1][:].bitcast(BF16), ACT.Copy).then_inc(s["hqT_copied"], 1)

            act.wait_ge(s["steps_made"], 2)

            def iteration(i, par=None):
                par, tile = (i % 2, lambda lag: 0 <= i - lag < NT) if par is None else (par, lambda lag: True)
                if tile(3):
                    copy_hqT(i - 3)
                if tile(0):
                    gates(i, par)

            for i in range(4):
                iteration(i)
            with act.Fori(2, NT // 2) as k:
                for parity in range(2):
                    iteration(act.snap(2 * k + parity), parity)
            for i in range(NT, NT + 3):
                iteration(i)

        @block.vector
        def _(dve):
            V = nc.vector

            def four_steps(blk, after_keep, after_h):
                v = [dve.snap(blk * BS + j + 1) if not isinstance(blk, int) else blk * BS + j + 1 for j in range(BS)]
                for j in range(BS):
                    hp, hn = h32[:, (j - 1) % BS], h32[:, j]
                    dve.wait_ge(s["r_s"], v[j])
                    V.scalar_tensor_tensor(out=rh_hi[:], in0=rg[:], scalar=1.0, in1=hp,
                                           op0=ALU.add, op1=ALU.mult).then_inc(s["rh_hi_s"], 1)
                    V.scalar_tensor_tensor(out=rh32[:], in0=rg[:], scalar=1.0, in1=hp,
                                           op0=ALU.add, op1=ALU.mult).then_inc(s["rh32_s"], 1)
                    dve.wait_ge(s["rh32_s"], v[j])
                    V.tensor_tensor(rh_lo[:], rh32[:], rh_hi[:], ALU.subtract).then_inc(s["rh_lo_s"], 1)
                    dve.wait_ge(s["z_s"], v[j])
                    V.tensor_scalar(second(zero_z[:]), zg[:], H_SCALE / 2, H_SCALE / 2, ALU.mult, ALU.add)
                    V.tensor_scalar(not_z[:], zg[:], -0.5, 0.5, ALU.mult, ALU.add).then_inc(s["not_z_s"], 1)
                    dve.wait_ge(s["not_z_s"], v[j])
                    V.tensor_tensor(second(cand_keep[:]), not_z[:], hp, ALU.mult).then_inc(s["keep_s"], 1)
                    after_keep(j)
                    dve.wait_ge(s["cand_s"], v[j])
                    dve.wait_ge(s["keep_s"], v[j])
                    if j == 0:
                        dve.wait_ge(s["h_saved"], blk + START)
                    V.tensor_tensor_scan(h_hi_pairs[:], zero_z[:], cand_keep[:], 0.0, ALU.mult, ALU.add).then_inc(s["h_hi_s"], 1)
                    V.tensor_tensor_scan(h32_pairs[:, j], zero_z[:], cand_keep[:], 0.0, ALU.mult, ALU.add).then_inc(s["h32_s"], 1)
                    dve.wait_ge(s["h32_s"], v[j])
                    V.tensor_tensor(h_lo[:], hn, h_hi, ALU.subtract).then_inc(s["h_lo_s"], 1)
                    after_h(j)

            def nothing(j):
                pass

            def add_b1(half, e, cnt):
                dve.wait_ge(s[f"up{half}_made"], cnt + 1 + START)
                dve.wait_ge(s[f"hid{half}_made"], cnt + START)
                c = slice(half * 256, half * 256 + 256)
                bias = (b1_sb[:, e, c] if isinstance(e, int)
                        else b1_sb[:, bass.ds(e, 1), c].rearrange("p a f -> p (a f)"))
                V.tensor_tensor(pre[:, c], p_up[half][:, 0:256], bias, ALU.add).then_inc(s[f"pre{half}_made"], 1)

            def gating(m, part):
                gc = lambda k: m * NG + k
                q = s["gchain"]
                if part == -1:
                    dve.wait_ge(s["logits_made"], m + 1)
                    V.tensor_copy(lgT[:], p_up[0][0:NE, 0:P]).then_inc(s["lgT_copied"], 1)
                elif part == 0:
                    dve.wait_ge(s["logits_turned"], m + 1)
                    V.tensor_copy(lg[:], p_up[1][:, 0:NE]).then_inc(q, 1)
                    dve.wait_ge(q, gc(1))
                    V.reduce_max(st[:, 0:1], lg[:], AX).then_inc(q, 1)
                    dve.wait_ge(q, gc(2))
                    V.tensor_scalar(dl[:], lg[:], st[:, 0:1], None, ALU.subtract).then_inc(q, 1)
                elif part == 1:
                    dve.wait_ge(q, gc(4))
                    V.reduce_sum(st[:, 1:2], ex[:], AX).then_inc(q, 1)
                elif part == 2:
                    dve.wait_ge(q, gc(5))
                    V.reciprocal(st[:, 2:3], st[:, 1:2]).then_inc(q, 1)
                    dve.wait_ge(q, gc(6))
                    V.tensor_scalar(pr[:], ex[:], st[:, 2:3], None, ALU.mult).then_inc(q, 1)
                elif part == 3:
                    dve.wait_ge(q, gc(7))
                    V.reduce_max(st[:, 3:4], pr[:], AX).then_inc(q, 1)
                elif part == 4:
                    dve.wait_ge(q, gc(8))
                    V.scalar_tensor_tensor(out=cd[:], in0=pr[:], scalar=st[:, 3:4], in1=desc[:],
                                           op0=ALU.is_equal, op1=ALU.mult).then_inc(q, 1)
                    dve.wait_ge(q, gc(9))
                    V.reduce_max(st[:, 4:5], cd[:], AX).then_inc(q, 1)
                elif part == 5:
                    dve.wait_ge(q, gc(10))
                    V.tensor_scalar(sel1[:], desc[:], st[:, 4:5], None, ALU.is_equal).then_inc(q, 1)
                elif part == 6:
                    dve.wait_ge(q, gc(11))
                    V.scalar_tensor_tensor(out=pr2[:], in0=sel1[:], scalar=-2.0, in1=pr[:],
                                           op0=ALU.mult, op1=ALU.add).then_inc(q, 1)
                    dve.wait_ge(q, gc(12))
                    V.reduce_max(st[:, 5:6], pr2[:], AX).then_inc(q, 1)
                elif part == 7:
                    dve.wait_ge(q, gc(13))
                    V.tensor_scalar(st[:, 7:8], st[:, 3:4], st[:, 5:6], 1e-10, ALU.add, ALU.max).then_inc(s["gsum_made"], 1)
                    V.scalar_tensor_tensor(out=cd[:], in0=pr2[:], scalar=st[:, 5:6], in1=desc[:],
                                           op0=ALU.is_equal, op1=ALU.mult).then_inc(q, 1)
                elif part == 8:
                    dve.wait_ge(q, gc(14))
                    V.reduce_max(st[:, 6:7], cd[:], AX).then_inc(s["second_found"], 1)
                    dve.wait_ge(s["gsum_made"], m + 1)
                    V.reciprocal(st[:, 7:8], st[:, 7:8]).then_inc(s["ginv_made"], 1)
                    dve.wait_ge(s["second_found"], m + 1)
                    V.scalar_tensor_tensor(out=sel[:], in0=desc[:], scalar=st[:, 6:7], in1=sel1[:],
                                           op0=ALU.is_equal, op1=ALU.add).then_inc(s["sel_made"], 1)
                    dve.wait_ge(s["ginv_made"], m + 1)
                    dve.wait_ge(s["sel_made"], m + 1)
                    dve.wait_ge(s["weighted_made"], m * NE + START)
                    V.scalar_tensor_tensor(out=gate[:], in0=pr[:], scalar=st[:, 7:8], in1=sel[:],
                                           op0=ALU.mult, op1=ALU.mult).then_inc(s["gate_made"], 1)

            V.memset(zero_z[:], 0.0)
            V.memset(h32_pairs[:], 0.0).then_inc(s["e_prep"], 1)
            V.memset(euler[:], 2.718281828459045).then_inc(s["e_prep"], 1)
            V.memset(h_hi_pairs[:], 0.0).then_inc(s["h_hi_s"], 1)
            V.memset(h_lo[:], 0.0).then_inc(s["h_lo_s"], 1)
            for i in range(3):
                dve.wait_ge(s["ld_u"], 16 * 3)
                if i:
                    dve.wait_ge(s["u_split"], i)
                V.tensor_scalar(split32[:], raw[3 + i], W_SCALE, None, ALU.mult).then_inc(s["u_scaled"], 1)
                dve.wait_ge(s["u_scaled"], i + 1)
                V.tensor_copy(uh[:, i, 0], split32[:]).then_inc(s["u_hi_made"], 1)
                dve.wait_ge(s["u_hi_made"], i + 1)
                V.tensor_tensor(uh[:, i, 1], split32[:], uh[:, i, 0], ALU.subtract).then_inc(s["u_split"], 1)
            dve.wait_ge(s["condC_made"], 3)
            for gt in range(3):
                last = V.tensor_tensor(vbias[:, gt], p_up[1][:, gt * GC:(gt + 1) * GC].rearrange("p (m b) -> p m b", b=NB),
                                       bias_sb[:, gt].unsqueeze(2).broadcast_to([P, KD, NB]), ALU.add)
            last.then_inc(s["e_prep"], 1)
            dve.wait_ge(s["e_prep"], 3)
            for gt in range(3):
                V.tensor_scalar(vbias[:, gt], vbias[:, gt], GATE_SCALE[gt], None, ALU.mult).then_inc(s["vb_made"], 1)

            def prepare_l1(q):
                if q < 2:
                    dve.wait_ge(s["ld_l1"], 16 * 6)
                    for k in range(KD):
                        V.scalar_tensor_tensor(out=mix_w4[:, q, k], in0=mix_raw[:, k], scalar=D ** -0.5, in1=cond_bc[:, q],
                                               op0=ALU.mult, op1=ALU.mult).then_inc(s["mw_made"], 1)
                elif q == 4:
                    dve.wait_ge(s["wsum_made"], 1)
                    V.tensor_scalar(wsum[:, 0:3], p_up[0][:, 0:3], 1.0 / (INNER * D), 1e-5, ALU.mult, ALU.max).then_inc(s["wscale_made"], 1)
                    dve.wait_ge(s["wscale_made"], 1)
                    V.reciprocal(wscale[:, 0:3], wsum[:, 0:3]).then_inc(s["wscale_made"], 1)
                elif 5 <= q < 23:
                    i, stage, half = (q - 5) // 6, (q - 5) % 6 // 2, (q - 5) % 2
                    c = slice(half * NW // 2, (half + 1) * NW // 2)
                    w = l1_raw[i][:, c]
                    if stage == 0:
                        dve.wait_ge(s["wscale_made"], 2)
                        V.tensor_scalar(w, w, wscale[:, i:i + 1], ROUND, ALU.mult, ALU.add).then_inc(s["wq1"], 1)
                    elif stage == 1:
                        dve.wait_ge(s["wq1"], 2 * i + half + 1)
                        V.tensor_scalar(w, w, ROUND, 1.0, ALU.subtract, ALU.min).then_inc(s["wq2"], 1)
                    else:
                        dve.wait_ge(s["wq2"], 2 * i + half + 1)
                        V.tensor_scalar(l1_q[i][:, c], w, -1.0, None, ALU.max).then_inc(s["wq3"], 1)
                    if q == 5:
                        dve.wait_ge(s["msq_made"], NB * KD)
                        V.tensor_scalar(msum[:], msum[:], 1e-8, None, ALU.add).then_inc(s["mn_made"], 1)
                elif q in (23, 24):
                    bb = q - 23
                    dve.wait_ge(s["mnorm_made"], 1)
                    for k in range(KD):
                        V.tensor_scalar(mix_n4[:, bb, k], mix_w4[:, bb, k], mnorm[:, bb * KD + k:bb * KD + k + 1], None,
                                        ALU.mult).then_inc(s["mixn_made"], 1)

            for blk in range(2):
                four_steps(blk, nothing, nothing)
            for blk in range(2, 9):
                four_steps(blk, nothing, lambda j: prepare_l1(4 * (blk - 2) + j))
            with dve.Fori(9, BPC) as k:
                four_steps(k, nothing, nothing)
            dve.wait_ge(s["ld_b1"], 16)

            def gating_slots(m):
                def after_keep(j):
                    if j == 3:
                        gating(m, 1)

                def after_h(j):
                    if j != 2:
                        gating(m, {0: -1, 1: 0, 3: 2}[j])
                return after_keep, after_h

            def first_slots(m, c0):
                def after_keep(j):
                    if j < 3:
                        gating(m, 3 + 2 * j)

                def after_h(j):
                    if j < 2:
                        add_b1(j, 0, c0)
                    if j < 3:
                        gating(m, 4 + 2 * j)
                return after_keep, after_h

            def expert_slots(x0, c0):
                def after_h(j):
                    if j < 2:
                        add_b1(j, x0, c0)
                return nothing, after_h

            def alone(slots):
                for j in range(BS):
                    slots[0](j)
                    slots[1](j)

            with dve.Fori(1, NCH) as n:
                m = dve.snap(n - 1)
                four_steps(n * BPC, *gating_slots(m))
                four_steps(n * BPC + 1, *first_slots(m, m * NE))
                with dve.Fori(1, NE) as e:
                    four_steps(n * BPC + 1 + e, *expert_slots(e, dve.snap(m * NE + e)))
                four_steps(n * BPC + BPC - 1, nothing, nothing)
            m = NCH - 1
            alone(gating_slots(m))
            alone(first_slots(m, m * NE))
            with dve.Fori(1, NE) as e:
                alone(expert_slots(e, dve.snap(m * NE + e)))

            for n in range(NB * KD * 2):
                c = slice(n * 512, (n + 1) * 512)
                two = slice(2 * n, 2 * n + 2)
                dve.wait_ge(s["mix_copied"], n + 1)
                V.tensor_reduce(x_max[:, two], mixed[:, c].rearrange("p (t i) -> p t i", t=2), AX, ALU.max,
                                apply_absolute_value=True).then_inc(s["x_chain"], 1)
                dve.wait_ge(s["x_chain"], 3 * n + 1)
                V.tensor_scalar(x_step[:, two], x_max[:, two], 1e-5, 1.0 / 127.0, ALU.max, ALU.mult).then_inc(s["x_chain"], 1)
                dve.wait_ge(s["x_chain"], 3 * n + 2)
                V.reciprocal(x_inv[:, two], x_step[:, two]).then_inc(s["x_chain"], 1)
                dve.wait_ge(s["x_chain"], 3 * n + 3)
                if n:
                    dve.wait_ge(s["q_made"], n)
                for i in range(2):
                    V.tensor_scalar(xr[:, i * D:(i + 1) * D], mixed[:, n * 512 + i * D:n * 512 + (i + 1) * D],
                                    x_inv[:, 2 * n + i:2 * n + i + 1], ROUND, ALU.mult, ALU.add).then_inc(s["xr_made"], 1)
                dve.wait_ge(s["xr_made"], 2 * n + 2)
                V.tensor_scalar(q_all[:, c], xr, ROUND, 127.0, ALU.subtract, ALU.min).then_inc(s["q_made"], 1)
            for i, st_ in enumerate((g_step, u_step)):
                V.tensor_scalar(st_[:], x_step[:], wsum[:, i:i + 1], None, ALU.mult).then_inc(s["steps_made"], 1)
            dve.wait_ge(s["steps_made"], 2)

            def times_up(t, par):
                for half in range(2):
                    c = slice(half * 512, (half + 1) * 512)
                    if half == 0:
                        dve.wait_ge(s["gs_made"], t + 1)
                    dve.wait_ge(s["up_mm"], 2 * t + half + 1)
                    V.scalar_tensor_tensor(out=hh[par][:, c], in0=(p_misc, p_tr)[half][:], scalar=u_step[:, bass.ds(t, 1)],
                                           in1=gs[par][:, c], op0=ALU.mult, op1=ALU.mult).then_inc(s["hh_made"], 1)

            def round_h(t, par):
                dve.wait_ge(s["hr_made"], t + 1)
                if not (isinstance(t, int) and t < 2):
                    dve.wait_ge(s["hqT_made"], t - 1 + START)
                V.tensor_scalar(hq[par], hr[par], ROUND, 127.0, ALU.subtract, ALU.min).then_inc(s["hq_made"], 1)

            def h_scales(t, par):
                dve.wait_ge(s["hh_made"], 2 * t + 2)
                V.tensor_reduce(h_max[:], hh[par], AX, ALU.max, apply_absolute_value=True).then_inc(s["h_chain"], 1)
                dve.wait_ge(s["h_chain"], 3 * t + 1)
                V.tensor_scalar(h_step[:], h_max[:], 1e-5, 1.0 / 127.0, ALU.max, ALU.mult).then_inc(s["h_chain"], 1)
                dve.wait_ge(s["h_chain"], 3 * t + 2)
                V.reciprocal(h_inv[:, par:par + 1], h_step[:]).then_inc(s["h_inv_made"], 1)
                V.tensor_scalar(d_step[:, bass.ds(t, 1)], h_step[:], wsum[:, 2:3], None, ALU.mult).then_inc(s["h_chain"], 1)

            def finish(t):
                dve.wait_ge(s["h_chain"], 3 * t + 3)
                dve.wait_ge(s["down_mm"], t + 1 + START)
                V.scalar_tensor_tensor(out=out_sb[:, bass.ds(t * D, D)], in0=p_gate[2][:, 0:D], scalar=d_step[:, bass.ds(t, 1)],
                                       in1=x1_mix[:, bass.ds(t * D, D)], op0=ALU.mult, op1=ALU.add).then_inc(s["out_made"], 1)

            def iteration(i, par=None):
                par, tile = (i % 2, lambda lag: 0 <= i - lag < NT) if par is None else (par, lambda lag: True)
                if tile(1):
                    times_up(i - 1, 1 - par)
                if tile(2):
                    round_h(i - 2, par)
                if tile(1):
                    h_scales(i - 1, 1 - par)
                if tile(3):
                    finish(i - 3)

            for i in range(4):
                iteration(i)
            with dve.Fori(2, NT // 2) as k:
                for parity in range(2):
                    iteration(dve.snap(2 * k + parity), parity)
            for i in range(NT, NT + 3):
                iteration(i)


_INS = ["x", "cond_1024", "L0_cond_W_z", "L0_cond_U_z", "L0_cond_C_z", "L0_cond_b_z", "L0_cond_W_r", "L0_cond_U_r",
        "L0_cond_C_r", "L0_cond_b_r", "L0_cond_W", "L0_cond_U", "L0_cond_C", "L0_cond_b", "L0_ffn_gate_w",
        "L0_ffn_w1", "L0_ffn_b1", "L0_ffn_w2", "L0_ffn_b2", "L1_cond_weight", "L1_ffn_w_gate", "L1_ffn_w_up",
        "L1_ffn_w_down"]


def kernel(**inputs):
    import numpy as np
    import concourse.bacc as bacc
    from concourse.bass_utils import run_bass_kernel_spmd

    nc = bacc.Bacc("TRN2", target_bir_lowering=False, num_devices=1)
    arrays, args = {}, []
    for name in _INS:
        a = np.ascontiguousarray(inputs[name])
        arrays["in_" + name] = a
        args.append(nc.dram_tensor("in_" + name, a.shape, mybir.dt.from_np(a.dtype), kind="ExternalInput").ap())
    out = nc.dram_tensor("out", (NB, T, D), F32, kind="ExternalOutput").ap()
    build(nc, *args, out)
    return run_bass_kernel_spmd(nc, [arrays], core_ids=[0]).results[0]["out"]
```
